# Optimizing a Trainium2 kernel written in Bass

```python
import numpy as np
import jax
import jax.numpy as jnp

def _softmax(x, axis=-1):
    return jax.nn.softmax(x, axis=axis)

def _gelu(x):
    return jax.nn.gelu(x, approximate=True)

def _silu(x):
    return jax.nn.silu(x)

def _sigmoid(x):
    return jax.nn.sigmoid(x)

def _layernorm(x, axis=-1, eps=1e-05):
    m = jnp.mean(x, axis=axis, keepdims=True)
    v = jnp.var(x, axis=axis, keepdims=True)
    return (x - m) / jnp.sqrt(v + eps)

def _scatter_add(tgt, idx, src, axis=0):
    return tgt.at[idx].add(src)

def _segment_sum(src, seg, n):
    return jax.ops.segment_sum(src, seg, n)
kernel_name = 'mk_adaln_d2_jaxref_r8_059e0f'

def setup_inputs(seed: int=0):
    np.random.seed(seed)
    _w = jnp.asarray

    def _L0_attn_setup():
        import jax, jax.numpy as jnp
        import numpy as np
        import math
        D_MODEL = 128
        N_HEADS = 16
        EPS_GN = 1e-05

        def channel_group_norm(x, gamma, beta, num_groups, eps=EPS_GN):
            B, T, D = x.shape
            g = num_groups
            xt = x.transpose(0, 2, 1).reshape(B, g, D // g, T)
            mu = xt.mean(axis=(2, 3), keepdims=True)
            var = xt.var(axis=(2, 3), keepdims=True)
            xn = ((xt - mu) / jnp.sqrt(var + eps)).reshape(B, D, T)
            xn = xn * gamma[None, :, None] + beta[None, :, None]
            return xn.transpose(0, 2, 1)

        def l2_normalize(x, eps=1e-12):
            n = jnp.linalg.norm(x, axis=-1, keepdims=True)
            return x / jnp.maximum(n, eps)

        def decay_gammas(num_heads, dtype=jnp.float32):
            return 1.0 - jnp.exp(jnp.linspace(math.log(1.0 / 32.0), math.log(1.0 / 512.0), num_heads)).astype(dtype)
        key = jax.random.key(seed)
        ks = jax.random.split(key, 16)
        B, T, D = (4, 128, D_MODEL)
        s = 1.0 / math.sqrt(D)
        inp = {'x': jax.random.normal(ks[0], (B, T, D), jnp.float32), 'norm_g': jnp.ones((D,), jnp.float32), 'norm_b': jnp.zeros((D,), jnp.float32), 'qw': jax.random.normal(ks[1], (D, D), jnp.float32) * s, 'kw': jax.random.normal(ks[2], (D, D), jnp.float32) * s, 'vw': jax.random.normal(ks[3], (D, D), jnp.float32) * s, 'ow': jax.random.normal(ks[4], (D, D), jnp.float32) * s, 'ob': jnp.zeros((D,), jnp.float32), 'ffn_norm_g': jnp.ones((D,), jnp.float32), 'ffn_norm_b': jnp.zeros((D,), jnp.float32), 'w1': jax.random.normal(ks[5], (2 * D, D), jnp.float32) * s, 'b1': jnp.zeros((2 * D,), jnp.float32), 'w2': jax.random.normal(ks[6], (D, 2 * D), jnp.float32) * (1.0 / math.sqrt(2 * D)), 'b2': jnp.zeros((D,), jnp.float32)}
        return inp
    _L0_attn_in = _L0_attn_setup()

    def _L0_ffn_setup():
        import jax, jax.numpy as jnp
        import numpy as np
        EMBED_DIM = 128
        HIDDEN_DIM = 512
        NUM_EXPERTS = 8
        TOP_K = 2
        key = jax.random.key(seed)
        ks = jax.random.split(key, 4)
        std1 = float(np.sqrt(2.0 / EMBED_DIM))
        std2 = float(np.sqrt(2.0 / HIDDEN_DIM))
        x = jax.random.normal(ks[0], (1, 256, EMBED_DIM), dtype=jnp.float32)
        w_router = jax.random.normal(ks[1], (EMBED_DIM, NUM_EXPERTS), dtype=jnp.float32) * 0.02
        w1 = jax.random.normal(ks[2], (NUM_EXPERTS, EMBED_DIM, HIDDEN_DIM), dtype=jnp.float32) * std1
        b1 = jnp.zeros((NUM_EXPERTS, HIDDEN_DIM), dtype=jnp.float32)
        w2 = jax.random.normal(ks[3], (NUM_EXPERTS, HIDDEN_DIM, EMBED_DIM), dtype=jnp.float32) * std2
        b2 = jnp.zeros((NUM_EXPERTS, EMBED_DIM), dtype=jnp.float32)
        return {'x': x, 'w_router': w_router, 'w1': w1, 'b1': b1, 'w2': w2, 'b2': b2}
    _L0_ffn_in = _L0_ffn_setup()
    _L0_c = _w((lambda *s: np.random.randn(*s).astype(np.float32) * 0.05)(1, 128))
    _L0_wmod = _w((lambda *s: np.random.randn(*s).astype(np.float32) * 0.05)(128, 6 * 128) * 128 ** (-0.5))

    def _L1_attn_setup():
        import jax, jax.numpy as jnp
        import numpy as np
        from jax import lax
        D_MODEL = 128
        D_STATE = 16
        D_CONV = 4
        D_INNER = 256
        DT_RANK = 64
        BATCH = 2
        SEQ = 512
        DT_INIT_FLOOR = 0.0001

        def _silu(v):
            return v * jax.nn.sigmoid(v)

        def _ssm_scan(x_val, A, Bm, Cm, dt):

            def step(h, inp):
                dt_t, xv_t, B_t, C_t = inp
                dA = jnp.exp(dt_t[:, :, None] * A[None])
                h = dA * h + (dt_t * xv_t)[:, :, None] * B_t[:, None, :]
                y_t = jnp.einsum('bdn,bn->bd', h, C_t)
                return (h, y_t)
            batch, length, d_inner = x_val.shape
            h0 = jnp.zeros((batch, d_inner, A.shape[1]), dtype=x_val.dtype)
            xs = (jnp.swapaxes(dt, 0, 1), jnp.swapaxes(x_val, 0, 1), jnp.swapaxes(Bm, 0, 1), jnp.swapaxes(Cm, 0, 1))
            _, ys = lax.scan(step, h0, xs)
            return jnp.swapaxes(ys, 0, 1)
        key = jax.random.key(seed)
        ks = jax.random.split(key, 10)
        x = jax.random.normal(ks[0], (BATCH, SEQ, D_MODEL), dtype=jnp.float32)
        W_in = jax.random.normal(ks[1], (2 * D_INNER, D_MODEL), dtype=jnp.float32) * 0.02
        conv_w = jax.random.normal(ks[2], (D_INNER, 1, D_CONV), dtype=jnp.float32) * 0.1
        conv_b = jax.random.normal(ks[3], (D_INNER,), dtype=jnp.float32) * 0.01
        A_log = jnp.tile(jnp.log(jnp.arange(1, D_STATE + 1, dtype=jnp.float32))[None, :], (D_INNER, 1))
        dt_std = DT_RANK ** (-0.5)
        W_dt = jax.random.uniform(ks[4], (D_INNER, DT_RANK), minval=-dt_std, maxval=dt_std, dtype=jnp.float32)
        b_dt = jnp.full((D_INNER,), np.log(DT_INIT_FLOOR), dtype=jnp.float32)
        W_B = jax.random.normal(ks[5], (D_STATE, D_MODEL), dtype=jnp.float32) * 0.02
        W_C = jax.random.normal(ks[6], (D_STATE, D_MODEL), dtype=jnp.float32) * 0.02
        W_out = jax.random.normal(ks[7], (D_MODEL, D_INNER), dtype=jnp.float32) * 0.02
        return {'x': x, 'W_in': W_in, 'conv_w': conv_w, 'conv_b': conv_b, 'A_log': A_log, 'W_dt': W_dt, 'b_dt': b_dt, 'W_B': W_B, 'W_C': W_C, 'W_out': W_out}
    _L1_attn_in = _L1_attn_setup()

    def _L1_ffn_setup():
        import jax, jax.numpy as jnp
        import numpy as np
        B, N, D = (4, 256, 128)
        SPARSITY = 0.01
        key = jax.random.key(seed)
        k1, k2, k3 = jax.random.split(key, 3)
        x = jax.random.normal(k1, (B, N, D), dtype=jnp.float32)
        spatial = jax.random.normal(k2, (D, D), dtype=jnp.float32) * 0.02
        freq = jnp.fft.fft(spatial, axis=-1)
        k = int(D * SPARSITY)
        mag = jnp.abs(freq)
        kth = jax.lax.top_k(mag, k)[0][:, -1:]
        w_sparse = jnp.where(mag >= kth, freq, 0.0 + 0j)
        bias = jax.random.normal(k3, (D,), dtype=jnp.float32) * 0.01
        return {'x': x, 'w_freq_real': jnp.real(w_sparse).astype(jnp.float32), 'w_freq_imag': jnp.imag(w_sparse).astype(jnp.float32), 'bias': bias}
    _L1_ffn_in = _L1_ffn_setup()
    _L1_c = _w((lambda *s: np.random.randn(*s).astype(np.float32) * 0.05)(1, 128))
    _L1_wmod = _w((lambda *s: np.random.randn(*s).astype(np.float32) * 0.05)(128, 6 * 128) * 128 ** (-0.5))
    _d = {'L0_attn_x': _L0_attn_in['x'], 'L0_attn_norm_g': _L0_attn_in['norm_g'], 'L0_attn_norm_b': _L0_attn_in['norm_b'], 'L0_attn_qw': _L0_attn_in['qw'], 'L0_attn_kw': _L0_attn_in['kw'], 'L0_attn_vw': _L0_attn_in['vw'], 'L0_attn_ow': _L0_attn_in['ow'], 'L0_attn_ob': _L0_attn_in['ob'], 'L0_attn_ffn_norm_g': _L0_attn_in['ffn_norm_g'], 'L0_attn_ffn_norm_b': _L0_attn_in['ffn_norm_b'], 'L0_attn_w1': _L0_attn_in['w1'], 'L0_attn_b1': _L0_attn_in['b1'], 'L0_attn_w2': _L0_attn_in['w2'], 'L0_attn_b2': _L0_attn_in['b2'], 'L0_ffn_w_router': _L0_ffn_in['w_router'], 'L0_ffn_w1': _L0_ffn_in['w1'], 'L0_ffn_b1': _L0_ffn_in['b1'], 'L0_ffn_w2': _L0_ffn_in['w2'], 'L0_ffn_b2': _L0_ffn_in['b2'], 'L0_c': _L0_c, 'L0_wmod': _L0_wmod, 'L1_attn_W_in': _L1_attn_in['W_in'], 'L1_attn_conv_w': _L1_attn_in['conv_w'], 'L1_attn_conv_b': _L1_attn_in['conv_b'], 'L1_attn_A_log': _L1_attn_in['A_log'], 'L1_attn_W_dt': _L1_attn_in['W_dt'], 'L1_attn_b_dt': _L1_attn_in['b_dt'], 'L1_attn_W_B': _L1_attn_in['W_B'], 'L1_attn_W_C': _L1_attn_in['W_C'], 'L1_attn_W_out': _L1_attn_in['W_out'], 'L1_ffn_w_freq_real': _L1_ffn_in['w_freq_real'], 'L1_ffn_w_freq_imag': _L1_ffn_in['w_freq_imag'], 'L1_ffn_bias': _L1_ffn_in['bias'], 'L1_c': _L1_c, 'L1_wmod': _L1_wmod}
    _x0 = _d['L0_attn_x']
    _d['L0_attn_x'] = jax.random.normal(jax.random.fold_in(jax.random.key(seed), 1), (1, 2048, 128), dtype=_x0.dtype)
    del _x0
    return _d

def reference(L0_attn_x, L0_attn_norm_g, L0_attn_norm_b, L0_attn_qw, L0_attn_kw, L0_attn_vw, L0_attn_ow, L0_attn_ob, L0_attn_ffn_norm_g, L0_attn_ffn_norm_b, L0_attn_w1, L0_attn_b1, L0_attn_w2, L0_attn_b2, L0_ffn_w_router, L0_ffn_w1, L0_ffn_b1, L0_ffn_w2, L0_ffn_b2, L0_c, L0_wmod, L1_attn_W_in, L1_attn_conv_w, L1_attn_conv_b, L1_attn_A_log, L1_attn_W_dt, L1_attn_b_dt, L1_attn_W_B, L1_attn_W_C, L1_attn_W_out, L1_ffn_w_freq_real, L1_ffn_w_freq_imag, L1_ffn_bias, L1_c, L1_wmod):

    def _L0_attn_ref(x, norm_g, norm_b, qw, kw, vw, ow, ob, ffn_norm_g, ffn_norm_b, w1, b1, w2, b2):
        import jax, jax.numpy as jnp
        import numpy as np
        import math
        D_MODEL = 128
        N_HEADS = 16
        EPS_GN = 1e-05

        def channel_group_norm(x, gamma, beta, num_groups, eps=EPS_GN):
            B, T, D = x.shape
            g = num_groups
            xt = x.transpose(0, 2, 1).reshape(B, g, D // g, T)
            mu = xt.mean(axis=(2, 3), keepdims=True)
            var = xt.var(axis=(2, 3), keepdims=True)
            xn = ((xt - mu) / jnp.sqrt(var + eps)).reshape(B, D, T)
            xn = xn * gamma[None, :, None] + beta[None, :, None]
            return xn.transpose(0, 2, 1)

        def l2_normalize(x, eps=1e-12):
            n = jnp.linalg.norm(x, axis=-1, keepdims=True)
            return x / jnp.maximum(n, eps)

        def decay_gammas(num_heads, dtype=jnp.float32):
            return 1.0 - jnp.exp(jnp.linspace(math.log(1.0 / 32.0), math.log(1.0 / 512.0), num_heads)).astype(dtype)
        B, T, D = x.shape
        H = N_HEADS
        dh = D // H
        residual = x
        xn = channel_group_norm(x, norm_g, norm_b, H)
        q = l2_normalize(xn @ qw.T)
        k = l2_normalize(xn @ kw.T)
        v = xn @ vw.T

        def heads(t):
            return t.reshape(B, T, H, dh).transpose(0, 2, 1, 3)
        qh, kh, vh = (heads(q), heads(k), heads(v))
        gammas = decay_gammas(H)
        n = jnp.arange(T)[:, None]
        m = jnp.arange(T)[None, :]
        diff = n - m
        causal = diff >= 0
        exponent = jnp.where(causal, diff, 0).astype(jnp.float32)
        dmask = jnp.where(causal[None], gammas[:, None, None] ** exponent[None], 0.0)
        scale = 1.0 / math.sqrt(dh)
        sim = jnp.einsum('bhnd,bhmd->bhnm', qh, kh) * scale
        sim = sim * dmask[None]
        yh = jnp.einsum('bhnm,bhmd->bhnd', sim, vh)
        y = yh.transpose(0, 2, 1, 3).reshape(B, T, D)
        y = y @ ow.T + ob
        x = residual + y
        residual = x
        xn = channel_group_norm(x, ffn_norm_g, ffn_norm_b, H)
        h = jax.nn.silu(xn @ w1.T + b1)
        x = residual + (h @ w2.T + b2)
        return x

    def _L0_ffn_ref(x, w_router, w1, b1, w2, b2):
        import jax, jax.numpy as jnp
        import numpy as np
        EMBED_DIM = 128
        HIDDEN_DIM = 512
        NUM_EXPERTS = 8
        TOP_K = 2
        orig_shape = x.shape
        xf = x.reshape(-1, EMBED_DIM)
        logits = xf @ w_router
        probs = jax.nn.softmax(logits, axis=-1)
        topk_w, topk_idx = jax.lax.top_k(probs, TOP_K)
        mask = jax.nn.one_hot(topk_idx, NUM_EXPERTS, dtype=xf.dtype)
        weights = jnp.sum(topk_w[..., None] * mask, axis=1)
        h = jnp.einsum('te,ieh->tih', xf, w1) + b1
        h = jax.nn.gelu(h)
        out = jnp.einsum('tih,ihe->tie', h, w2) + b2
        out = jnp.sum(out * weights[..., None], axis=1)
        return out.reshape(orig_shape)

    def _L1_attn_ref(x, W_in, conv_w, conv_b, A_log, W_dt, b_dt, W_B, W_C, W_out):
        import jax, jax.numpy as jnp
        import numpy as np
        from jax import lax
        D_MODEL = 128
        D_STATE = 16
        D_CONV = 4
        D_INNER = 256
        DT_RANK = 64
        BATCH = 2
        SEQ = 512
        DT_INIT_FLOOR = 0.0001

        def _silu(v):
            return v * jax.nn.sigmoid(v)

        def _ssm_scan(x_val, A, Bm, Cm, dt):

            def step(h, inp):
                dt_t, xv_t, B_t, C_t = inp
                dA = jnp.exp(dt_t[:, :, None] * A[None])
                h = dA * h + (dt_t * xv_t)[:, :, None] * B_t[:, None, :]
                y_t = jnp.einsum('bdn,bn->bd', h, C_t)
                return (h, y_t)
            batch, length, d_inner = x_val.shape
            h0 = jnp.zeros((batch, d_inner, A.shape[1]), dtype=x_val.dtype)
            xs = (jnp.swapaxes(dt, 0, 1), jnp.swapaxes(x_val, 0, 1), jnp.swapaxes(Bm, 0, 1), jnp.swapaxes(Cm, 0, 1))
            _, ys = lax.scan(step, h0, xs)
            return jnp.swapaxes(ys, 0, 1)
        B, L, D = x.shape
        xz = x @ W_in.T
        x_val, z = jnp.split(xz, 2, axis=-1)
        xv = jnp.swapaxes(x_val, 1, 2)
        xv = lax.conv_general_dilated(xv, conv_w, window_strides=(1,), padding=[(D_CONV - 1, 0)], dimension_numbers=('NCH', 'OIH', 'NCH'), feature_group_count=conv_w.shape[0])
        xv = xv + conv_b[None, :, None]
        x_val = _silu(jnp.swapaxes(xv, 1, 2))
        A = -jnp.exp(A_log)
        dt_rank = W_dt.shape[1]
        dt = jax.nn.softplus(x[:, :, :dt_rank] @ W_dt.T + b_dt)
        Bm = x @ W_B.T
        Cm = x @ W_C.T
        y = _ssm_scan(x_val, A, Bm, Cm, dt)
        y = y * _silu(z)
        return y @ W_out.T

    def _L1_ffn_ref(x, w_freq_real, w_freq_imag, bias):
        import jax, jax.numpy as jnp
        import numpy as np
        B, N, D = (4, 256, 128)
        SPARSITY = 0.01
        w = jax.lax.complex(w_freq_real, w_freq_imag)
        x_freq = jnp.fft.fft(x, axis=-1)
        y_freq = jnp.einsum('bnd,do->bno', x_freq, w)
        y = jnp.real(jnp.fft.ifft(y_freq, axis=-1))
        return y + bias
    x = L0_attn_x
    mod = (_silu(L0_c) @ L0_wmod).reshape(L0_c.shape[0], 6, 1, -1)
    sa, ca, ga, sb, cb, gb = (mod[:, 0], mod[:, 1], mod[:, 2], mod[:, 3], mod[:, 4], mod[:, 5])
    ga = (2 * (ga >= 0) - 1) * jnp.maximum(jnp.abs(ga), 0.25)
    gb = (2 * (gb >= 0) - 1) * jnp.maximum(jnp.abs(gb), 0.25)
    h = _layernorm(x, axis=-1) * (1 + ca) + sa
    x = x + ga * _L0_attn_ref(h, L0_attn_norm_g, L0_attn_norm_b, L0_attn_qw, L0_attn_kw, L0_attn_vw, L0_attn_ow, L0_attn_ob, L0_attn_ffn_norm_g, L0_attn_ffn_norm_b, L0_attn_w1, L0_attn_b1, L0_attn_w2, L0_attn_b2)
    h = _layernorm(x, axis=-1) * (1 + cb) + sb
    x = x + gb * _L0_ffn_ref(h, L0_ffn_w_router, L0_ffn_w1, L0_ffn_b1, L0_ffn_w2, L0_ffn_b2)
    mod = (_silu(L1_c) @ L1_wmod).reshape(L1_c.shape[0], 6, 1, -1)
    sa, ca, ga, sb, cb, gb = (mod[:, 0], mod[:, 1], mod[:, 2], mod[:, 3], mod[:, 4], mod[:, 5])
    ga = (2 * (ga >= 0) - 1) * jnp.maximum(jnp.abs(ga), 0.25)
    gb = (2 * (gb >= 0) - 1) * jnp.maximum(jnp.abs(gb), 0.25)
    h = _layernorm(x, axis=-1) * (1 + ca) + sa
    x = x + ga * _L1_attn_ref(h, L1_attn_W_in, L1_attn_conv_w, L1_attn_conv_b, L1_attn_A_log, L1_attn_W_dt, L1_attn_b_dt, L1_attn_W_B, L1_attn_W_C, L1_attn_W_out)
    h = _layernorm(x, axis=-1) * (1 + cb) + sb
    x = x + gb * _L1_ffn_ref(h, L1_ffn_w_freq_real, L1_ffn_w_freq_imag, L1_ffn_bias)
    return x

_drawn_inputs = setup_inputs


def setup_inputs(seed=0):
    import zlib

    import numpy as np

    out = dict(_drawn_inputs(seed))
    spreads = {'L0_attn_norm_g': (1.0, 0.6),
     'L0_attn_norm_b': (0.0, 0.738),
     'L0_attn_ob': (0.0, 0.1),
     'L0_attn_ffn_norm_g': (1.0, 0.567),
     'L0_attn_ffn_norm_b': (0.0, 0.417),
     'L0_attn_b1': (0.0, 0.466),
     'L0_attn_b2': (0.0, 0.281),
     'L0_ffn_b1': (0.0, 0.8),
     'L0_ffn_b2': (0.0, 0.8),
     'L1_attn_b_dt': (-9.21034049987793, 0.6)}
    factors = {'L1_attn_W_in': 8.0,
     'L1_attn_conv_w': 8.0,
     'L1_attn_conv_b': 8.0,
     'L1_attn_A_log': 8.0,
     'L1_attn_W_dt': 8.0,
     'L1_attn_W_B': 8.0,
     'L1_attn_W_C': 8.0,
     'L1_attn_W_out': 8.0,
     'L1_ffn_bias': 200.0,
     'L1_ffn_w_freq_real': 8.0,
     'L1_ffn_w_freq_imag': 8.0}
    for name, (base, spread) in spreads.items():
        noise = np.random.default_rng([zlib.crc32(name.encode()), seed]).standard_normal(out[name].shape)
        drawn = base * np.exp(spread * noise) if base else spread * noise
        out[name] = jnp.asarray(drawn.astype(out[name].dtype))
    for name, factor in factors.items():
        out[name] = (out[name] * factor).astype(out[name].dtype)
    return out
```

```python
from contextlib import ExitStack

import numpy as np

import concourse.bass as bass
from concourse import mybir

ALU = mybir.AluOpType
ACT = mybir.ActivationFunctionType
AX = mybir.AxisListType
F32 = mybir.dt.float32
BF16 = mybir.dt.bfloat16

P = 128
T = 2048
D = 128
TC = 512
NC = T // TC
NJ = TC // P
HEADS = 16
DH = D // HEADS
E = 8
HID = 512
NK = HID // P
NS = 16
DI = 256
ND = DI // P
TAPS = 4
RANK = 64
EPS = 1e-5

COLS = ["norm_g", "norm_b", "ob", "ffn_g", "ffn_b", "b1_0", "b1_1", "b2", "conv_b0", "conv_b1",
        "b_dt0", "b_dt1", "c0", "c1", "gamma"] + [f"conv_w{d}{k}" for d in range(ND) for k in range(TAPS)]
COL = {n: i for i, n in enumerate(COLS)}


def build(nc, a, out):
    ctx = ExitStack()
    with ctx:
        def sb(name, shape, dt=F32):
            return ctx.enter_context(nc.sbuf_tensor(name, shape, dt))

        def ps(name):
            return ctx.enter_context(nc.psum_tensor(name, [P, TC], F32))

        def sem(name):
            return ctx.enter_context(nc.semaphore(name))

        cols = sb("cols", [P, len(COLS)])
        ident = sb("ident", [P, P])
        ones = sb("ones", [P, 8])
        group_avg = sb("group_avg", [P, P])
        dft = sb("dft", [P, 3, P])
        tie = sb("tie", [P, E, E])
        sel = sb("sel", [96, 2 * NS, P], BF16)
        part_row = sb("part_row", [96, 2 * NS])
        w_qkv = sb("w_qkv", [P, 3, P])
        w_kq_rep = sb("w_kq_rep", [P, 2, DH, P])
        w_o = sb("w_o", [P, P])
        w_f1 = sb("w_f1", [P, 2, P])
        w_f2 = sb("w_f2", [P, 2, P])
        w_router = sb("w_router", [P, E])
        w_e1 = sb("w_e1", [P, E, HID])
        w_e2 = sb("w_e2", [P, E * NK, P])
        b_e1 = sb("b_e1", [P, E * NK])
        b_e2 = sb("b_e2", [P, NJ, P])
        w_mod = sb("w_mod", [P, 6 * P])
        w_in = sb("w_in", [P, 4, P])
        w_dt = sb("w_dt", [P, ND, P])
        w_bc = sb("w_bc", [P, 96])
        w_out = sb("w_out", [P, ND, P])
        a_neg = sb("a_neg", [P, ND, NS])
        w_freq = sb("w_freq", [P, 2, P])
        g_freq = sb("g_freq", [P, 2, P])
        w_fft = sb("w_fft", [P, P])
        bias_row = sb("bias_row", [P, P])
        silu_c = sb("silu_c", [P, 2])
        silu_cb = sb("silu_cb", [P, 2, P])
        mods = sb("mods", [P, 8])
        gates = sb("gates", [P, 4, P])
        gate_t = sb("gate_t", [P, 2, P])
        diag_ga = sb("diag_ga", [P, P])
        eps4 = sb("mhalf", [P, 4])

        X = sb("X", [P, NC * NJ, D])
        hT = sb("hT", [P, NC, TC])
        ln_st = sb("ln_st", [P, NJ, 6])
        ln_mv = sb("ln_mv", [P, NJ, 2])
        ln_ve = sb("ln_ve", [P, NJ])
        ln_rs = sb("ln_rs", [P, NJ])
        ln_x = sb("ln_x", [P, NJ, D])
        gn_st = sb("gn_st", [P, NC, 6])
        gn_mv = sb("gn_mv", [P, 2])
        gn_me = sb("gn_me", [P, 2])
        gn_g = sb("gn_g", [P, 2])
        gn_ve = sb("gn_ve", [P, 1])
        gn_rs = sb("gn_rs", [P, 1])
        gn_sb = sb("gn_sb", [P, 2])
        xn = sb("xn", [P, 2, TC])
        vp = sb("vp", [P, TC])
        att_t = sb("att_t", [P, TC])
        nrm = sb("nrm", [P, 2 * NJ])
        rnm = sb("rnm", [P, 2 * NJ])
        x3T = sb("x3T", [P, 2, TC])
        h2T = sb("h2T", [P, 2, TC])
        h3T = sb("h3T", [P, TC])
        h4T = sb("h4T", [P, TC])
        gel = sb("gel", [P, 4, TC])
        lg = sb("lg", [P, NJ, E])
        ex = sb("ex", [P, NJ, E])
        pr = sb("pr", [P, NJ, E])
        s4 = sb("s4", [P, 3, NJ])
        cmp_ = sb("cmp", [P, 2, NJ * E, E])
        rank = sb("rank", [P, NJ, E])
        wts = sb("wts", [P, P])
        wT = sb("wT", [P, P])
        big8 = sb("big8", [P, 8, TC])
        big4a = sb("big4a", [P, 4, TC])
        big4b = sb("big4b", [P, 4, TC])
        big4c = sb("big4c", [P, 4, TC])
        S = big8
        q2 = big4a[:, 0:2, :]
        rb = big4a[:, 2:4, :]
        U = big4b[:, 0:2, :]
        ZA = big4b[:, 2:4, :]
        h1 = big4c
        dA = big8[:, 0:4, :]
        UB = big8[:, 4:6, :]
        Hs = big8[:, 6:8, :]
        Z = big4a
        ab = big4b[:, 0:2, :]
        exd = big4b[:, 2:4, :]
        lnd = big4c[:, 0:2, :]
        y2 = big4c[:, 2:4, :]
        xr = sb("xr", [P, ND, TC + TAPS - 1])
        cv = sb("cv", [P, ND, TC])
        gz = sb("gz", [P, ND, TC])
        xc = sb("xc", [P, ND, TC])
        dt = sb("dt", [P, ND, TC])
        u = sb("u", [P, ND, TC])
        r1 = sb("r1", [96, TC])
        P1 = sb("P1", [96, TC], BF16)
        ST = sb("ST", [96, TC], BF16)
        HL = sb("HL", [P, ND, NS])
        outb = sb("outb", [P, 2, NJ, D])
        XB = sb("XB", [P, NJ, D])

        pT, pO, pH0, pH1, pY0, pY1, pB, pC = (ps(n) for n in ("pT", "pO", "pH0", "pH1", "pY0", "pY1", "pB", "pC"))
        pH = [pH0, pH1]
        pY = [pY0, pY1]

        def j4(ap):
            return ap.rearrange("p (j d) -> p j d", j=NJ)

        def col(n):
            return cols[:, COL[n]:COL[n] + 1]

        names = """ld_small ld_attn ld_ffn ld_moe ld_mam
            silu_c_ready mod_mm set_cb set_dve set_pool fr_mm fr_sb fft_mm exp_A
            ln_stats ln_rstd ln_xn ln_tr ln_evac
            gn_m gn_mm gn_v gn_r gn_ready xn_ready
            att_qkv att_sq att_ss att_nr att_r att_rb att_rbs att_kb att_qb att_u att_z att_ow att_x2
            ffn_h ffn_silu ffn_o ffn_x3 ffn_tok ffn_x1
            moe_rt moe_lg moe_ex moe_w moe_wt moe_wts moe_bias moe_xb moe_h moe_g moe_g2 moe_acc
            mam_hist mam_xz mam_xr mam_gz mam_dtp mam_bc mam_cv mam_xc mam_ab mam_r0 mam_ex mam_ln mam_dt mam_u
            mam_st0 mam_r1 mam_st mam_bB mam_bC mam_ub mam_dA mam_sc mam_z mam_y mam_y2 mam_o mam_x
            fft_o fft_x vec_chain act_chain pool_chain out_done0 out_done1""".split()
        s = {n: sem(n) for n in names}
        ld_x = [sem(f"ld_x{c}") for c in range(NC)]
        NSM, NAT, NFF, NMO, NMA = 6, 3, 2, 5, 9

        block = ctx.enter_context(nc.Block())


        @block.sync
        def _(sp):
            sp.dma_start(cols[:, :], a["cols"]).then_inc(s["ld_small"], 16)
            xv = a["x"].rearrange("(c j p) d -> c p j d", c=NC, j=NJ)
            for c in range(NC):
                sp.dma_start(X[:, c * NJ:(c + 1) * NJ, :], xv[c]).then_inc(ld_x[c], 16)
                if c == 0:
                    sp.dma_start(ident[:, :], a["ident"]).then_inc(s["ld_small"], 16)
            sp.dma_start(w_kq_rep[:, :, :, :], a["w_kq_rep"]).then_inc(s["ld_attn"], 16)
            sp.dma_start(w_qkv[:, :, :], a["w_qkv"]).then_inc(s["ld_attn"], 16)
            sp.dma_start(w_o[:, :], a["w_o"]).then_inc(s["ld_attn"], 16)
            sp.dma_start(w_f1[:, :, :], a["w_f1"]).then_inc(s["ld_ffn"], 16)
            sp.dma_start(w_f2[:, :, :], a["w_f2"]).then_inc(s["ld_ffn"], 16)
            sp.dma_start(w_router[:, :], a["w_router"]).then_inc(s["ld_moe"], 16)
            sp.dma_start(w_e1[:, :, :], a["w_e1"]).then_inc(s["ld_moe"], 16)
            sp.dma_start(w_e2[:, :, :], a["w_e2"]).then_inc(s["ld_moe"], 16)
            sp.dma_start(b_e1[:, :], a["b_e1"]).then_inc(s["ld_moe"], 16)
            sp.dma_start(b_e2[:, :, :], a["b_e2"]).then_inc(s["ld_moe"], 16)
            for n, t in (("w_in", w_in), ("w_dt", w_dt), ("w_bc", w_bc), ("w_out", w_out), ("a_log", a_neg),
                         ("w_freq", w_freq), ("part_row", part_row), ("tie", tie), ("dft", dft)):
                sp.dma_start(t[:], a[n]).then_inc(s["ld_mam"], 16)
            ov = out.rearrange("(c j p) d -> c p j d", c=NC, j=NJ)
            for c in range(NC):
                sp.wait_ge(s["fft_x"], c + 1)
                sp.dma_start(ov[c], outb[:, c % 2, :, :]).then_inc(s[f"out_done{c % 2}"], 16)
            for p_ in range(2):
                sp.wait_ge(s[f"out_done{p_}"], 16 * (NC // 2))

        @block.gpsimd
        def _(pool):
            chain = [0]

            def link(ins):
                ins.then_inc(s["pool_chain"], 1)
                chain[0] += 1
                pool.wait_ge(s["pool_chain"], chain[0])

            L = [0]

            def ln():
                pool.wait_ge(s["ln_stats"], L[0] + 1)
                link(pool.tensor_scalar(ln_ve[:, :], ln_mv[:, :, 1], EPS, None, ALU.add))
                pool.tensor_tensor(ln_rs[:, :], ln_ve[:, :], eps4[:, :], ALU.pow).then_inc(s["ln_rstd"], 1)
                L[0] += 1

            def gn(g):
                pool.wait_ge(s["gn_v"], g + 1)
                pool.tensor_tensor(gn_rs[:, :], gn_ve[:, :], eps4[:, 0:1], ALU.pow).then_inc(s["gn_r"], 1)

            link(pool.memset(eps4[:, :], -0.5))
            pool.memset(ones[:, :], 1.0).then_inc(s["set_pool"], 1)
            for c in range(NC):
                ln()
            pool.wait_ge(s["ld_moe"], 16 * NMO)
            pool.wait_ge(s["set_dve"], 1)
            gb = gates[:, 1:2, :]
            pool.tensor_tensor(w_e2[:, :, :], w_e2[:, :, :], gb.to_broadcast([P, E * NK, P]), ALU.mult).then_inc(s["set_pool"], 1)
            pool.tensor_tensor(b_e2[:, :, :], b_e2[:, :, :], gb.to_broadcast([P, NJ, P]), ALU.mult).then_inc(s["set_pool"], 1)
            pool.wait_ge(s["ld_mam"], 16 * NMA)
            pool.tensor_tensor(w_out[:, :, :], w_out[:, :, :], gates[:, 2:3, :].to_broadcast([P, ND, P]), ALU.mult).then_inc(s["set_pool"], 1)
            pool.tensor_copy(sel[:, :, :], part_row[:, :, None].to_broadcast([96, 2 * NS, P])).then_inc(s["set_pool"], 1)
            gn(0)
            gn(1)
            ln()
            for c in range(NC):
                ln()
                if c + 1 < NC:
                    ln()
                ln()

        @block.vector
        def _(vec):
            chain = [0]
            L = [0]

            def link(ins):
                ins.then_inc(s["vec_chain"], 1)
                chain[0] += 1
                vec.wait_ge(s["vec_chain"], chain[0])

            def sig(ins, name, count):
                ins.then_inc(s[name], 1)
                vec.wait_ge(s[name], count)

            def ln(c):
                Xc = X[:, c * NJ:(c + 1) * NJ, :]
                for j in range(NJ):
                    ins = vec.bn_stats(ln_st[:, j, :], Xc[:, j, :])
                    if j == NJ - 1:
                        link(ins)
                for j in range(NJ):
                    ins = vec.bn_aggr(ln_mv[:, j, :], ln_st[:, j, :])
                ins.then_inc(s["ln_stats"], 1)
                vec.wait_ge(s["ln_rstd"], L[0] + 1)
                if L[0]:
                    vec.wait_ge(s["ln_tr"], L[0])
                for j in range(NJ):
                    vec.tensor_scalar(ln_x[:, j, :], Xc[:, j, :], ln_mv[:, j, 0:1], ln_rs[:, j:j + 1],
                                      ALU.subtract, ALU.mult).then_inc(s["ln_xn"], 1)
                L[0] += 1

            def gn(g, gamma, beta):
                link(vec.bn_aggr(gn_mv[:, :], gn_st[:, :, :].rearrange("p c k -> p (c k)")))
                vec.tensor_copy(gn_me[:, 0:1], gn_mv[:, 0:1])
                vec.scalar_tensor_tensor(gn_me[:, 1:2], gn_mv[:, 0:1], gn_mv[:, 0:1], gn_mv[:, 1:2],
                                         ALU.mult, ALU.add).then_inc(s["gn_m"], 1)
                vec.wait_ge(s["gn_mm"], g + 1)
                link(vec.tensor_copy(gn_g[:, :], pO[:, 0:2]))
                link(vec.scalar_tensor_tensor(gn_ve[:, :], gn_g[:, 0:1], gn_g[:, 0:1], gn_g[:, 1:2],
                                              ALU.mult, ALU.subtract))
                vec.tensor_scalar(gn_ve[:, :], gn_ve[:, :], -1.0, EPS, ALU.mult, ALU.add).then_inc(s["gn_v"], 1)
                vec.wait_ge(s["gn_r"], g + 1)
                link(vec.tensor_tensor(gn_sb[:, 0:1], gn_rs[:, :], col(gamma), ALU.mult))
                link(vec.scalar_tensor_tensor(gn_sb[:, 1:2], gn_g[:, 0:1], gn_sb[:, 0:1], col(beta),
                                              ALU.mult, ALU.subtract))
                vec.tensor_scalar(gn_sb[:, 1:2], gn_sb[:, 1:2], -1.0, None, ALU.mult).then_inc(s["gn_ready"], 1)

            vec.wait_ge(s["silu_c_ready"], 1)
            vec.tensor_copy(silu_cb[:, 0, :], silu_c[:, 0:1].to_broadcast([P, P])).then_inc(s["set_cb"], 1)
            vec.tensor_copy(silu_cb[:, 1, :], silu_c[:, 1:2].to_broadcast([P, P])).then_inc(s["set_cb"], 1)
            vec.memset(wts[:, :], 0.0)
            vec.memset(xr[:, :, 0:TAPS - 1], 0.0).then_inc(s["mam_hist"], 1)
            for l in range(2):
                vec.wait_ge(s["mod_mm"], 2 * l + 2)
                vec.tensor_copy(mods[:, 4 * l:4 * l + 4], pT[:, 0:4])
                link(vec.tensor_copy(gates[:, 2 * l:2 * l + 2, :], pO[:, 0:256].rearrange("p (g d) -> p g d", g=2)))
                g = gates[:, 2 * l:2 * l + 2, :]
                link(vec.tensor_scalar(gate_t[:, :, :], g, 0.0, 2.0, ALU.is_ge, ALU.mult))
                link(vec.scalar_tensor_tensor(g, g, -1.0, g, ALU.mult, ALU.max))
                link(vec.tensor_scalar(g, g, 0.25, None, ALU.max))
                link(vec.scalar_tensor_tensor(g, gate_t[:, :, :], -1.0, g, ALU.add, ALU.mult))
                mc = mods[:, 4 * l:4 * l + 4].rearrange("p (a b) -> p a b", b=2)[:, :, 1]
                ins = vec.tensor_scalar(mc, mc, 1.0, None, ALU.add)
                if l == 0:
                    link(ins)
                    vec.wait_ge(s["ld_small"], 16 * NSM)
                    vec.tensor_tensor(diag_ga[:, :], ident[:, :], gates[:, 0, :], ALU.mult).then_inc(s["set_dve"], 1)
                else:
                    link(ins)
                    vec.tensor_tensor(bias_row[:, :], bias_row[:, :], gates[:, 3, :], ALU.mult).then_inc(s["set_dve"], 1)

            for c in range(NC):
                vec.wait_ge(ld_x[c], 16)
                ln(c)
                if c:
                    vec.wait_ge(s["ln_evac"], c)
                    vec.bn_stats(gn_st[:, c - 1, :], hT[:, c - 1, :])
            vec.wait_ge(s["ln_evac"], NC)
            link(vec.bn_stats(gn_st[:, NC - 1, :], hT[:, NC - 1, :]))
            gn(0, "norm_g", "norm_b")

            for c in range(NC):
                vec.wait_ge(s["att_nr"], c + 1)
                link(vec.tensor_scalar(nrm[:, :], nrm[:, :], 1e-12, None, ALU.max))
                link(vec.reciprocal(rnm[:, :], nrm[:, :]))
                vec.tensor_scalar(rnm[:, 0:NJ], rnm[:, 0:NJ], float(1.0 / np.sqrt(DH)), None, ALU.mult).then_inc(s["att_r"], 1)
                vec.wait_ge(s["att_qkv"], 3 * c + 3)
                vec.wait_ge(s["att_rbs"], 2 * c + 2)
                link(vec.tensor_tensor(vp[:, :], pB[:, :], rb[:, 1, :], ALU.mult))
                for i in range(DH):
                    n = DH * c + i
                    vec.wait_ge(s["att_kb"], n + 1)
                    sig(vec.tensor_tensor(U[:, i % 2, :], pH[i % 2][:, :], vp[:, :], ALU.mult), "att_u", n + 1)
                    link(vec.tensor_tensor_scan(S[:, i, :], col("gamma").to_broadcast([P, TC]), U[:, i % 2, :],
                                                S[:, i, TC - 1:TC] if c else 0.0, ALU.mult, ALU.add))
                    vec.wait_ge(s["att_qb"], n + 1)
                    if n >= 2:
                        vec.wait_ge(s["att_ow"], n - 1)
                    vec.tensor_tensor(ZA[:, i % 2, :], [pC, pT][i % 2][:, :], S[:, i, :], ALU.mult).then_inc(s["att_z"], 1)
                vec.wait_ge(s["att_ow"], DH * (c + 1))
                link(vec.tensor_tensor(att_t[:, :], pO[:, :], rb[:, 0, :], ALU.mult))
                sig(vec.scalar_tensor_tensor(hT[:, c, :], att_t[:, :], col("ob"), hT[:, c, :], ALU.add, ALU.add),
                    "att_x2", c + 1)
                link(vec.bn_stats(gn_st[:, c, :], hT[:, c, :]))
            gn(1, "ffn_g", "ffn_b")

            def ffn_x1(c):
                vec.wait_ge(s["ffn_tok"], c + 1)
                Xc = X[:, c * NJ:(c + 1) * NJ, :]
                sig(vec.tensor_tensor(Xc, Xc, j4([pB, pC][c % 2][:, :]), ALU.add), "ffn_x1", c + 1)

            for c in range(NC):
                vec.wait_ge(s["ffn_o"], c + 1)
                if c >= 2:
                    vec.wait_ge(s["ffn_tok"], c - 1)
                vec.scalar_tensor_tensor(x3T[:, c % 2, :], pY[c % 2][:, :], col("b2"), hT[:, c, :], ALU.add,
                                         ALU.add).then_inc(s["ffn_x3"], 1)
                if c:
                    ffn_x1(c - 1)
            ffn_x1(NC - 1)

            def moe_prep(c):
                ln(c)
                vec.wait_ge(s["moe_rt"], c + 1)
                logits = pO[:, 0:NJ * E].rearrange("p (j e) -> p j e", j=NJ)
                mx, sm, rs = (s4[:, k, :] for k in range(3))

                def over(v):
                    return v[:, :, None].to_broadcast([P, NJ, E])
                link(vec.tensor_reduce(mx, logits, AX.X, ALU.max))
                vec.tensor_tensor(lg[:, :, :], logits, over(mx), ALU.subtract).then_inc(s["moe_lg"], 1)
                vec.wait_ge(s["moe_ex"], c + 1)
                link(vec.tensor_reduce(sm, ex[:, :, :], AX.X, ALU.add))
                link(vec.reciprocal(rs, sm))
                link(vec.tensor_tensor(pr[:, :, :], ex[:, :, :], over(rs), ALU.mult))
                flat = pr[:, :, :].rearrange("p j e -> p (j e)")
                mine = flat[:, :, None].to_broadcast([P, NJ * E, E])
                for j in range(NJ):
                    rows = slice(j * E, (j + 1) * E)
                    others = pr[:, j:j + 1, :].to_broadcast([P, E, E])
                    vec.tensor_tensor(cmp_[:, 0, rows, :], others, mine[:, rows, :], ALU.is_gt)
                    link(vec.tensor_tensor(cmp_[:, 1, rows, :], others, mine[:, rows, :], ALU.is_equal))
                    link(vec.tensor_tensor(cmp_[:, 1, rows, :], cmp_[:, 1, rows, :], tie[:, :, :], ALU.mult))
                link(vec.tensor_tensor(cmp_[:, 0, :, :], cmp_[:, 0, :, :], cmp_[:, 1, :, :], ALU.add))
                link(vec.tensor_reduce(rank[:, :, :].rearrange("p j e -> p (j e)"), cmp_[:, 0, :, :], AX.X, ALU.add))
                sig(vec.scalar_tensor_tensor(wts[:, 0:NJ * E], rank[:, :, :].rearrange("p j e -> p (j e)"), 2.0, flat,
                                             ALU.is_lt, ALU.mult), "moe_w", c + 1)
                vec.wait_ge(s["moe_bias"], c + 1)
                Xc = X[:, c * NJ:(c + 1) * NJ, :]
                sig(vec.tensor_tensor(Xc, Xc, j4(pO[:, :]), ALU.add), "moe_xb", c + 1)

            def moe_acc(c, e):
                n = E * c + e
                vec.wait_ge(s["moe_g2"], NK * (n + 1))
                for j in range(NJ):
                    Xj = X[:, c * NJ + j, :]
                    ins = vec.scalar_tensor_tensor(Xj, pO[:, j * P:(j + 1) * P], wts[:, j * E + e:j * E + e + 1], Xj,
                                                   ALU.mult, ALU.add)
                sig(ins, "moe_acc", n + 1)

            def mam_prep(c):
                ln(c)
                vec.wait_ge(s["mam_xr"], 2 * c + 2)
                for d in range(ND):
                    def w(k):
                        return col(f"conv_w{d}{k}")
                    link(vec.tensor_scalar(cv[:, d, :], xr[:, d, 0:TC], w(0), col(f"conv_b{d}"), ALU.mult, ALU.add))
                    for k in range(1, TAPS):
                        ins = vec.scalar_tensor_tensor(cv[:, d, :], xr[:, d, k:k + TC], w(k), cv[:, d, :], ALU.mult, ALU.add)
                        if k < TAPS - 1:
                            link(ins)
                    sig(ins, "mam_cv", 2 * c + d + 1)
                if c + 1 < NC:
                    vec.tensor_copy(xr[:, :, 0:TAPS - 1], xr[:, :, TC:TC + TAPS - 1]).then_inc(s["mam_hist"], 1)
                vec.wait_ge(s["mam_st0"], c + 1)
                sig(vec.tensor_tensor(r1[:, :], pB[0:96, :], ST[:, :], ALU.subtract), "mam_r1", c + 1)
                vec.tensor_copy(P1[:, :], r1[:, :])
                link(vec.tensor_copy(ST[32:64, :], r1[32:64, :]))
                vec.tensor_tensor(ST[64:96, :], r1[64:96, :], P1[64:96, :], ALU.subtract).then_inc(s["mam_st"], 1)
                for d in range(ND):
                    vec.wait_ge(s["mam_dtp"], 2 * c + d + 1)
                    if d == 0:
                        vec.wait_ge(s["mam_ab"], 2 * c + 2)
                    link(vec.tensor_scalar(dt[:, d, :], pY[d][:, :], col(f"b_dt{d}"), 0.0, ALU.add, ALU.max))
                vec.wait_ge(s["mam_ln"], c + 1)
                link(vec.tensor_scalar(cv[:, :, :], exd, 1.0, -1.0, ALU.add, ALU.add))
                link(vec.tensor_tensor(cv[:, :, :], exd, cv[:, :, :], ALU.subtract))
                link(vec.tensor_tensor(cv[:, :, :], cv[:, :, :], lnd, ALU.add))
                sig(vec.tensor_tensor(dt[:, :, :], dt[:, :, :], cv[:, :, :], ALU.add), "mam_dt", c + 1)
                vec.wait_ge(s["mam_xc"], 2 * c + 2)
                sig(vec.tensor_tensor(u[:, :, :], dt[:, :, :], xc[:, :, :], ALU.mult), "mam_u", c + 1)

            def mam_slot(c, n):
                m = NS * c + n
                vec.wait_ge(s["mam_bB"], m + 1)
                sig(vec.tensor_tensor(UB, u[:, :, :], pB[:, None, :].to_broadcast([P, ND, TC]), ALU.mult), "mam_ub", m + 1)
                for d in range(ND):
                    vec.wait_ge(s["mam_dA"], 2 * m + d + 1)
                    ins = vec.tensor_tensor_scan(Hs[:, d, :], dA[:, 2 * (m % 2) + d, :], UB[:, d, :],
                                                 HL[:, d, n:n + 1] if c else 0.0, ALU.mult, ALU.add)
                sig(ins, "mam_sc", m + 1)
                vec.tensor_copy(HL[:, :, n:n + 1], Hs[:, :, TC - 1:TC])
                vec.wait_ge(s["mam_bC"], m + 1)
                if m >= 2:
                    vec.wait_ge(s["mam_y"], m - 1)
                z = Z[:, 2 * (m % 2):2 * (m % 2) + 2, :]
                sig(vec.tensor_tensor(z, Hs, pC[:, None, :].to_broadcast([P, ND, TC]), ALU.mult), "mam_z", m + 1)

            def mam_end(c):
                vec.wait_ge(s["mam_y"], NS * (c + 1))
                for d in range(ND):
                    vec.tensor_tensor(y2[:, d, :], pY[d][:, :], gz[:, d, :], ALU.mult).then_inc(s["mam_y2"], 1)
                vec.wait_ge(s["mam_o"], c + 1)
                Xc = X[:, c * NJ:(c + 1) * NJ, :]
                sig(vec.tensor_tensor(Xc, Xc, j4(pB[:, :]), ALU.add), "mam_x", c + 1)

            def fft(c):
                ln(c)
                Xc = X[:, c * NJ:(c + 1) * NJ, :]
                link(vec.tensor_tensor(XB[:, :, :], Xc, bias_row[:, None, :].to_broadcast([P, NJ, D]), ALU.add))
                vec.wait_ge(s["fft_o"], c + 1)
                if c >= 2:
                    vec.wait_ge(s[f"out_done{c % 2}"], 16 * (c // 2))
                sig(vec.tensor_tensor(outb[:, c % 2, :, :], j4(pC[:, :]), XB[:, :, :], ALU.add), "fft_x", c + 1)

            vec.wait_ge(s["fr_mm"], 2)
            vec.tensor_copy(g_freq[:, 0, :], pH0[:, 0:P]).then_inc(s["fr_sb"], 1)
            vec.tensor_copy(g_freq[:, 1, :], pH1[:, 0:P]).then_inc(s["fr_sb"], 1)
            vec.wait_ge(s["exp_A"], 1)
            vec.tensor_scalar(a_neg[:, :, :], a_neg[:, :, :], -1.0, None, ALU.mult)
            vec.wait_ge(s["fft_mm"], 1)
            link(vec.scalar_tensor_tensor(w_fft[:, :], pH0[:, 0:P], 1.0 / D, gates[:, 3, :], ALU.mult, ALU.mult))

            moe_prep(0)
            for e in range(E):
                moe_acc(0, e)
            for c in range(NC):
                mam_prep(c)
                if c + 1 < NC:
                    moe_prep(c + 1)
                for n in range(NS):
                    mam_slot(c, n)
                    if c + 1 < NC and n >= 2 and n % 2 == 0:
                        moe_acc(c + 1, n // 2 - 1)
                if c + 1 < NC:
                    moe_acc(c + 1, E - 1)
                mam_end(c)
                fft(c)

        @block.scalar
        def _(act):
            chain = [0]
            L = [0]

            def link(ins):
                ins.then_inc(s["act_chain"], 1)
                chain[0] += 1
                act.wait_ge(s["act_chain"], chain[0])

            act.dma_start(w_mod[:, :], a["w_mod0"]).then_inc(s["ld_small"], 16)
            act.dma_start(group_avg[:, :], a["group_avg"]).then_inc(s["ld_small"], 16)
            act.dma_start(bias_row[:, :], a["fft_bias"].to_broadcast([P, P])).then_inc(s["ld_small"], 16)
            act.dma_start(gel[:, 0, :], a["w_mod1"][:, 0:TC]).then_inc(s["ld_small"], 16)
            act.dma_start(gel[:, 1, 0:256], a["w_mod1"][:, TC:768]).then_inc(s["ld_small"], 16)
            act.wait_ge(s["ld_small"], 16 * 7)
            nc.scalar.activation(silu_c[:, :], cols[:, COL["c0"]:COL["c0"] + 2], ACT.Silu).then_inc(s["silu_c_ready"], 1)

            def ln(dest, m):
                act.wait_ge(s["ln_tr"], L[0] + 1)
                nc.scalar.activation(dest, pT[:, :], ACT.Identity, bias=mods[:, m:m + 1],
                                     scale=mods[:, m + 1:m + 2]).then_inc(s["ln_evac"], 1)
                L[0] += 1

            act.wait_ge(s["set_dve"], 2)
            for c in range(NC):
                ln(hT[:, c, :], 0)

            def xn_of(k, c):
                act.wait_ge(s["gn_ready"], k + 1)
                if c >= 2:
                    act.wait_ge(s["att_kb" if k == 0 else "ffn_h"], (DH if k == 0 else 2) * (c - 1))
                    if k == 0:
                        act.wait_ge(s["att_qb"], DH * (c - 1))
                nc.scalar.activation(xn[:, c % 2, :], hT[:, c, :], ACT.Identity, bias=gn_sb[:, 1:2],
                                     scale=gn_sb[:, 0:1]).then_inc(s["xn_ready"], 1)

            xn_of(0, 0)
            for c in range(NC):
                if c + 1 < NC:
                    xn_of(0, c + 1)
                for k in range(2):
                    act.wait_ge(s["att_qkv"], 3 * c + k + 1)
                    nc.scalar.activation(q2[:, k, :], pY[k][:, :], ACT.Square).then_inc(s["att_sq"], 1)
                act.wait_ge(s["att_ss"], c + 1)
                nc.scalar.activation(nrm[:, :], pC[:, 0:2 * NJ], ACT.Sqrt).then_inc(s["att_nr"], 1)
                act.wait_ge(s["att_rb"], c + 1)
                for k in range(2):
                    nc.scalar.copy(rb[:, k, :], pY[k][:, :]).then_inc(s["att_rbs"], 1)

            xn_of(1, 0)
            for c in range(NC):
                if c + 1 < NC:
                    xn_of(1, c + 1)
                for m in range(2):
                    act.wait_ge(s["ffn_h"], 2 * c + m + 1)
                    if c >= 2:
                        act.wait_ge(s["ffn_o"], c - 1)
                    nc.scalar.activation(h1[:, 2 * (c % 2) + m, :], pH[m][:, :], ACT.Silu,
                                         bias=col(f"b1_{m}")).then_inc(s["ffn_silu"], 1)

            def moe_prep(c):
                ln(h2T[:, c % 2, :], 2)
                act.wait_ge(s["moe_lg"], c + 1)
                nc.scalar.activation(ex[:, :, :], lg[:, :, :], ACT.Exp).then_inc(s["moe_ex"], 1)
                act.wait_ge(s["moe_wt"], c + 1)
                nc.scalar.copy(wT[:, :], pO[:, P:2 * P]).then_inc(s["moe_wts"], 1)

            def moe_slot(c, t):
                for m in range(2):
                    kt = 2 * t + m
                    n = E * NK * c + kt
                    act.wait_ge(s["moe_h"], n + 1)
                    if n >= 4:
                        act.wait_ge(s["moe_g2"], n - 3)
                    nc.scalar.activation(gel[:, n % 4, :], pH[n % 2][:, :], ACT.Gelu_apprx_tanh,
                                         bias=b_e1[:, kt:kt + 1]).then_inc(s["moe_g"], 1)

            def mam_prep(c):
                ln(h3T[:, :], 4)
                act.wait_ge(s["mam_hist"], c + 1)
                for d in range(ND):
                    act.wait_ge(s["mam_xz"], 4 * c + d + 1)
                    nc.scalar.copy(xr[:, d, TAPS - 1:TC + TAPS - 1], pY[d][:, :]).then_inc(s["mam_xr"], 1)
                for d in range(ND):
                    act.wait_ge(s["mam_xz"], 4 * c + 3 + d)
                    nc.scalar.activation(gz[:, d, :], [pB, pC][d][:, :], ACT.Silu).then_inc(s["mam_gz"], 1)
                for d in range(ND):
                    act.wait_ge(s["mam_cv"], 2 * c + d + 1)
                    nc.scalar.activation(xc[:, d, :], cv[:, d, :], ACT.Silu).then_inc(s["mam_xc"], 1)
                act.wait_ge(s["mam_bc"], c + 1)
                nc.scalar.copy(ST[:, :], pB[0:96, :]).then_inc(s["mam_st0"], 1)
                for d in range(ND):
                    act.wait_ge(s["mam_dtp"], 2 * c + d + 1)
                    nc.scalar.activation(ab[:, d, :], pY[d][:, :], ACT.Abs, bias=col(f"b_dt{d}")).then_inc(s["mam_ab"], 1)
                act.wait_ge(s["mam_ab"], 2 * c + 2)
                nc.scalar.activation(exd, ab, ACT.Exp, scale=-1.0).then_inc(s["mam_ex"], 1)
                act.wait_ge(s["mam_ex"], c + 1)
                nc.scalar.activation(lnd, exd, ACT.Ln, bias=1.0).then_inc(s["mam_ln"], 1)

            def mam_slot(c, n):
                m = NS * c + n
                if n == 0:
                    act.wait_ge(s["mam_dt"], c + 1)
                if m >= 2:
                    act.wait_ge(s["mam_sc"], m - 1)
                for d in range(ND):
                    nc.scalar.activation(dA[:, 2 * (m % 2) + d, :], dt[:, d, :], ACT.Exp,
                                         scale=a_neg[:, d, n:n + 1]).then_inc(s["mam_dA"], 1)

            act.wait_ge(s["ld_mam"], 16 * NMA)
            nc.scalar.activation(a_neg[:, :, :], a_neg[:, :, :], ACT.Exp).then_inc(s["exp_A"], 1)
            moe_prep(0)
            for t in range(2 * E):
                moe_slot(0, t)
            for c in range(NC):
                mam_prep(c)
                if c + 1 < NC:
                    moe_prep(c + 1)
                for n in range(NS):
                    mam_slot(c, n)
                    if c + 1 < NC:
                        moe_slot(c + 1, n)
                ln(h4T[:, :], 6)

        @block.tensor
        def _(pe):
            mm = nc.tensor.matmul
            L = [0]

            def ln():
                pe.wait_ge(s["ln_xn"], NJ * (L[0] + 1))
                if L[0]:
                    pe.wait_ge(s["ln_evac"], L[0])
                for j in range(NJ):
                    ins = nc.tensor.transpose(pT[:, j * P:(j + 1) * P], ln_x[:, j, :], ident[:, :])
                ins.then_inc(s["ln_tr"], 1)
                L[0] += 1

            def gn(g):
                pe.wait_ge(s["gn_m"], g + 1)
                mm(pO[:, 0:2], group_avg[:, :], gn_me[:, :], start=True, stop=True).then_inc(s["gn_mm"], 1)

            pe.wait_ge(s["ld_small"], 16 * 7)
            pe.wait_ge(s["set_cb"], 2)
            for l in range(2):
                def wm(k):
                    if l == 0:
                        return w_mod[:, k * P:(k + 1) * P]
                    return gel[:, k // 4, (k % 4) * P:(k % 4 + 1) * P]
                if l:
                    pe.wait_ge(s["set_dve"], 1)
                for i, k in enumerate((0, 1, 3, 4)):
                    mm(pT[:, i:i + 1], wm(k), silu_c[:, l:l + 1], start=True, stop=True)
                for i, k in enumerate((2, 5)):
                    ins = mm(pO[:, i * P:(i + 1) * P], silu_cb[:, l, :], wm(k), start=True, stop=True)
                    ins.then_inc(s["mod_mm"], 1)
            pe.wait_ge(s["set_dve"], 2)
            for c in range(NC):
                ln()
            gn(0)
            pe.wait_ge(s["ld_attn"], 16 * NAT)
            pe.wait_ge(s["set_pool"], 1)
            for c in range(NC):
                x_ = xn[:, c % 2, :]
                pe.wait_ge(s["xn_ready"], c + 1)
                if c:
                    pe.wait_ge(s["att_x2"], c)
                for k, bank in enumerate((pY0, pY1, pB)):
                    mm(bank[:, :], w_qkv[:, k, :], x_, start=True, stop=True).then_inc(s["att_qkv"], 1)
                pe.wait_ge(s["att_sq"], 2 * c + 2)
                for k in range(2):
                    for j in range(NJ):
                        ins = mm(pC[:, k * NJ + j:k * NJ + j + 1], q2[:, k, j * P:(j + 1) * P], ones[:, 0:1],
                                 start=True, stop=True)
                ins.then_inc(s["att_ss"], 1)
                pe.wait_ge(s["att_r"], c + 1)
                for k in range(2):
                    for j in range(NJ):
                        r = rnm[:, k * NJ + j:k * NJ + j + 1].to_broadcast([P, P])
                        ins = mm(pY[k][:, j * P:(j + 1) * P], r, ident[:, :], start=True, stop=True)
                ins.then_inc(s["att_rb"], 1)

                def project(i):
                    n = DH * c + i
                    pe.wait_ge(s["att_z"], n)
                    mm(pO[:, :], w_o[:, :], ZA[:, (i - 1) % 2, :], start=(i == 1), stop=(i == DH)).then_inc(s["att_ow"], 1)

                for i in range(DH):
                    n = DH * c + i
                    if n >= 2:
                        pe.wait_ge(s["att_u"], n - 1)
                    mm(pH[i % 2][:, :], w_kq_rep[:, 0, i, :], x_, start=True, stop=True).then_inc(s["att_kb"], 1)
                    if n >= 2:
                        pe.wait_ge(s["att_z"], n - 1)
                    mm([pC, pT][i % 2][:, :], w_kq_rep[:, 1, i, :], x_, start=True, stop=True).then_inc(s["att_qb"], 1)
                    if i:
                        project(i)
                project(DH)
            gn(1)
            pe.wait_ge(s["ld_ffn"], 16 * NFF)

            def ffn_tok(c):
                pe.wait_ge(s["ffn_x3"], c + 1)
                if c >= 2:
                    pe.wait_ge(s["ffn_x1"], c - 1)
                for j in range(NJ):
                    ins = mm([pB, pC][c % 2][:, j * P:(j + 1) * P], x3T[:, c % 2, j * P:(j + 1) * P], diag_ga[:, :],
                             start=True, stop=True)
                ins.then_inc(s["ffn_tok"], 1)

            for c in range(NC):
                pe.wait_ge(s["xn_ready"], NC + c + 1)
                for m in range(2):
                    if c:
                        pe.wait_ge(s["ffn_silu"], 2 * c + m - 1)
                    mm(pH[m][:, :], w_f1[:, m, :], xn[:, c % 2, :], start=True, stop=True).then_inc(s["ffn_h"], 1)
                if c:
                    ffn_tok(c - 1)
                for m in range(2):
                    pe.wait_ge(s["ffn_silu"], 2 * c + m + 1)
                    if m == 0 and c >= 2:
                        pe.wait_ge(s["ffn_x3"], c - 1)
                    ins = mm(pY[c % 2][:, :], w_f2[:, m, :], h1[:, 2 * (c % 2) + m, :], start=(m == 0), stop=(m == 1))
                ins.then_inc(s["ffn_o"], 1)
            ffn_tok(NC - 1)

            pe.wait_ge(s["ld_mam"], 16 * NMA)
            pe.wait_ge(s["ffn_silu"], 2 * NC)
            for k in range(2):
                mm(pH[k][:, 0:P], w_freq[:, k, :], dft[:, 0, :], start=True, stop=False)
                mm(pH[k][:, 0:P], w_freq[:, 1 - k, :], dft[:, 1 + k, :], start=False, stop=True).then_inc(s["fr_mm"], 1)
            pe.wait_ge(s["fr_sb"], 2)
            mm(pH0[:, 0:P], g_freq[:, 0, :], dft[:, 0, :], start=True, stop=False)
            mm(pH0[:, 0:P], g_freq[:, 1, :], dft[:, 2, :], start=False, stop=True).then_inc(s["fft_mm"], 1)

            def moe_prep(c):
                ln()
                pe.wait_ge(s["ln_evac"], L[0])
                if c:
                    pe.wait_ge(s["moe_acc"], E * c)
                else:
                    pe.wait_ge(s["ffn_x1"], NC)
                    pe.wait_ge(s["set_pool"], 5)
                    pe.wait_ge(s["ld_moe"], 16 * NMO)
                h = h2T[:, c % 2, :]
                for j in range(NJ):
                    ins = mm(pO[:, j * E:(j + 1) * E], h[:, j * P:(j + 1) * P], w_router[:, :], start=True, stop=True)
                ins.then_inc(s["moe_rt"], 1)
                pe.wait_ge(s["moe_w"], c + 1)
                nc.tensor.transpose(pO[:, P:2 * P], wts[:, :], ident[:, :]).then_inc(s["moe_wt"], 1)
                pe.wait_ge(s["moe_wts"], c + 1)
                for j in range(NJ):
                    ins = mm(pO[:, j * P:(j + 1) * P], wT[:, :], b_e2[:, j, :], start=True, stop=True)
                ins.then_inc(s["moe_bias"], 1)

            def moe_up(c, t):
                for m in range(2):
                    kt = 2 * t + m
                    n = E * NK * c + kt
                    if n >= 2:
                        pe.wait_ge(s["moe_g"], n - 1)
                    mm(pH[n % 2][:, :], w_e1[:, kt // NK, (kt % NK) * P:(kt % NK + 1) * P], h2T[:, c % 2, :],
                       start=True, stop=True).then_inc(s["moe_h"], 1)

            def moe_down(c, t):
                for m in range(2):
                    kt = 2 * t + m
                    e, k = kt // NK, kt % NK
                    n = E * NK * c + kt
                    if k == 0:
                        if e == 0:
                            pe.wait_ge(s["moe_xb"], c + 1)
                        else:
                            pe.wait_ge(s["moe_acc"], E * c + e)
                    pe.wait_ge(s["moe_g"], n + 1)
                    for j in range(NJ):
                        ins = mm(pO[:, j * P:(j + 1) * P], gel[:, n % 4, j * P:(j + 1) * P], w_e2[:, kt, :],
                                 start=(k == 0 and j == 0), stop=(k == NK - 1 and j == NJ - 1), skip_group_check=True)
                    ins.then_inc(s["moe_g2"], 1)

            def mam_prep(c):
                ln()
                pe.wait_ge(s["ln_evac"], L[0])
                if c:
                    pe.wait_ge(s["mam_y2"], 2 * c)
                    pe.wait_ge(s["mam_x"], c)
                    pe.wait_ge(s["fft_x"], c)
                for m, bank in enumerate((pY0, pY1, pB, pC)):
                    mm(bank[:, :], w_in[:, m, :], h3T[:, :], start=True, stop=True).then_inc(s["mam_xz"], 1)
                pe.wait_ge(s["mam_gz"], 2 * c + 1)
                mm(pB[0:96, :], w_bc[:, :], h3T[:, :], start=True, stop=True).then_inc(s["mam_bc"], 1)
                for d in range(ND):
                    pe.wait_ge(s["mam_xr"], 2 * c + d + 1)
                    mm(pY[d][:, :], w_dt[:, d, :], h3T[:, :], start=True, stop=True).then_inc(s["mam_dtp"], 1)

            def mam_rows(c, n):
                m = NS * c + n
                if n == 0:
                    pe.wait_ge(s["mam_st"], c + 1)
                    pe.wait_ge(s["mam_gz"], 2 * c + 2)
                if m:
                    pe.wait_ge(s["mam_ub"], m)
                mm(pB[:, :], sel[:, n, :], ST[:, :], start=True, stop=True).then_inc(s["mam_bB"], 1)
                if m:
                    pe.wait_ge(s["mam_z"], m)
                mm(pC[:, :], sel[:, NS + n, :], ST[:, :], start=True, stop=True).then_inc(s["mam_bC"], 1)

            def mam_sum(c, n):
                m = NS * c + n
                if n == 0:
                    pe.wait_ge(s["mam_u"], c + 1)
                pe.wait_ge(s["mam_z"], m + 1)
                for d in range(ND):
                    ins = mm(pY[d][:, :], ident[:, :], Z[:, 2 * (m % 2) + d, :], start=(n == 0), stop=(n == NS - 1))
                ins.then_inc(s["mam_y"], 1)

            def mam_end(c):
                pe.wait_ge(s["mam_y2"], 2 * c + 2)
                for j in range(NJ):
                    for d in range(ND):
                        ins = mm(pB[:, j * P:(j + 1) * P], y2[:, d, j * P:(j + 1) * P], w_out[:, d, :],
                                 start=(d == 0), stop=(d == 1))
                ins.then_inc(s["mam_o"], 1)

            def fft(c):
                ln()
                pe.wait_ge(s["ln_evac"], L[0])
                for j in range(NJ):
                    ins = mm(pC[:, j * P:(j + 1) * P], h4T[:, j * P:(j + 1) * P], w_fft[:, :], start=True, stop=True)
                ins.then_inc(s["fft_o"], 1)

            moe_prep(0)
            for t in range(2 * E):
                moe_up(0, t)
                if t:
                    moe_down(0, t - 1)
            moe_down(0, 2 * E - 1)
            for c in range(NC):
                mam_prep(c)
                if c + 1 < NC:
                    moe_prep(c + 1)
                for n in range(NS):
                    mam_rows(c, n)
                    if c + 1 < NC:
                        moe_up(c + 1, n)
                        if n:
                            moe_down(c + 1, n - 1)
                    if n:
                        mam_sum(c, n - 1)
                if c + 1 < NC:
                    moe_down(c + 1, NS - 1)
                mam_sum(c, NS - 1)
                mam_end(c)
                fft(c)


def constants():
    n = np.arange(D)
    turn = 2 * np.pi * (np.outer(n, n) % D) / D
    dft = np.stack([np.cos(turn), np.sin(turn), -np.sin(turn)], 1).astype(np.float32)
    group = (n[:, None] // DH == n[None, :] // DH).astype(np.float32) / DH
    tie = np.broadcast_to((np.arange(E)[None, :] < np.arange(E)[:, None]).astype(np.float32), (P, E, E))
    m = np.arange(96) % 32
    part_row = (m[:, None] == np.arange(2 * NS)[None, :]).astype(np.float32)
    gam = np.float32(1.0) - np.exp(np.linspace(np.log(1 / 32), np.log(1 / 512), HEADS).astype(np.float32))
    return {"dft": dft, "group_avg": group, "tie": np.ascontiguousarray(tie), "part_row": part_row,
            "ident": np.eye(P, dtype=np.float32), "gamma": np.repeat(gam.astype(np.float32), DH)}


def kernel(**inputs):
    import concourse.bacc as bacc
    from concourse.bass_utils import run_bass_kernel_spmd

    v = {k: np.asarray(x) for k, x in inputs.items()}
    k = constants()

    def tiles(w, n):
        return w.reshape(w.shape[0], n, -1)

    def rows(w, n):
        return w.reshape(n, P, -1).transpose(1, 0, 2)

    qT, kT, vT = (v[f"L0_attn_{n}w"].T for n in "qkv")
    rep = [np.repeat(w.reshape(D, HEADS, DH).transpose(0, 2, 1), DH, axis=2) for w in (kT, qT)]
    cols = {
        "norm_g": v["L0_attn_norm_g"], "norm_b": v["L0_attn_norm_b"], "ob": v["L0_attn_ob"],
        "ffn_g": v["L0_attn_ffn_norm_g"], "ffn_b": v["L0_attn_ffn_norm_b"],
        "b1_0": v["L0_attn_b1"][:P], "b1_1": v["L0_attn_b1"][P:], "b2": v["L0_attn_b2"],
        "conv_b0": v["L1_attn_conv_b"][:P], "conv_b1": v["L1_attn_conv_b"][P:],
        "b_dt0": v["L1_attn_b_dt"][:P], "b_dt1": v["L1_attn_b_dt"][P:],
        "c0": v["L0_c"][0], "c1": v["L1_c"][0], "gamma": k["gamma"],
    }
    for d in range(ND):
        for t in range(TAPS):
            cols[f"conv_w{d}{t}"] = v["L1_attn_conv_w"][d * P:(d + 1) * P, 0, t]
    w_dt = np.zeros((P, DI), np.float32)
    w_dt[:RANK] = v["L1_attn_W_dt"].T
    b_e2 = np.zeros((P, NJ, P), np.float32)
    for j in range(NJ):
        b_e2[j * E:(j + 1) * E, j] = v["L0_ffn_b2"]
    bc = np.concatenate([v["L1_attn_W_B"], v["L1_attn_W_C"]], 0).T
    arrays = {
        "x": v["L0_attn_x"][0], "cols": np.stack([cols[n] for n in COLS], 1), "ident": k["ident"],
        "group_avg": k["group_avg"], "dft": k["dft"], "tie": k["tie"], "part_row": k["part_row"],
        "w_qkv": np.stack([qT, kT, vT], 1), "w_kq_rep": np.stack(rep, 1), "w_o": v["L0_attn_ow"].T,
        "w_f1": tiles(v["L0_attn_w1"].T, 2), "w_f2": rows(v["L0_attn_w2"].T, 2),
        "w_router": v["L0_ffn_w_router"], "w_e1": v["L0_ffn_w1"].transpose(1, 0, 2),
        "w_e2": v["L0_ffn_w2"].reshape(E * NK, P, D).transpose(1, 0, 2),
        "b_e1": v["L0_ffn_b1"].reshape(E * NK, P).T, "b_e2": b_e2,
        "w_mod0": v["L0_wmod"], "w_mod1": v["L1_wmod"],
        "w_in": tiles(v["L1_attn_W_in"].T, 4), "w_dt": tiles(w_dt, ND),
        "w_bc": np.concatenate([bc, bc, bc], 1), "w_out": rows(v["L1_attn_W_out"].T, ND),
        "a_log": rows(v["L1_attn_A_log"], ND),
        "w_freq": np.stack([v["L1_ffn_w_freq_real"], v["L1_ffn_w_freq_imag"]], 1),
        "fft_bias": v["L1_ffn_bias"][None],
    }
    arrays = {n: np.ascontiguousarray(x) for n, x in arrays.items()}
    nc = bacc.Bacc("TRN2", target_bir_lowering=False, num_devices=1)
    aps = {n: nc.dram_tensor(f"in_{n}", x.shape, mybir.dt.from_np(x.dtype), kind="ExternalInput").ap()
           for n, x in arrays.items()}
    out = nc.dram_tensor("out_0", (T, D), F32, kind="ExternalOutput").ap()
    build(nc, aps, out)
    r = run_bass_kernel_spmd(nc, [{f"in_{n}": x for n, x in arrays.items()}], core_ids=[0])
    return r.results[0]["out_0"].reshape(1, T, D)
```

```python
from contextlib import ExitStack

import numpy as np

import concourse.bass as bass
from concourse import mybir

ALU = mybir.AluOpType
ACT = mybir.ActivationFunctionType
AX = mybir.AxisListType
F32 = mybir.dt.float32
BF16 = mybir.dt.bfloat16

P = 128
T = 2048
D = 128
TC = 512
NC = T // TC
NJ = TC // P
HEADS = 16
DH = D // HEADS
E = 8
HID = 512
NK = HID // P
NS = 16
DI = 256
ND = DI // P
TAPS = 4
RANK = 64
EPS = 1e-5
NP = NS // 2
AHEAD = 12

COLS = ["norm_g", "norm_b", "ob", "ffn_g", "ffn_b", "b1_0", "b1_1", "b2", "conv_b0", "conv_b1",
        "b_dt0", "b_dt1", "c0", "c1", "gamma"] + [f"conv_w{d}{k}" for d in range(ND) for k in range(TAPS)]
COL = {n: i for i, n in enumerate(COLS)}


def build(nc, a, out):
    ctx = ExitStack()
    with ctx:
        def sb(name, shape, dt=F32):
            return ctx.enter_context(nc.sbuf_tensor(name, shape, dt))

        def ps(name):
            return ctx.enter_context(nc.psum_tensor(name, [P, TC], F32))

        def sem(name):
            return ctx.enter_context(nc.semaphore(name))

        cols = sb("cols", [P, len(COLS)])
        ident = sb("ident", [P, P])
        tie = sb("tie", [P, E, E])
        sel = sb("sel", [96, 2 * NS, P], BF16)
        w_router = sb("w_router", [P, E])
        w_e1 = sb("w_e1", [P, E, HID])
        w_e2 = sb("w_e2", [P, E * NK, P])
        b_e1 = sb("b_e1", [P, E * NK])
        b_e2 = sb("b_e2", [P, NJ, P])
        w_in = sb("w_in", [P, 4, P])
        w_dt = sb("w_dt", [P, ND, P])
        w_bc = sb("w_bc", [P, 96])
        w_out = sb("w_out", [P, ND, P])
        a_neg = sb("a_neg", [P, ND, NS])
        w_fft = sb("w_fft", [P, P])
        bias_row = sb("bias_row", [P, P])
        mods = sb("mods", [P, 8])
        gates = sb("gates", [P, 4, P])
        mhalf = sb("mhalf", [P, NJ])
        X = sb("X", [P, NC * NJ, D])
        ln_st = sb("ln_st", [P, NJ, 6])
        ln_mv = sb("ln_mv", [P, NJ, 2])
        ln_ve = sb("ln_ve", [P, NJ])
        ln_rs = sb("ln_rs", [P, NJ])
        ln_x = sb("ln_x", [P, NJ, D])
        wts = sb("wts", [P, 2, P])
        wT = sb("wT", [P, P])

        early = ExitStack()

        def sbe(name, shape, dt=F32):
            return early.enter_context(nc.sbuf_tensor(name, shape, dt))

        ones = sbe("ones", [P, 8])
        group_avg = sbe("group_avg", [P, P])
        dft = sbe("dft", [P, 3, P])
        part_row = sbe("part_row", [96, 2 * NS])
        w_qkv = sbe("w_qkv", [P, 3, P])
        w_kq_rep = sbe("w_kq_rep", [P, 2, DH, P])
        w_o = sbe("w_o", [P, P])
        w_f1 = sbe("w_f1", [P, 2, P])
        w_f2 = sbe("w_f2", [P, 2, P])
        w_mod = sbe("w_mod", [P, 2, 6 * P])
        w_freq = sbe("w_freq", [P, 2, P])
        g_freq = sbe("g_freq", [P, 2, P])
        silu_c = sbe("silu_c", [P, 2])
        silu_cb = sbe("silu_cb", [P, 2, P])
        gate_t = sbe("gate_t", [P, 2, P])
        diag_ga = sbe("diag_ga", [P, P])
        hT = sbe("hT", [P, NC, TC])
        gn_st = sbe("gn_st", [P, NC, 6])
        gn_mv = sbe("gn_mv", [P, 2])
        gn_me = sbe("gn_me", [P, 2])
        gn_g = sbe("gn_g", [P, 2])
        gn_ve = sbe("gn_ve", [P, 1])
        gn_rs = sbe("gn_rs", [P, 1])
        gn_sb = sbe("gn_sb", [P, 2])
        xn = sbe("xn", [P, 2, TC])
        vp = sbe("vp", [P, TC])
        att_t = sbe("att_t", [P, TC])
        nrm = sbe("nrm", [P, 2 * NJ])
        rnm = sbe("rnm", [P, 2 * NJ])
        x3T = sbe("x3T", [P, 2, TC])
        S = sbe("S", [P, DH, TC])
        q2 = sbe("q2", [P, 2, TC])
        rb = sbe("rb", [P, 2, TC])
        U = sbe("U", [P, 2, TC])
        ZA = sbe("ZA", [P, 2, TC])
        h1 = sbe("h1", [P, 4, TC])
        early.close()

        h2T = sb("h2T", [P, 2, TC])
        h3T = sb("h3T", [P, TC])
        h4T = h3T
        gel = sb("gel", [P, 2 * NK, TC])
        lg = sb("lg", [P, NJ, E])
        ex = sb("ex", [P, NJ, E])
        pr = sb("pr", [P, NJ, E])
        s4 = sb("s4", [P, 3, NJ])
        cmp_ = sb("cmp", [P, 2, NJ * E, E])
        rank = sb("rank", [P, NJ, E])
        dA = sb("dA", [P, 2 * 2 * ND, TC])
        UB = sb("UB", [P, ND, TC])
        UBo = sb("UBo", [P, 2 * ND, TC])
        Bsb = sb("Bsb", [P, 2, TC])
        Hs = sb("Hs", [P, 2 * ND, TC])
        Zev = sb("Zev", [P, 2 * ND, TC])
        Zod = sb("Zod", [P, ND, TC])
        ZS = sb("ZS", [P, 2 * ND, TC])
        Csb = sb("Csb", [P, 2, TC])
        exd = sb("exd", [P, ND, TC])
        lnd = sb("lnd", [P, ND, TC])
        y2 = exd
        xr = sb("xr", [P, ND, TC + TAPS - 1])
        cv = sb("cv", [P, ND, TC])
        wx = cv
        gz = sb("gz", [P, 2 * ND, TC])
        xc = sb("xc", [P, ND, TC])
        dt = sb("dt", [P, 2 * ND, TC])
        u = sb("u", [P, 2 * ND, TC])
        BCf = sb("BCf", [96, TC])
        P1 = sb("P1", [96, TC], BF16)
        ST = sb("ST", [96, 2, TC], BF16)
        HL = sb("HL", [P, ND, NS])
        outb = sb("outb", [P, 2, NJ, D])
        XB = sb("XB", [P, NJ, D])

        pT, pO, pH0, pH1, pY0, pY1, pB, pC = (ps(n) for n in ("pT", "pO", "pH0", "pH1", "pY0", "pY1", "pB", "pC"))
        pH = [pH0, pH1]
        pY = [pY0, pY1]

        def j4(ap):
            return ap.rearrange("p (j d) -> p j d", j=NJ)

        def half_of(t, c):
            return t[:, ND * (c % 2):ND * (c % 2) + ND, :]

        def col(n):
            return cols[:, COL[n]:COL[n] + 1]

        names = """ld_small ld_attn ld_ffn ld_moe ld_mam
            silu_c_ready mod_mm set_cb set_dve set_pool fr_mm fr_sb fft_mm exp_A
            ln_stats ln_rstd ln_xn ln_tr ln_evac
            gn_m gn_mm gn_v gn_r gn_ready xn_ready
            att_qkv att_sq att_ss att_nr att_r att_rb att_rbs att_kb att_qb att_u att_z att_ow att_x2
            ffn_h ffn_silu ffn_o ffn_x3 ffn_tok ffn_x1
            moe_rt moe_lg moe_ex moe_w moe_wt moe_wts moe_bias moe_xb moe_h moe_g moe_g2 moe_acc
            mam_hist mam_xz mam_xr mam_gz mam_dtp mam_bc mam_bcs mam_cv mam_xc mam_v mam_ab mam_ex mam_w mam_ln mam_dt mam_u
            mam_st0 mam_st mam_Bs mam_uo mam_Cs mam_zo mam_zs mam_bB mam_bC mam_ub mam_dA mam_sc mam_z mam_y mam_y2 mam_o mam_x
            fft_o fft_b fft_x vec_chain act_chain pool_chain out_done0 out_done1""".split()
        s = {n: sem(n) for n in names}
        ld_x = [sem(f"ld_x{c}") for c in range(NC)]
        NSM, NAT, NFF, NMO, NMA = 6, 3, 2, 5, 9

        block = ctx.enter_context(nc.Block())

        def later_stages():
            def between(p, o):
                c, at = p // NP, 2 * (p % NP) + o
                head, tail, front = c + 2, c - 1, c + 1
                if 0 <= tail:
                    yield from {1: [("gate", tail)], 2: [("project", tail), ("ln_stats", tail)],
                                3: [("ln_apply", tail, 2)], 4: [("fft", tail)]}.get(at, [])
                if 0 < head < NC:
                    yield from {4: [("ln_stats", head)], 5: [("ln_apply", head, 0)], 6: [("route", head)],
                                7: [("turn", head)], 8: [("weigh", head)]}.get(at, [])
                if 0 <= front < NC:
                    yield from {10: [("ln_stats", front)], 11: [("ln_apply", front, 1)],
                                12: [("x_part", front), ("rows", front)], 13: [("dt_part", front), ("z_part", front)],
                                14: [("step", front)]}.get(at, [])
            yield from [("ln_stats", 0), ("ln_apply", 0, 0), ("route", 0), ("turn", 0), ("weigh", 0)]
            for p in range(-AHEAD, NC * NP):
                for o in range(2):
                    yield ("half", p, o)
                    yield from between(p, o)
            yield from [("total", NC * NP - 1), ("gate", NC - 1), ("project", NC - 1), ("ln_stats", NC - 1),
                        ("ln_apply", NC - 1, 2), ("fft", NC - 1)]

        @block.sync
        def _(sp):
            sp.dma_start(cols[:, :], a["cols"]).then_inc(s["ld_small"], 16)
            xv = a["x"].rearrange("(c j p) d -> c p j d", c=NC, j=NJ)
            for c in range(NC):
                sp.dma_start(X[:, c * NJ:(c + 1) * NJ, :], xv[c]).then_inc(ld_x[c], 16)
                if c == 0:
                    sp.dma_start(ident[:, :], a["ident"]).then_inc(s["ld_small"], 16)
            sp.dma_start(w_kq_rep[:, :, :, :], a["w_kq_rep"]).then_inc(s["ld_attn"], 16)
            sp.dma_start(w_qkv[:, :, :], a["w_qkv"]).then_inc(s["ld_attn"], 16)
            sp.dma_start(w_o[:, :], a["w_o"]).then_inc(s["ld_attn"], 16)
            sp.dma_start(w_f1[:, :, :], a["w_f1"]).then_inc(s["ld_ffn"], 16)
            sp.dma_start(w_f2[:, :, :], a["w_f2"]).then_inc(s["ld_ffn"], 16)
            sp.dma_start(w_router[:, :], a["w_router"]).then_inc(s["ld_moe"], 16)
            sp.dma_start(w_e1[:, :, :], a["w_e1"]).then_inc(s["ld_moe"], 16)
            sp.dma_start(w_e2[:, :, :], a["w_e2"]).then_inc(s["ld_moe"], 16)
            sp.dma_start(b_e1[:, :], a["b_e1"]).then_inc(s["ld_moe"], 16)
            sp.dma_start(b_e2[:, :, :], a["b_e2"]).then_inc(s["ld_moe"], 16)
            for n, t in (("w_in", w_in), ("w_dt", w_dt), ("w_bc", w_bc), ("w_out", w_out), ("a_log", a_neg),
                         ("w_freq", w_freq), ("part_row", part_row), ("tie", tie), ("dft", dft)):
                sp.dma_start(t[:], a[n]).then_inc(s["ld_mam"], 16)
            ov = out.rearrange("(c j p) d -> c p j d", c=NC, j=NJ)
            for c in range(NC):
                sp.wait_ge(s["fft_x"], c + 1)
                sp.dma_start(ov[c], outb[:, c % 2, :, :]).then_inc(s[f"out_done{c % 2}"], 16)
            for p_ in range(2):
                sp.wait_ge(s[f"out_done{p_}"], 16 * (NC // 2))

        @block.gpsimd
        def _(pool):
            chain = [0]

            def link(ins):
                ins.then_inc(s["pool_chain"], 1)
                chain[0] += 1
                pool.wait_ge(s["pool_chain"], chain[0])

            L = [0]

            def ln():
                pool.wait_ge(s["ln_stats"], L[0] + 1)
                link(pool.tensor_scalar(ln_ve[:, :], ln_mv[:, :, 1], EPS, None, ALU.add))
                pool.tensor_tensor(ln_rs[:, :], ln_ve[:, :], mhalf[:, :], ALU.pow).then_inc(s["ln_rstd"], 1)
                L[0] += 1

            def gn(g):
                pool.wait_ge(s["gn_v"], g + 1)
                pool.tensor_tensor(gn_rs[:, :], gn_ve[:, :], mhalf[:, 0:1], ALU.pow).then_inc(s["gn_r"], 1)

            def odd_input(p):
                c = p // NP
                pool.wait_ge(s["mam_Bs"], p + 1)
                pool.wait_ge(s["mam_u"], c + 1)
                if p >= 2:
                    pool.wait_ge(s["mam_sc"], 2 * (p - 1))
                h = slice(2 * (p % 2), 2 * (p % 2) + 2)
                pool.tensor_tensor(UBo[:, h, :], half_of(u, c), Bsb[:, p % 2:p % 2 + 1, :].to_broadcast([P, ND, TC]),
                                   ALU.mult).then_inc(s["mam_uo"], 1)

            def odd_output(p):
                pool.wait_ge(s["mam_Cs"], p + 1)
                if p:
                    pool.wait_ge(s["mam_zs"], p)
                pool.wait_ge(s["mam_sc"], 2 * p + 2)
                pool.tensor_tensor(Zod[:, :, :], Hs[:, 2:4, :], Csb[:, p % 2:p % 2 + 1, :].to_broadcast([P, ND, TC]),
                                   ALU.mult).then_inc(s["mam_zo"], 1)
                pool.wait_ge(s["mam_zo"], p + 1)
                pool.wait_ge(s["mam_z"], p + 1)
                if p >= 2:
                    pool.wait_ge(s["mam_y"], p - 1)
                h = slice(2 * (p % 2), 2 * (p % 2) + 2)
                pool.tensor_tensor(ZS[:, h, :], Zev[:, h, :], Zod[:, :, :], ALU.add).then_inc(s["mam_zs"], 1)

            link(pool.memset(mhalf[:, :], -0.5))
            pool.memset(ones[:, :], 1.0).then_inc(s["set_pool"], 1)
            for c in range(NC):
                ln()
            gn(0)
            pool.wait_ge(s["ld_moe"], 16 * NMO)
            pool.wait_ge(s["set_dve"], 1)
            gb = gates[:, 1:2, :]
            pool.tensor_tensor(w_e2[:, :, :], w_e2[:, :, :], gb.to_broadcast([P, E * NK, P]), ALU.mult).then_inc(s["set_pool"], 1)
            pool.tensor_tensor(b_e2[:, :, :], b_e2[:, :, :], gb.to_broadcast([P, NJ, P]), ALU.mult).then_inc(s["set_pool"], 1)
            pool.wait_ge(s["ld_mam"], 16 * NMA)
            pool.tensor_tensor(w_out[:, :, :], w_out[:, :, :], gates[:, 2:3, :].to_broadcast([P, ND, P]), ALU.mult).then_inc(s["set_pool"], 1)
            pool.tensor_copy(sel[:, :, :], part_row[:, :, None].to_broadcast([96, 2 * NS, P])).then_inc(s["set_pool"], 1)
            gn(1)
            for stage, c, *k in later_stages():
                if stage == "ln_stats":
                    ln()
                elif stage == "half" and k[0] == 1:
                    p = c
                    if 0 <= p + 1 < NC * NP and (p + 1) % NP:
                        odd_input(p + 1)
                    if p >= 0:
                        odd_output(p)
                    if 0 <= p + 1 < NC * NP and (p + 1) % NP == 0:
                        odd_input(p + 1)
                elif stage == "rows":
                    st = ST[:, c % 2, :]
                    pool.wait_ge(s["mam_st0"], c + 1)
                    link(pool.tensor_tensor(st[32:64, :], BCf[32:64, :], st[32:64, :], ALU.subtract))
                    link(pool.tensor_tensor(P1[64:96, :], BCf[64:96, :], st[64:96, :], ALU.subtract))
                    link(pool.tensor_tensor(BCf[64:96, :], BCf[64:96, :], st[64:96, :], ALU.subtract))
                    pool.tensor_tensor(st[64:96, :], BCf[64:96, :], P1[64:96, :], ALU.subtract).then_inc(s["mam_st"], 1)
                    pool.wait_ge(s["mam_st"], c + 1)
                elif stage == "fft":
                    pool.wait_ge(s["mam_x"], c + 1)
                    if c:
                        pool.wait_ge(s["fft_x"], c)
                    pool.tensor_tensor(XB[:, :, :], X[:, c * NJ:(c + 1) * NJ, :], bias_row[:, None, :].to_broadcast([P, NJ, D]),
                                       ALU.add).then_inc(s["fft_b"], 1)

        @block.vector
        def _(vec):
            chain = [0]
            L = [0]

            def link(ins):
                ins.then_inc(s["vec_chain"], 1)
                chain[0] += 1
                vec.wait_ge(s["vec_chain"], chain[0])

            def sig(ins, name, count):
                ins.then_inc(s[name], 1)
                vec.wait_ge(s[name], count)

            def ln_stats(c):
                Xc = X[:, c * NJ:(c + 1) * NJ, :]
                for j in range(NJ):
                    ins = vec.bn_stats(ln_st[:, j, :], Xc[:, j, :])
                link(ins)
                for j in range(NJ):
                    ins = vec.bn_aggr(ln_mv[:, j, :], ln_st[:, j, :])
                ins.then_inc(s["ln_stats"], 1)

            def ln_apply(c):
                Xc = X[:, c * NJ:(c + 1) * NJ, :]
                vec.wait_ge(s["ln_stats"], L[0] + 1)
                vec.wait_ge(s["ln_rstd"], L[0] + 1)
                if L[0]:
                    vec.wait_ge(s["ln_tr"], L[0])
                for j in range(NJ):
                    vec.tensor_scalar(ln_x[:, j, :], Xc[:, j, :], ln_mv[:, j, 0:1], ln_rs[:, j:j + 1],
                                      ALU.subtract, ALU.mult).then_inc(s["ln_xn"], 1)
                L[0] += 1

            def gn(g, gamma, beta):
                link(vec.bn_aggr(gn_mv[:, :], gn_st[:, :, :].rearrange("p c k -> p (c k)")))
                vec.tensor_copy(gn_me[:, 0:1], gn_mv[:, 0:1])
                vec.scalar_tensor_tensor(gn_me[:, 1:2], gn_mv[:, 0:1], gn_mv[:, 0:1], gn_mv[:, 1:2],
                                         ALU.mult, ALU.add).then_inc(s["gn_m"], 1)
                vec.wait_ge(s["gn_mm"], g + 1)
                link(vec.tensor_copy(gn_g[:, :], pO[:, 0:2]))
                link(vec.scalar_tensor_tensor(gn_ve[:, :], gn_g[:, 0:1], gn_g[:, 0:1], gn_g[:, 1:2],
                                              ALU.mult, ALU.subtract))
                vec.tensor_scalar(gn_ve[:, :], gn_ve[:, :], -1.0, EPS, ALU.mult, ALU.add).then_inc(s["gn_v"], 1)
                vec.wait_ge(s["gn_r"], g + 1)
                link(vec.tensor_tensor(gn_sb[:, 0:1], gn_rs[:, :], col(gamma), ALU.mult))
                link(vec.scalar_tensor_tensor(gn_sb[:, 1:2], gn_g[:, 0:1], gn_sb[:, 0:1], col(beta),
                                              ALU.mult, ALU.subtract))
                vec.tensor_scalar(gn_sb[:, 1:2], gn_sb[:, 1:2], -1.0, None, ALU.mult).then_inc(s["gn_ready"], 1)

            vec.wait_ge(s["silu_c_ready"], 1)
            vec.tensor_copy(silu_cb[:, 0, :], silu_c[:, 0:1].to_broadcast([P, P])).then_inc(s["set_cb"], 1)
            vec.tensor_copy(silu_cb[:, 1, :], silu_c[:, 1:2].to_broadcast([P, P])).then_inc(s["set_cb"], 1)
            vec.memset(wts[:, :, :], 0.0)
            for l in range(2):
                vec.wait_ge(s["mod_mm"], 2 * l + 2)
                vec.tensor_copy(mods[:, 4 * l:4 * l + 4], pT[:, 0:4])
                link(vec.tensor_copy(gates[:, 2 * l:2 * l + 2, :], pO[:, 0:256].rearrange("p (g d) -> p g d", g=2)))
                g = gates[:, 2 * l:2 * l + 2, :]
                link(vec.tensor_scalar(gate_t[:, :, :], g, 0.0, 2.0, ALU.is_ge, ALU.mult))
                link(vec.scalar_tensor_tensor(g, g, -1.0, g, ALU.mult, ALU.max))
                link(vec.tensor_scalar(g, g, 0.25, None, ALU.max))
                link(vec.scalar_tensor_tensor(g, gate_t[:, :, :], -1.0, g, ALU.add, ALU.mult))
                mc = mods[:, 4 * l:4 * l + 4].rearrange("p (a b) -> p a b", b=2)[:, :, 1]
                ins = vec.tensor_scalar(mc, mc, 1.0, None, ALU.add)
                if l == 0:
                    link(ins)
                    vec.wait_ge(s["ld_small"], 16 * NSM)
                    vec.tensor_tensor(diag_ga[:, :], ident[:, :], gates[:, 0, :], ALU.mult).then_inc(s["set_dve"], 1)
                else:
                    link(ins)
                    vec.tensor_tensor(bias_row[:, :], bias_row[:, :], gates[:, 3, :], ALU.mult).then_inc(s["set_dve"], 1)

            for c in range(NC):
                vec.wait_ge(ld_x[c], 16)
                ln_stats(c)
                ln_apply(c)
                if c:
                    vec.wait_ge(s["ln_evac"], c)
                    vec.bn_stats(gn_st[:, c - 1, :], hT[:, c - 1, :])
            vec.wait_ge(s["ln_evac"], NC)
            link(vec.bn_stats(gn_st[:, NC - 1, :], hT[:, NC - 1, :]))
            gn(0, "norm_g", "norm_b")

            for c in range(NC):
                vec.wait_ge(s["att_nr"], c + 1)
                link(vec.tensor_scalar(nrm[:, :], nrm[:, :], 1e-12, None, ALU.max))
                link(vec.reciprocal(rnm[:, :], nrm[:, :]))
                vec.tensor_scalar(rnm[:, 0:NJ], rnm[:, 0:NJ], float(1.0 / np.sqrt(DH)), None, ALU.mult).then_inc(s["att_r"], 1)
                vec.wait_ge(s["att_qkv"], 3 * c + 3)
                vec.wait_ge(s["att_rbs"], 2 * c + 2)
                link(vec.tensor_tensor(vp[:, :], pB[:, :], rb[:, 1, :], ALU.mult))
                for i in range(DH):
                    n = DH * c + i
                    vec.wait_ge(s["att_kb"], n + 1)
                    sig(vec.tensor_tensor(U[:, i % 2, :], pH[i % 2][:, :], vp[:, :], ALU.mult), "att_u", n + 1)
                    link(vec.tensor_tensor_scan(S[:, i, :], col("gamma").to_broadcast([P, TC]), U[:, i % 2, :],
                                                S[:, i, TC - 1:TC] if c else 0.0, ALU.mult, ALU.add))
                    vec.wait_ge(s["att_qb"], n + 1)
                    if n >= 2:
                        vec.wait_ge(s["att_ow"], n - 1)
                    vec.tensor_tensor(ZA[:, i % 2, :], [pC, pT][i % 2][:, :], S[:, i, :], ALU.mult).then_inc(s["att_z"], 1)
                vec.wait_ge(s["att_ow"], DH * (c + 1))
                link(vec.tensor_tensor(att_t[:, :], pO[:, :], rb[:, 0, :], ALU.mult))
                sig(vec.scalar_tensor_tensor(hT[:, c, :], att_t[:, :], col("ob"), hT[:, c, :], ALU.add, ALU.add),
                    "att_x2", c + 1)
                link(vec.bn_stats(gn_st[:, c, :], hT[:, c, :]))
            gn(1, "ffn_g", "ffn_b")

            def ffn_x1(c):
                vec.wait_ge(s["ffn_tok"], c + 1)
                Xc = X[:, c * NJ:(c + 1) * NJ, :]
                sig(vec.tensor_tensor(Xc, Xc, j4([pB, pC][c % 2][:, :]), ALU.add), "ffn_x1", c + 1)

            for c in range(NC):
                vec.wait_ge(s["ffn_o"], c + 1)
                if c >= 2:
                    vec.wait_ge(s["ffn_tok"], c - 1)
                vec.scalar_tensor_tensor(x3T[:, c % 2, :], pY[c % 2][:, :], col("b2"), hT[:, c, :], ALU.add,
                                         ALU.add).then_inc(s["ffn_x3"], 1)
                if c:
                    ffn_x1(c - 1)
            ffn_x1(NC - 1)

            def route(c):
                vec.wait_ge(s["moe_rt"], c + 1)
                logits = pT[:, 0:NJ * E].rearrange("p (j e) -> p j e", j=NJ)
                mx, sm, rs = (s4[:, k, :] for k in range(3))

                def over(v):
                    return v[:, :, None].to_broadcast([P, NJ, E])
                link(vec.tensor_reduce(mx, logits, AX.X, ALU.max))
                vec.tensor_tensor(lg[:, :, :], logits, over(mx), ALU.subtract).then_inc(s["moe_lg"], 1)
                vec.wait_ge(s["moe_ex"], c + 1)
                link(vec.tensor_reduce(sm, ex[:, :, :], AX.X, ALU.add))
                link(vec.reciprocal(rs, sm))
                link(vec.tensor_tensor(pr[:, :, :], ex[:, :, :], over(rs), ALU.mult))
                flat = pr[:, :, :].rearrange("p j e -> p (j e)")
                mine = flat[:, :, None].to_broadcast([P, NJ * E, E])
                for j in range(NJ):
                    rows = slice(j * E, (j + 1) * E)
                    others = pr[:, j:j + 1, :].to_broadcast([P, E, E])
                    vec.tensor_tensor(cmp_[:, 0, rows, :], others, mine[:, rows, :], ALU.is_gt)
                    link(vec.tensor_tensor(cmp_[:, 1, rows, :], others, mine[:, rows, :], ALU.is_equal))
                    link(vec.tensor_tensor(cmp_[:, 1, rows, :], cmp_[:, 1, rows, :], tie[:, :, :], ALU.mult))
                link(vec.tensor_tensor(cmp_[:, 0, :, :], cmp_[:, 0, :, :], cmp_[:, 1, :, :], ALU.add))
                link(vec.tensor_reduce(rank[:, :, :].rearrange("p j e -> p (j e)"), cmp_[:, 0, :, :], AX.X, ALU.add))
                sig(vec.scalar_tensor_tensor(wts[:, c % 2, 0:NJ * E], rank[:, :, :].rearrange("p j e -> p (j e)"), 2.0, flat,
                                             ALU.is_lt, ALU.mult), "moe_w", c + 1)

            def weigh(c):
                vec.wait_ge(s["moe_bias"], c + 1)
                Xc = X[:, c * NJ:(c + 1) * NJ, :]
                sig(vec.tensor_tensor(Xc, Xc, j4(pT[:, :]), ALU.add), "moe_xb", c + 1)

            def moe_acc(g):
                c, e = divmod(g, E)
                vec.wait_ge(s["moe_g2"], NK * (g + 1))
                for j in range(NJ):
                    Xj = X[:, c * NJ + j, :]
                    ins = vec.scalar_tensor_tensor(Xj, pO[:, j * P:(j + 1) * P], wts[:, c % 2, j * E + e:j * E + e + 1], Xj,
                                                   ALU.mult, ALU.add)
                sig(ins, "moe_acc", g + 1)

            def conv(c):
                vec.wait_ge(s["mam_xr"], 2 * c + 2)
                for k in range(TAPS):
                    for d in range(ND):
                        w = col(f"conv_w{d}{k}")
                        if k == 0:
                            ins = vec.tensor_scalar(cv[:, d, :], xr[:, d, 0:TC], w, col(f"conv_b{d}"), ALU.mult, ALU.add)
                        else:
                            ins = vec.scalar_tensor_tensor(cv[:, d, :], xr[:, d, k:k + TC], w, cv[:, d, :], ALU.mult, ALU.add)
                    if k < TAPS - 1:
                        link(ins)
                sig(ins, "mam_cv", c + 1)
                if c + 1 < NC:
                    vec.tensor_copy(xr[:, :, 0:TAPS - 1], xr[:, :, TC:TC + TAPS - 1]).then_inc(s["mam_hist"], 1)

            def step(c):
                d_ = half_of(dt, c)
                vec.wait_ge(s["mam_w"], c + 1)
                link(vec.scalar_tensor_tensor(wx[:, :, :], wx[:, :, :], -1.0, exd[:, :, :], ALU.add, ALU.subtract))
                vec.wait_ge(s["mam_ln"], c + 1)
                link(vec.scalar_tensor_tensor(d_, d_, 0.0, lnd[:, :, :], ALU.max, ALU.add))
                sig(vec.tensor_tensor(d_, d_, wx[:, :, :], ALU.subtract), "mam_dt", c + 1)
                vec.wait_ge(s["mam_xc"], 2 * c + 2)
                sig(vec.tensor_tensor(half_of(u, c), d_, xc[:, :, :], ALU.mult), "mam_u", c + 1)

            def half(p, o):
                c, k = divmod(p, NP)
                m = 2 * p + o
                n = 2 * k + o
                if p >= 0 and o == 0:
                    vec.wait_ge(s["mam_bB"], m + 2)
                    sig(vec.tensor_tensor(UB[:, :, :], half_of(u, c), pB[:, None, :].to_broadcast([P, ND, TC]), ALU.mult),
                        "mam_ub", p + 1)
                if o == 0 and 0 <= p + AHEAD - 2 < NC * E:
                    moe_acc(p + AHEAD - 2)
                if p < 0:
                    return
                vec.wait_ge(s["mam_dA"], 2 * ND * (p + 1))
                if o:
                    vec.wait_ge(s["mam_uo"], p + 1)
                    if p:
                        vec.wait_ge(s["mam_zo"], p)
                for d in range(ND):
                    r = 2 * o + d
                    in_ = UBo[:, 2 * (p % 2) + d, :] if o else UB[:, d, :]
                    ins = vec.tensor_tensor_scan(Hs[:, r, :], dA[:, 4 * (p % 2) + r, :], in_,
                                                 HL[:, d, n:n + 1] if c else 0.0, ALU.mult, ALU.add)
                sig(ins, "mam_sc", m + 1)
                if c + 1 < NC:
                    vec.tensor_copy(HL[:, :, n:n + 1], Hs[:, 2 * o:2 * o + 2, TC - 1:TC])
                if o == 0:
                    vec.wait_ge(s["mam_bC"], m + 1)
                    if p >= 2:
                        vec.wait_ge(s["mam_zs"], p - 1)
                    z = Zev[:, 2 * (p % 2):2 * (p % 2) + 2, :]
                    sig(vec.tensor_tensor(z, Hs[:, 0:2, :], pC[:, None, :].to_broadcast([P, ND, TC]), ALU.mult),
                        "mam_z", p + 1)

            def gate(c):
                vec.wait_ge(s["mam_y"], NS // 2 * (c + 1))
                for d in range(ND):
                    vec.tensor_tensor(y2[:, d, :], pY[d][:, :], half_of(gz, c)[:, d, :], ALU.mult).then_inc(s["mam_y2"], 1)

            def project(c):
                vec.wait_ge(s["mam_o"], c + 1)
                Xc = X[:, c * NJ:(c + 1) * NJ, :]
                sig(vec.tensor_tensor(Xc, Xc, j4(pT[:, :]), ALU.add), "mam_x", c + 1)

            def fft(c):
                vec.wait_ge(s["fft_b"], c + 1)
                vec.wait_ge(s["fft_o"], c + 1)
                if c >= 2:
                    vec.wait_ge(s[f"out_done{c % 2}"], 16 * (c // 2))
                sig(vec.tensor_tensor(outb[:, c % 2, :, :], j4(pT[:, :]), XB[:, :, :], ALU.add), "fft_x", c + 1)

            vec.wait_ge(s["fr_mm"], 2)
            vec.tensor_copy(g_freq[:, 0, :], pH0[:, 0:P]).then_inc(s["fr_sb"], 1)
            vec.tensor_copy(g_freq[:, 1, :], pH1[:, 0:P]).then_inc(s["fr_sb"], 1)
            vec.wait_ge(s["exp_A"], 1)
            vec.tensor_scalar(a_neg[:, :, :], a_neg[:, :, :], -1.0, None, ALU.mult)
            vec.wait_ge(s["fft_mm"], 1)
            link(vec.scalar_tensor_tensor(w_fft[:, :], pH0[:, 0:P], 1.0 / D, gates[:, 3, :], ALU.mult, ALU.mult))

            vec.memset(xr[:, :, 0:TAPS - 1], 0.0).then_inc(s["mam_hist"], 1)
            for stage, c, *k in later_stages():
                if stage == "ln_stats":
                    ln_stats(c)
                elif stage == "ln_apply":
                    ln_apply(c)
                elif stage == "half":
                    half(c, *k)
                elif stage == "dt_part":
                    conv(c)
                elif stage in ("route", "weigh", "step", "gate", "project", "fft"):
                    {"route": route, "weigh": weigh, "step": step, "gate": gate, "project": project,
                     "fft": fft}[stage](c)

        @block.scalar
        def _(act):
            chain = [0]
            L = [0]

            def link(ins):
                ins.then_inc(s["act_chain"], 1)
                chain[0] += 1
                act.wait_ge(s["act_chain"], chain[0])

            act.dma_start(w_mod[:, 0, :], a["w_mod0"]).then_inc(s["ld_small"], 16)
            act.dma_start(group_avg[:, :], a["group_avg"]).then_inc(s["ld_small"], 16)
            act.dma_start(bias_row[:, :], a["fft_bias"].to_broadcast([P, P])).then_inc(s["ld_small"], 16)
            act.dma_start(w_mod[:, 1, :], a["w_mod1"]).then_inc(s["ld_small"], 16)
            act.wait_ge(s["ld_small"], 16 * NSM)
            nc.scalar.activation(silu_c[:, :], cols[:, COL["c0"]:COL["c0"] + 2], ACT.Silu).then_inc(s["silu_c_ready"], 1)

            def ln(dest, m):
                act.wait_ge(s["ln_tr"], L[0] + 1)
                nc.scalar.activation(dest, pT[:, :], ACT.Identity, bias=mods[:, m:m + 1],
                                     scale=mods[:, m + 1:m + 2]).then_inc(s["ln_evac"], 1)
                L[0] += 1

            act.wait_ge(s["set_dve"], 2)
            for c in range(NC):
                ln(hT[:, c, :], 0)

            def xn_of(k, c):
                act.wait_ge(s["gn_ready"], k + 1)
                if c >= 2:
                    act.wait_ge(s["att_kb" if k == 0 else "ffn_h"], (DH if k == 0 else 2) * (c - 1))
                    if k == 0:
                        act.wait_ge(s["att_qb"], DH * (c - 1))
                nc.scalar.activation(xn[:, c % 2, :], hT[:, c, :], ACT.Identity, bias=gn_sb[:, 1:2],
                                     scale=gn_sb[:, 0:1]).then_inc(s["xn_ready"], 1)

            xn_of(0, 0)
            for c in range(NC):
                if c + 1 < NC:
                    xn_of(0, c + 1)
                for k in range(2):
                    act.wait_ge(s["att_qkv"], 3 * c + k + 1)
                    nc.scalar.activation(q2[:, k, :], pY[k][:, :], ACT.Square).then_inc(s["att_sq"], 1)
                act.wait_ge(s["att_ss"], c + 1)
                nc.scalar.activation(nrm[:, :], pC[:, 0:2 * NJ], ACT.Sqrt).then_inc(s["att_nr"], 1)
                act.wait_ge(s["att_rb"], c + 1)
                for k in range(2):
                    nc.scalar.copy(rb[:, k, :], pY[k][:, :]).then_inc(s["att_rbs"], 1)

            xn_of(1, 0)
            for c in range(NC):
                if c + 1 < NC:
                    xn_of(1, c + 1)
                for m in range(2):
                    act.wait_ge(s["ffn_h"], 2 * c + m + 1)
                    if c >= 2:
                        act.wait_ge(s["ffn_o"], c - 1)
                    nc.scalar.activation(h1[:, 2 * (c % 2) + m, :], pH[m][:, :], ACT.Silu,
                                         bias=col(f"b1_{m}")).then_inc(s["ffn_silu"], 1)

            def route(c):
                act.wait_ge(s["moe_lg"], c + 1)
                nc.scalar.activation(ex[:, :, :], lg[:, :, :], ACT.Exp).then_inc(s["moe_ex"], 1)

            def turn(c):
                act.wait_ge(s["moe_wt"], c + 1)
                nc.scalar.copy(wT[:, :], pT[:, P:2 * P]).then_inc(s["moe_wts"], 1)

            def x_part(c):
                act.wait_ge(s["mam_hist"], c + 1)
                for d in range(ND):
                    act.wait_ge(s["mam_xz"], 4 * c + d + 1)
                    nc.scalar.copy(xr[:, d, TAPS - 1:TC + TAPS - 1], pH[d][:, :]).then_inc(s["mam_xr"], 1)

            def rows(c):
                act.wait_ge(s["mam_bc"], c + 1)
                if c:
                    act.wait_ge(s["mam_st"], c)
                nc.scalar.copy(BCf[:, :], pT[0:96, :]).then_inc(s["mam_bcs"], 1)
                act.wait_ge(s["mam_bcs"], c + 1)
                nc.scalar.copy(ST[:, c % 2, :], BCf[:, :]).then_inc(s["mam_st0"], 1)

            def dt_part(c):
                v_ = half_of(dt, c)
                for d in range(ND):
                    act.wait_ge(s["mam_dtp"], 2 * c + d + 1)
                    nc.scalar.activation(v_[:, d, :], pH[d][:, :], ACT.Identity,
                                         bias=col(f"b_dt{d}")).then_inc(s["mam_v"], 1)

            def z_part(c):
                for d in range(ND):
                    act.wait_ge(s["mam_xz"], 4 * c + 3 + d)
                    nc.scalar.activation(half_of(gz, c)[:, d, :], pH[d][:, :], ACT.Silu).then_inc(s["mam_gz"], 1)
                act.wait_ge(s["mam_cv"], c + 1)
                for d in range(ND):
                    nc.scalar.activation(xc[:, d, :], cv[:, d, :], ACT.Silu).then_inc(s["mam_xc"], 1)
                act.wait_ge(s["mam_v"], 2 * c + 2)
                nc.scalar.activation(exd[:, :, :], half_of(dt, c), ACT.Abs).then_inc(s["mam_ab"], 1)

            def step(c):
                act.wait_ge(s["mam_ab"], c + 1)
                nc.scalar.activation(exd[:, :, :], exd[:, :, :], ACT.Exp, scale=-1.0).then_inc(s["mam_ex"], 1)
                act.wait_ge(s["mam_ex"], c + 1)
                nc.scalar.activation(wx[:, :, :], exd[:, :, :], ACT.Identity, bias=1.0).then_inc(s["mam_w"], 1)
                nc.scalar.activation(lnd[:, :, :], exd[:, :, :], ACT.Ln, bias=1.0).then_inc(s["mam_ln"], 1)

            def hidden(g, ks):
                for k in ks:
                    n = NK * g + k
                    e = g % E
                    act.wait_ge(s["moe_h"], n + 1)
                    if n >= 2 * NK:
                        act.wait_ge(s["moe_g2"], n - 2 * NK + 1)
                    nc.scalar.activation(gel[:, n % (2 * NK), :], pH[n % 2][:, :], ACT.Gelu_apprx_tanh,
                                         bias=b_e1[:, NK * e + k:NK * e + k + 1]).then_inc(s["moe_g"], 1)

            def decays(p):
                c, k = divmod(p, NP)
                if k == 0:
                    act.wait_ge(s["mam_dt"], c + 1)
                if p >= 2:
                    act.wait_ge(s["mam_sc"], 2 * (p - 1))
                for r in range(4):
                    n = 2 * k + r // 2
                    nc.scalar.activation(dA[:, 4 * (p % 2) + r, :], half_of(dt, c)[:, r % 2, :], ACT.Exp,
                                         scale=a_neg[:, r % 2, n:n + 1]).then_inc(s["mam_dA"], 1)

            def odd_row(p):
                act.wait_ge(s["mam_bC"], 2 * p + 2)
                if p >= 2:
                    act.wait_ge(s["mam_zo"], p - 1)
                nc.scalar.copy(Csb[:, p % 2, :], pC[:, :]).then_inc(s["mam_Cs"], 1)

            def odd_input_row(p):
                act.wait_ge(s["mam_bB"], 2 * p + 1)
                if p >= 2:
                    act.wait_ge(s["mam_uo"], p - 1)
                nc.scalar.copy(Bsb[:, p % 2, :], pB[:, :]).then_inc(s["mam_Bs"], 1)

            def half(p, o):
                nxt = p + 1 if 0 <= p + 1 < NC * NP else None
                if p + AHEAD < NC * E:
                    hidden(p + AHEAD, (2 * o, 2 * o + 1))
                if o == 0:
                    if nxt is not None:
                        if nxt % NP == 0:
                            step(nxt // NP)
                        odd_input_row(nxt)
                        if nxt % NP:
                            decays(nxt)
                    if p >= 0:
                        odd_row(p)
                elif nxt is not None and nxt % NP == 0:
                    decays(nxt)

            act.wait_ge(s["ld_mam"], 16 * NMA)
            nc.scalar.activation(a_neg[:, :, :], a_neg[:, :, :], ACT.Exp).then_inc(s["exp_A"], 1)
            for stage, c, *k in later_stages():
                if stage == "ln_apply":
                    ln([h2T[:, c % 2, :], h3T[:, :], h4T[:, :]][k[0]], 2 + 2 * k[0])
                elif stage == "half":
                    half(c, *k)
                elif stage in ("route", "turn", "x_part", "rows", "dt_part", "z_part"):
                    {"route": route, "turn": turn, "x_part": x_part, "rows": rows, "dt_part": dt_part,
                     "z_part": z_part}[stage](c)

        @block.tensor
        def _(pe):
            mm = nc.tensor.matmul
            L = [0]
            L3 = [0]
            held = {}

            def use(bank, free, count):
                if bank in held:
                    pe.wait_ge(s[held[bank][0]], held[bank][1])
                held[bank] = (free, count)

            def ln():
                use("pT", "ln_evac", L[0] + 1)
                pe.wait_ge(s["ln_xn"], NJ * (L[0] + 1))
                for j in range(NJ):
                    ins = nc.tensor.transpose(pT[:, j * P:(j + 1) * P], ln_x[:, j, :], ident[:, :])
                ins.then_inc(s["ln_tr"], 1)
                L[0] += 1

            def gn(g):
                pe.wait_ge(s["gn_m"], g + 1)
                mm(pO[:, 0:2], group_avg[:, :], gn_me[:, :], start=True, stop=True).then_inc(s["gn_mm"], 1)

            pe.wait_ge(s["ld_small"], 16 * NSM)
            pe.wait_ge(s["set_cb"], 2)
            for l in range(2):
                def wm(k):
                    return w_mod[:, l, k * P:(k + 1) * P]
                if l:
                    pe.wait_ge(s["set_dve"], 1)
                for i, k in enumerate((0, 1, 3, 4)):
                    mm(pT[:, i:i + 1], wm(k), silu_c[:, l:l + 1], start=True, stop=True)
                for i, k in enumerate((2, 5)):
                    ins = mm(pO[:, i * P:(i + 1) * P], silu_cb[:, l, :], wm(k), start=True, stop=True)
                    ins.then_inc(s["mod_mm"], 1)
            pe.wait_ge(s["set_dve"], 2)
            for c in range(NC):
                ln()
            gn(0)
            pe.wait_ge(s["ld_attn"], 16 * NAT)
            pe.wait_ge(s["set_pool"], 1)
            for c in range(NC):
                x_ = xn[:, c % 2, :]
                pe.wait_ge(s["xn_ready"], c + 1)
                if c:
                    pe.wait_ge(s["att_x2"], c)
                for k, bank in enumerate((pY0, pY1, pB)):
                    mm(bank[:, :], w_qkv[:, k, :], x_, start=True, stop=True).then_inc(s["att_qkv"], 1)
                pe.wait_ge(s["att_sq"], 2 * c + 2)
                for k in range(2):
                    for j in range(NJ):
                        ins = mm(pC[:, k * NJ + j:k * NJ + j + 1], q2[:, k, j * P:(j + 1) * P], ones[:, 0:1],
                                 start=True, stop=True)
                ins.then_inc(s["att_ss"], 1)
                pe.wait_ge(s["att_r"], c + 1)
                for k in range(2):
                    for j in range(NJ):
                        r = rnm[:, k * NJ + j:k * NJ + j + 1].to_broadcast([P, P])
                        ins = mm(pY[k][:, j * P:(j + 1) * P], r, ident[:, :], start=True, stop=True)
                ins.then_inc(s["att_rb"], 1)

                def project(i):
                    n = DH * c + i
                    pe.wait_ge(s["att_z"], n)
                    mm(pO[:, :], w_o[:, :], ZA[:, (i - 1) % 2, :], start=(i == 1), stop=(i == DH)).then_inc(s["att_ow"], 1)

                for i in range(DH):
                    n = DH * c + i
                    if n >= 2:
                        pe.wait_ge(s["att_u"], n - 1)
                    mm(pH[i % 2][:, :], w_kq_rep[:, 0, i, :], x_, start=True, stop=True).then_inc(s["att_kb"], 1)
                    if n >= 2:
                        pe.wait_ge(s["att_z"], n - 1)
                    mm([pC, pT][i % 2][:, :], w_kq_rep[:, 1, i, :], x_, start=True, stop=True).then_inc(s["att_qb"], 1)
                    if i:
                        project(i)
                project(DH)
            gn(1)
            pe.wait_ge(s["ld_ffn"], 16 * NFF)

            def ffn_tok(c):
                pe.wait_ge(s["ffn_x3"], c + 1)
                if c >= 2:
                    pe.wait_ge(s["ffn_x1"], c - 1)
                for j in range(NJ):
                    ins = mm([pB, pC][c % 2][:, j * P:(j + 1) * P], x3T[:, c % 2, j * P:(j + 1) * P], diag_ga[:, :],
                             start=True, stop=True)
                ins.then_inc(s["ffn_tok"], 1)

            for c in range(NC):
                pe.wait_ge(s["xn_ready"], NC + c + 1)
                for m in range(2):
                    if c:
                        pe.wait_ge(s["ffn_silu"], 2 * c + m - 1)
                    mm(pH[m][:, :], w_f1[:, m, :], xn[:, c % 2, :], start=True, stop=True).then_inc(s["ffn_h"], 1)
                if c:
                    ffn_tok(c - 1)
                for m in range(2):
                    pe.wait_ge(s["ffn_silu"], 2 * c + m + 1)
                    if m == 0 and c >= 2:
                        pe.wait_ge(s["ffn_x3"], c - 1)
                    ins = mm(pY[c % 2][:, :], w_f2[:, m, :], h1[:, 2 * (c % 2) + m, :], start=(m == 0), stop=(m == 1))
                ins.then_inc(s["ffn_o"], 1)
            ffn_tok(NC - 1)

            pe.wait_ge(s["ld_mam"], 16 * NMA)
            pe.wait_ge(s["ffn_silu"], 2 * NC)
            for k in range(2):
                mm(pH[k][:, 0:P], w_freq[:, k, :], dft[:, 0, :], start=True, stop=False)
                mm(pH[k][:, 0:P], w_freq[:, 1 - k, :], dft[:, 1 + k, :], start=False, stop=True).then_inc(s["fr_mm"], 1)
            pe.wait_ge(s["fr_sb"], 2)
            mm(pH0[:, 0:P], g_freq[:, 0, :], dft[:, 0, :], start=True, stop=False)
            mm(pH0[:, 0:P], g_freq[:, 1, :], dft[:, 2, :], start=False, stop=True).then_inc(s["fft_mm"], 1)

            def route(c):
                pe.wait_ge(s["ln_evac"], L[0])
                if c == 0:
                    pe.wait_ge(s["set_pool"], 5)
                    pe.wait_ge(s["ld_moe"], 16 * NMO)
                h = h2T[:, c % 2, :]
                use("pT", "moe_w", c + 1)
                for j in range(NJ):
                    ins = mm(pT[:, j * E:(j + 1) * E], h[:, j * P:(j + 1) * P], w_router[:, :], start=True, stop=True)
                ins.then_inc(s["moe_rt"], 1)

            def turn(c):
                use("pT", "moe_wts", c + 1)
                nc.tensor.transpose(pT[:, P:2 * P], wts[:, c % 2, :], ident[:, :]).then_inc(s["moe_wt"], 1)

            def weigh(c):
                use("pT", "moe_xb", c + 1)
                for j in range(NJ):
                    ins = mm(pT[:, j * P:(j + 1) * P], wT[:, :], b_e2[:, j, :], start=True, stop=True)
                ins.then_inc(s["moe_bias"], 1)

            def up(g, k):
                n = NK * g + k
                use(n % 2, "moe_g", n + 1)
                mm(pH[n % 2][:, :], w_e1[:, g % E, k * P:(k + 1) * P], h2T[:, g // E % 2, :],
                   start=True, stop=True).then_inc(s["moe_h"], 1)

            def down(g, k):
                n = NK * g + k
                if k == 0 and g:
                    pe.wait_ge(s["moe_acc"], g)
                pe.wait_ge(s["moe_g"], n + 1)
                for j in range(NJ):
                    ins = mm(pO[:, j * P:(j + 1) * P], gel[:, n % (2 * NK), j * P:(j + 1) * P], w_e2[:, NK * (g % E) + k, :],
                             start=(k == 0 and j == 0), stop=(k == NK - 1 and j == NJ - 1), skip_group_check=True)
                ins.then_inc(s["moe_g2"], 1)

            def half(p, o):
                g = p + AHEAD
                if g < NC * E:
                    up(g, 2 * o)
                    up(g, 2 * o + 1)
                if 0 <= p + 1 < NC * NP:
                    row_b(p + 1, 1 - o)
                    if o == 1:
                        row_c(2 * p + 2)
                if 0 < g <= NC * E:
                    down(g - 1, 2 * o)
                if o == 0 and p > 0:
                    total(p - 1)
                if o == 0 and p >= 0:
                    row_c(2 * p + 1)
                if 0 < g <= NC * E:
                    down(g - 1, 2 * o + 1)

            def x_part(c):
                pe.wait_ge(s["ln_evac"], L3[0])
                for d in range(ND):
                    use(d, "mam_xr", 2 * c + d + 1)
                    mm(pH[d][:, :], w_in[:, d, :], h3T[:, :], start=True, stop=True).then_inc(s["mam_xz"], 1)

            def rows(c):
                use("pT", "mam_bcs", c + 1)
                mm(pT[0:96, :], w_bc[:, :], h3T[:, :], start=True, stop=True).then_inc(s["mam_bc"], 1)

            def dt_part(c):
                for d in range(ND):
                    use(d, "mam_v", 2 * c + d + 1)
                    mm(pH[d][:, :], w_dt[:, d, :], h3T[:, :], start=True, stop=True).then_inc(s["mam_dtp"], 1)

            def z_part(c):
                for d in range(ND):
                    use(d, "mam_gz", 2 * c + d + 1)
                    mm(pH[d][:, :], w_in[:, ND + d, :], h3T[:, :], start=True, stop=True).then_inc(s["mam_xz"], 1)

            def row_b(p, o):
                c, k = divmod(p, NP)
                if o:
                    if k == 0:
                        pe.wait_ge(s["mam_st"], c + 1)
                    if p:
                        pe.wait_ge(s["mam_ub"], p)
                else:
                    pe.wait_ge(s["mam_Bs"], p + 1)
                mm(pB[:, :], sel[:, 2 * k + o, :], ST[:, c % 2, :], start=True, stop=True).then_inc(s["mam_bB"], 1)

            def row_c(m):
                c, n = divmod(m, NS)
                if n % 2:
                    pe.wait_ge(s["mam_z"], (m + 1) // 2)
                elif m:
                    pe.wait_ge(s["mam_Cs"], m // 2)
                mm(pC[:, :], sel[:, NS + n, :], ST[:, c % 2, :], start=True, stop=True).then_inc(s["mam_bC"], 1)

            def total(p):
                c, k = divmod(p, NP)
                if k == 0 and c:
                    pe.wait_ge(s["mam_y2"], 2 * c)
                pe.wait_ge(s["mam_zs"], p + 1)
                for d in range(ND):
                    ins = mm(pY[d][:, :], ident[:, :], ZS[:, 2 * (p % 2) + d, :], start=(k == 0), stop=(k == NP - 1))
                ins.then_inc(s["mam_y"], 1)

            def project(c):
                pe.wait_ge(s["mam_y2"], 2 * c + 2)
                use("pT", "mam_x", c + 1)
                for j in range(NJ):
                    for d in range(ND):
                        ins = mm(pT[:, j * P:(j + 1) * P], y2[:, d, j * P:(j + 1) * P], w_out[:, d, :],
                                 start=(d == 0), stop=(d == 1))
                ins.then_inc(s["mam_o"], 1)

            def fft(c):
                use("pT", "fft_x", c + 1)
                for j in range(NJ):
                    ins = mm(pT[:, j * P:(j + 1) * P], h4T[:, j * P:(j + 1) * P], w_fft[:, :], start=True, stop=True)
                ins.then_inc(s["fft_o"], 1)

            for stage, c, *k in later_stages():
                if stage == "ln_apply":
                    ln()
                    if k[0] == 1:
                        L3[0] = L[0]
                elif stage == "half":
                    half(c, *k)
                elif stage in ("route", "turn", "weigh", "x_part", "rows", "dt_part", "z_part", "total", "project", "fft"):
                    {"route": route, "turn": turn, "weigh": weigh, "x_part": x_part, "rows": rows, "dt_part": dt_part,
                     "z_part": z_part, "total": total, "project": project, "fft": fft}[stage](c)


def constants():
    n = np.arange(D)
    turn = 2 * np.pi * (np.outer(n, n) % D) / D
    dft = np.stack([np.cos(turn), np.sin(turn), -np.sin(turn)], 1).astype(np.float32)
    group = (n[:, None] // DH == n[None, :] // DH).astype(np.float32) / DH
    tie = np.broadcast_to((np.arange(E)[None, :] < np.arange(E)[:, None]).astype(np.float32), (P, E, E))
    m = np.arange(96) % 32
    part_row = (m[:, None] == np.arange(2 * NS)[None, :]).astype(np.float32)
    gam = np.float32(1.0) - np.exp(np.linspace(np.log(1 / 32), np.log(1 / 512), HEADS).astype(np.float32))
    return {"dft": dft, "group_avg": group, "tie": np.ascontiguousarray(tie), "part_row": part_row,
            "ident": np.eye(P, dtype=np.float32), "gamma": np.repeat(gam.astype(np.float32), DH)}


def kernel(**inputs):
    import concourse.bacc as bacc
    from concourse.bass_utils import run_bass_kernel_spmd

    v = {k: np.asarray(x) for k, x in inputs.items()}
    k = constants()

    def tiles(w, n):
        return w.reshape(w.shape[0], n, -1)

    def rows(w, n):
        return w.reshape(n, P, -1).transpose(1, 0, 2)

    qT, kT, vT = (v[f"L0_attn_{n}w"].T for n in "qkv")
    rep = [np.repeat(w.reshape(D, HEADS, DH).transpose(0, 2, 1), DH, axis=2) for w in (kT, qT)]
    cols = {
        "norm_g": v["L0_attn_norm_g"], "norm_b": v["L0_attn_norm_b"], "ob": v["L0_attn_ob"],
        "ffn_g": v["L0_attn_ffn_norm_g"], "ffn_b": v["L0_attn_ffn_norm_b"],
        "b1_0": v["L0_attn_b1"][:P], "b1_1": v["L0_attn_b1"][P:], "b2": v["L0_attn_b2"],
        "conv_b0": v["L1_attn_conv_b"][:P], "conv_b1": v["L1_attn_conv_b"][P:],
        "b_dt0": v["L1_attn_b_dt"][:P], "b_dt1": v["L1_attn_b_dt"][P:],
        "c0": v["L0_c"][0], "c1": v["L1_c"][0], "gamma": k["gamma"],
    }
    for d in range(ND):
        for t in range(TAPS):
            cols[f"conv_w{d}{t}"] = v["L1_attn_conv_w"][d * P:(d + 1) * P, 0, t]
    w_dt = np.zeros((P, DI), np.float32)
    w_dt[:RANK] = v["L1_attn_W_dt"].T
    b_e2 = np.zeros((P, NJ, P), np.float32)
    for j in range(NJ):
        b_e2[j * E:(j + 1) * E, j] = v["L0_ffn_b2"]
    bc = np.concatenate([v["L1_attn_W_B"], v["L1_attn_W_C"]], 0).T
    arrays = {
        "x": v["L0_attn_x"][0], "cols": np.stack([cols[n] for n in COLS], 1), "ident": k["ident"],
        "group_avg": k["group_avg"], "dft": k["dft"], "tie": k["tie"], "part_row": k["part_row"],
        "w_qkv": np.stack([qT, kT, vT], 1), "w_kq_rep": np.stack(rep, 1), "w_o": v["L0_attn_ow"].T,
        "w_f1": tiles(v["L0_attn_w1"].T, 2), "w_f2": rows(v["L0_attn_w2"].T, 2),
        "w_router": v["L0_ffn_w_router"], "w_e1": v["L0_ffn_w1"].transpose(1, 0, 2),
        "w_e2": v["L0_ffn_w2"].reshape(E * NK, P, D).transpose(1, 0, 2),
        "b_e1": v["L0_ffn_b1"].reshape(E * NK, P).T, "b_e2": b_e2,
        "w_mod0": v["L0_wmod"], "w_mod1": v["L1_wmod"],
        "w_in": tiles(v["L1_attn_W_in"].T, 4), "w_dt": tiles(w_dt, ND),
        "w_bc": np.concatenate([bc, bc, bc], 1), "w_out": rows(v["L1_attn_W_out"].T, ND),
        "a_log": rows(v["L1_attn_A_log"], ND),
        "w_freq": np.stack([v["L1_ffn_w_freq_real"], v["L1_ffn_w_freq_imag"]], 1),
        "fft_bias": v["L1_ffn_bias"][None],
    }
    arrays = {n: np.ascontiguousarray(x) for n, x in arrays.items()}
    nc = bacc.Bacc("TRN2", target_bir_lowering=False, num_devices=1)
    aps = {n: nc.dram_tensor(f"in_{n}", x.shape, mybir.dt.from_np(x.dtype), kind="ExternalInput").ap()
           for n, x in arrays.items()}
    out = nc.dram_tensor("out_0", (T, D), F32, kind="ExternalOutput").ap()
    build(nc, aps, out)
    r = run_bass_kernel_spmd(nc, [{f"in_{n}": x for n, x in arrays.items()}], core_ids=[0])
    return r.results[0]["out_0"].reshape(1, T, D)
```

```python
from contextlib import ExitStack

import numpy as np

import concourse.bass as bass
from concourse import mybir

ALU = mybir.AluOpType
ACT = mybir.ActivationFunctionType
AX = mybir.AxisListType
F32 = mybir.dt.float32
F32R = mybir.dt.float32r
BF16 = mybir.dt.bfloat16

P = 128
T = 2048
D = 128
TC = 512
NC = T // TC
NJ = TC // P
HEADS = 16
DH = D // HEADS
E = 8
HID = 512
NK = HID // P
NG = 6
NS = 16
DI = 256
ND = DI // P
TAPS = 4
RANK = 64
EPS = 1e-5
NP = NS // 2
NR = DH // 2
AHEAD = 12

COLS = ["norm_g", "norm_b", "ob", "ffn_g", "ffn_b", "b1_0", "b1_1", "b2", "conv_b0", "conv_b1",
        "b_dt0", "b_dt1", "c0", "c1", "gamma"] + [f"conv_w{d}{k}" for d in range(ND) for k in range(TAPS)]
COL = {n: i for i, n in enumerate(COLS)}


def build(nc, a, out):
    ctx = ExitStack()
    with ctx:
        def sb(name, shape, dt=F32):
            return ctx.enter_context(nc.sbuf_tensor(name, shape, dt))

        def ps(name):
            return ctx.enter_context(nc.psum_tensor(name, [P, TC], F32))

        def sem(name):
            return ctx.enter_context(nc.semaphore(name))

        cols = sb("cols", [P, len(COLS)])
        ident = sb("ident", [P, P])
        later = sb("later", [P, E, E + 1])
        sel = sb("sel", [96, 2 * NS], BF16)
        w_router = sb("w_router", [P, E])
        w_e1h = sb("w_e1h", [P, E, HID], F32R)
        w_e1l = sb("w_e1l", [P, E, HID], F32R)
        w_e2 = sb("w_e2", [P, E * NK, P])
        b_e1 = sb("b_e1", [P, E * NK])
        b_e2 = sb("b_e2", [P, NJ, P])
        w_in = sb("w_in", [P, 4, P])
        w_dt = sb("w_dt", [P, ND, P])
        w_bc = sb("w_bc", [P, 96])
        w_out = sb("w_out", [P, ND, P])
        a_neg = sb("a_neg", [P, ND, NS])
        w_fft = sb("w_fft", [P, P])
        bias_row = sb("bias_row", [P, P])
        mods = sb("mods", [P, 8])
        gates = sb("gates", [P, 4, P])
        mhalf = sb("mhalf", [P, NJ])
        X = sb("X", [P, NC * NJ, D])
        ln_st = sb("ln_st", [P, NJ, 6])
        ln_mv = sb("ln_mv", [P, NJ, 2])
        ln_ve = sb("ln_ve", [P, NJ])
        ln_rs = sb("ln_rs", [P, NJ])
        ln_x = sb("ln_x", [P, NJ, D])
        wts = sb("wts", [P, 2, P])
        wT = sb("wT", [P, P])

        early = ExitStack()

        def sbe(name, shape, dt=F32):
            return early.enter_context(nc.sbuf_tensor(name, shape, dt))

        ones = sbe("ones", [P, 8])
        group_avg = sbe("group_avg", [P, P])
        dft = sbe("dft", [P, 3, P])
        part_row = sbe("part_row", [96, 2 * NS])
        w_qkv = sbe("w_qkv", [P, 3, P])
        qk_hi = sbe("qk_hi", [P, 4, TC], F32R)
        pick = sbe("pick", [P, DH, P], F32R)
        w_o = sbe("w_o", [P, P])
        w_f1 = sbe("w_f1", [P, 2, P])
        w_f2 = sbe("w_f2", [P, 2, P])
        w_freq = sbe("w_freq", [P, 2, P])
        g_freq = sbe("g_freq", [P, 2, P])
        silu_c = sbe("silu_c", [P, 2])
        silu_cb = sbe("silu_cb", [P, 2, P])
        gate_t = sbe("gate_t", [P, 4, P])
        diag_ga = sbe("diag_ga", [P, P])
        ln0_st = sbe("ln0_st", [P, NC * NJ, 6])
        ln0_mv = sbe("ln0_mv", [P, NC * NJ, 2])
        ln0_ve = sbe("ln0_ve", [P, NC * NJ])
        ln0_rs = sbe("ln0_rs", [P, NC * NJ])
        hT = sbe("hT", [P, NC, TC])
        gn_st = sbe("gn_st", [P, NC, 6])
        gn_mv = sbe("gn_mv", [P, 2])
        gn_me = sbe("gn_me", [P, 2])
        gn_g = sbe("gn_g", [P, 2])
        gn_ve = sbe("gn_ve", [P, 1])
        gn_rs = sbe("gn_rs", [P, 1])
        gn_sb = sbe("gn_sb", [P, 2])
        xn = sbe("xn", [P, 2, TC])
        qk_lo = sbe("qk_lo", [P, 4, TC], F32R)
        vp = sbe("vp", [P, TC])
        att_t = sbe("att_t", [P, TC])
        nrm = sbe("nrm", [P, 2 * NJ])
        rnm = sbe("rnm", [P, 2 * NJ])
        x3T = sbe("x3T", [P, 2, TC])
        S = sbe("S", [P, DH, TC])
        q2 = sbe("q2", [P, 2, TC])
        rb = sbe("rb", [P, 4, TC])
        w_mod = S[:, 0:3, :].rearrange("p a b -> p (a b)").rearrange("p (l n) -> p l n", l=2)
        U = sbe("U", [P, 2, TC])
        Qsb = sbe("Qsb", [P, 4, TC])
        ln0_x = Qsb[:, :, :].rearrange("p a (j d) -> p (a j) d", d=D)
        ZA = sbe("ZA", [P, 2, TC])
        ZAs = sbe("ZAs", [P, 2, TC])
        h1 = sbe("h1", [P, 4, TC])
        w_e1 = sbe("w_e1", [P, E, HID])
        early.close()

        h2T = sb("h2T", [P, TC])
        h2h = sb("h2h", [P, 2, TC], F32R)
        h2l = sb("h2l", [P, 2, TC], F32R)
        h3T = sb("h3T", [P, TC])
        h4T = h3T
        gel = sb("gel", [P, NG, TC])
        lg = sb("lg", [P, NJ, E])
        ex = sb("ex", [P, NJ, E])
        pr = sb("pr", [P, NJ, E])
        s4 = sb("s4", [P, 3, NJ])
        rank = sb("rank", [P, NJ, E])
        dA = sb("dA", [P, 2 * 2 * ND, TC])
        UB = sb("UB", [P, ND, TC])
        UBo = sb("UBo", [P, 2 * ND, TC])
        Bsb = sb("Bsb", [P, 2, TC])
        Hs = sb("Hs", [P, 2 * ND, TC])
        Zev = sb("Zev", [P, 2 * ND, TC])
        Zod = sb("Zod", [P, ND, TC])
        ZS = sb("ZS", [P, 2 * ND, TC])
        Csb = sb("Csb", [P, 2, TC])
        exd = sb("exd", [P, ND, TC])
        lnd = sb("lnd", [P, ND, TC])
        y2 = exd
        xr = sb("xr", [P, ND, TC + TAPS - 1])
        cv = sb("cv", [P, ND, TC])
        wx = cv
        gz = sb("gz", [P, 2 * ND, TC])
        xc = sb("xc", [P, ND, TC])
        dt = sb("dt", [P, 2 * ND, TC])
        u = sb("u", [P, 2 * ND, TC])
        BCf = lnd[0:96, 0, :]
        cmp_ = lnd[:, 1, :].rearrange("p (k t i j) -> p k t i j", k=2, t=NJ, i=E)
        P1 = exd[0:96, 0, 0:TC // 2].bitcast(BF16)
        ST = sb("ST", [96, 2, TC], BF16)
        HL = sb("HL", [P, ND, NS])
        outb = sb("outb", [P, NJ, D])

        pO, pY0, pY1, pB = (ps(n) for n in ("pO", "pY0", "pY1", "pB"))
        pH01 = ctx.enter_context(nc.psum_tensor("pH01", [P, 2, TC], F32))
        pH0, pH1 = pH = [pH01[:, 0, :], pH01[:, 1, :]]
        pCT = ctx.enter_context(nc.psum_tensor("pCT", [P, 2, TC], F32))
        pC, pT = pCT[:, 0, :], pCT[:, 1, :]
        pY = [pY0, pY1]

        def j4(ap):
            return ap.rearrange("p (j d) -> p j d", j=NJ)

        def half_of(t, c):
            return t[:, ND * (c % 2):ND * (c % 2) + ND, :]

        def alone(p):
            return p + AHEAD >= NC * E

        def col(n):
            return cols[:, COL[n]:COL[n] + 1]

        names = """ld_small ld_attn ld_ffn ld_moe ld_mam
            silu_c_ready mod_mm set_cb set_dve set_pool w_hi h2_hi h2_lo fr_mm fr_sb fft_mm fft_w exp_A neg_A
            ln_stats ln_rstd ln_xn ln_tr ln_evac
            gn_m gn_mm gn_v gn_r gn_ready xn_ready
            att_pick att_qkv att_sq att_hi att_lo att_ss att_nr att_r att_rb att_rbs att_vp
            att_kb att_qb att_qs att_u att_sc att_zo att_zs att_ow att_x2
            ffn_h ffn_silu ffn_o ffn_x3 ffn_tok ffn_x1
            moe_rt moe_lg moe_ex moe_w moe_wt moe_wts moe_bias moe_xb moe_h moe_g moe_g2 moe_acc
            mam_hist mam_xz mam_xr mam_gz mam_dtp mam_bc mam_bcs mam_cv mam_xc mam_v mam_ab mam_ex mam_ln mam_dt mam_u
            mam_st0 mam_st mam_Bs mam_uo mam_Cs mam_zo mam_zs mam_bB mam_bC mam_ub mam_dA mam_sc mam_z mam_y mam_y2 mam_o mam_x
            fft_o fft_b fft_x vec_chain act_chain pool_chain out_done""".split()
        s = {n: sem(n) for n in names}
        ld_x = [sem(f"ld_x{c}") for c in range(NC)]
        NSM, NAT, NFF, NMO, NMA = 6, 2, 2, 5, 9

        block = ctx.enter_context(nc.Block())

        def later_stages():
            def between(p, o):
                c, at = p // NP, 2 * (p % NP) + o
                head, tail, front = c + 2, c - 1, c + 1
                plan = {}
                if 0 <= tail:
                    plan = {"gate": (1, tail), "project": (1, tail), "ln_stats2": (2, tail), "ln_apply2": (3, tail),
                            "fft": (4, tail)}
                if 0 < head < NC:
                    plan |= {"ln_stats0": (4, head), "ln_apply0": (5, head), "route": (6, head), "turn": (7, head),
                             "weigh": (8, head)}
                if 0 <= front < NC:
                    plan |= {"ln_stats1": (10, front), "ln_apply1": (11, front), "x_part": (12, front),
                             "rows": (12, front), "conv0": (12, front), "dt_part": (12, front), "conv1": (12, front),
                             "z_part": (13, front), "soft": (13, front), "step": (15, front)}
                for name, (when, chunk) in plan.items():
                    if when == at:
                        yield (name.rstrip("012"), chunk) + ((int(name[-1]),) if name[-1].isdigit() else ())
            yield from [("route", 0), ("turn", 0), ("weigh", 0)]
            for p in range(-AHEAD, NC * NP):
                for o in range(2):
                    yield ("half", p, o)
                    yield from between(p, o)
            yield from [("total", NC * NP - 1), ("gate", NC - 1), ("project", NC - 1), ("ln_stats", NC - 1),
                        ("ln_apply", NC - 1, 2), ("fft", NC - 1)]

        @block.sync
        def _(sp):
            sp.dma_start(cols[:, :], a["cols"]).then_inc(s["ld_small"], 16)
            xv = a["x"].rearrange("(c j p) d -> c p j d", c=NC, j=NJ)
            for c in range(NC):
                sp.dma_start(X[:, c * NJ:(c + 1) * NJ, :], xv[c]).then_inc(ld_x[c], 16)
                if c == 0:
                    sp.dma_start(ident[:, :], a["ident"]).then_inc(s["ld_small"], 16)
            sp.dma_start(w_qkv[:, :, :], a["w_qkv"]).then_inc(s["ld_attn"], 16)
            sp.dma_start(w_o[:, :], a["w_o"]).then_inc(s["ld_attn"], 16)
            sp.dma_start(w_f1[:, :, :], a["w_f1"]).then_inc(s["ld_ffn"], 16)
            sp.dma_start(w_f2[:, :, :], a["w_f2"]).then_inc(s["ld_ffn"], 16)
            sp.dma_start(w_router[:, :], a["w_router"]).then_inc(s["ld_moe"], 16)
            sp.dma_start(w_e1[:, :, :], a["w_e1"]).then_inc(s["ld_moe"], 16)
            sp.dma_start(w_e2[:, :, :], a["w_e2"]).then_inc(s["ld_moe"], 16)
            sp.dma_start(b_e1[:, :], a["b_e1"]).then_inc(s["ld_moe"], 16)
            sp.dma_start(b_e2[:, :, :], a["b_e2"]).then_inc(s["ld_moe"], 16)
            for n, t in (("w_in", w_in), ("w_dt", w_dt), ("w_bc", w_bc), ("w_out", w_out), ("a_log", a_neg),
                         ("w_freq", w_freq), ("part_row", part_row), ("later", later), ("dft", dft)):
                sp.dma_start(t[:], a[n]).then_inc(s["ld_mam"], 16)
            ov = out.rearrange("(c j p) d -> c p j d", c=NC, j=NJ)
            for c in range(NC):
                sp.wait_ge(s["fft_x"], c + 1)
                sp.dma_start(ov[c], outb[:, :, :]).then_inc(s["out_done"], 16)
            sp.wait_ge(s["out_done"], 16 * NC)

        @block.gpsimd
        def _(pool):
            chain = [0]

            def link(ins):
                ins.then_inc(s["pool_chain"], 1)
                chain[0] += 1
                pool.wait_ge(s["pool_chain"], chain[0])

            L = [0]

            def ln():
                pool.wait_ge(s["ln_stats"], L[0] + 1)
                link(pool.tensor_scalar(ln_ve[:, :], ln_mv[:, :, 1], EPS, None, ALU.add))
                pool.tensor_tensor(ln_rs[:, :], ln_ve[:, :], mhalf[:, :], ALU.pow).then_inc(s["ln_rstd"], 1)
                L[0] += 1

            def gn(g):
                pool.wait_ge(s["gn_v"], g + 1)
                pool.tensor_tensor(gn_rs[:, :], gn_ve[:, :], mhalf[:, 0:1], ALU.pow).then_inc(s["gn_r"], 1)

            done = {"mam_uo": 0, "mam_zs": 0}

            def odd_input(p):
                c = p // NP
                pool.wait_ge(s["mam_Bs"], p + 1)
                pool.wait_ge(s["mam_u"], c + 1)
                if p >= 2:
                    pool.wait_ge(s["mam_sc"], 2 * (p - 1))
                h = slice(2 * (p % 2), 2 * (p % 2) + 2)
                pool.tensor_tensor(UBo[:, h, :], half_of(u, c), Bsb[:, p % 2:p % 2 + 1, :].to_broadcast([P, ND, TC]),
                                   ALU.mult).then_inc(s["mam_uo"], 1)
                done["mam_uo"] = p + 1

            def odd_output(p):
                h = slice(2 * (p % 2), 2 * (p % 2) + 2)
                if p == NC * NP - 1:
                    return
                pool.wait_ge(s["mam_Cs"], p + 1)
                if p:
                    pool.wait_ge(s["mam_zo"], p)
                    pool.wait_ge(s["mam_zs"], min(p, NC * E - AHEAD))
                pool.wait_ge(s["mam_sc"], 2 * p + 2)
                if alone(p):
                    pool.wait_ge(s["mam_y"], p - 1)
                pool.tensor_tensor(ZS[:, h, :] if alone(p) else Zod[:, :, :], Hs[:, 2:4, :],
                                   Csb[:, p % 2:p % 2 + 1, :].to_broadcast([P, ND, TC]), ALU.mult).then_inc(s["mam_zo"], 1)
                if alone(p):
                    return
                pool.wait_ge(s["mam_zo"], p + 1)
                pool.wait_ge(s["mam_z"], p + 1)
                if p >= 2:
                    pool.wait_ge(s["mam_y"], p - 1)
                pool.tensor_tensor(ZS[:, h, :], Zev[:, h, :], Zod[:, :, :], ALU.add).then_inc(s["mam_zs"], 1)
                done["mam_zs"] = p + 1

            link(pool.memset(mhalf[:, :], -0.5))
            pool.memset(ones[:, :], 1.0).then_inc(s["set_pool"], 1)
            for c in range(NC):
                jj = slice(c * NJ, (c + 1) * NJ)
                pool.wait_ge(s["ln_stats"], c + 1)
                link(pool.tensor_scalar(ln0_ve[:, jj], ln0_mv[:, jj, 1], EPS, None, ALU.add))
                pool.tensor_tensor(ln0_rs[:, jj], ln0_ve[:, jj], mhalf[:, :], ALU.pow).then_inc(s["ln_rstd"], 1)
            L[0] = NC
            gn(0)

            def expert_weights(q):
                if q == 0:
                    pool.wait_ge(s["ld_moe"], 16 * NMO)
                    pool.wait_ge(s["set_dve"], 3)
                gb = gates[:, 1:2, :]
                part = slice(E * NK // NC * q, E * NK // NC * (q + 1))
                pool.tensor_tensor(w_e2[:, part, :], w_e2[:, part, :], gb.to_broadcast([P, E * NK // NC, P]),
                                   ALU.mult).then_inc(s["set_pool"], 1)
                part = slice(E // NC * q, E // NC * (q + 1))
                pool.wait_ge(s["w_hi"], q + 1)
                pool.tensor_tensor(w_e1l[:, part, :], w_e1[:, part, :], w_e1h[:, part, :].bitcast(F32),
                                   ALU.subtract).then_inc(s["set_pool"], 1)
                if q == 0:
                    pool.tensor_tensor(b_e2[:, :, :], b_e2[:, :, :], gb.to_broadcast([P, NJ, P]),
                                       ALU.mult).then_inc(s["set_pool"], 1)

            pool.wait_ge(s["ld_mam"], 16 * NMA)
            pool.tensor_copy(sel[:, :], part_row[:, :]).then_inc(s["set_pool"], 1)
            for c in range(NC):
                for r in range(NR):
                    R = NR * c + r
                    pool.wait_ge(s["att_qs"], R + 1)
                    pool.wait_ge(s["att_sc"], R + 1)
                    if R:
                        pool.wait_ge(s["att_zs"], R)
                    pool.tensor_tensor(ZA[:, :, :], Qsb[:, 2 * (R % 2):2 * (R % 2) + 2, :], S[:, 2 * r:2 * r + 2, :],
                                       ALU.mult).then_inc(s["att_zo"], 1)
                    pool.wait_ge(s["att_zo"], R + 1)
                    if R >= 2:
                        pool.wait_ge(s["att_ow"], R - 1)
                    pool.tensor_tensor(ZAs[:, R % 2, :], ZA[:, 0, :], ZA[:, 1, :], ALU.add).then_inc(s["att_zs"], 1)
                if c < NC // 2:
                    expert_weights(c)
            gn(1)
            ln()
            for q in range(NC // 2, NC):
                expert_weights(q)
            pool.tensor_tensor(w_out[:, :, :], w_out[:, :, :], gates[:, 2:3, :].to_broadcast([P, ND, P]),
                               ALU.mult).then_inc(s["set_pool"], 1)
            for stage, c, *k in later_stages():
                if stage == "ln_stats":
                    ln()
                elif stage == "half":
                    p, o = c, k[0]
                    if 0 <= p + 1 < NC * NP and o == 0 and (p + 1) % NP:
                        odd_input(p + 1)
                    if o == 1 and p >= 0:
                        odd_output(p)
                    if 0 <= p + 1 < NC * NP and o == 1 and (p + 1) % NP == 0:
                        odd_input(p + 1)
                elif stage == "rows":
                    st = ST[:, c % 2, :]
                    pool.wait_ge(s["mam_st0"], c + 1)
                    for name, count in done.items():
                        if count:
                            pool.wait_ge(s[name], count)
                    link(pool.tensor_tensor(st[32:64, :], BCf[32:64, :], st[32:64, :], ALU.subtract))
                    link(pool.tensor_tensor(P1[64:96, :], BCf[64:96, :], st[64:96, :], ALU.subtract))
                    link(pool.tensor_tensor(BCf[64:96, :], BCf[64:96, :], st[64:96, :], ALU.subtract))
                    pool.tensor_tensor(st[64:96, :], BCf[64:96, :], P1[64:96, :], ALU.subtract).then_inc(s["mam_st"], 1)
                    pool.wait_ge(s["mam_st"], c + 1)
                elif stage == "fft":
                    pool.wait_ge(s["mam_x"], c + 1)
                    if c:
                        pool.wait_ge(s["out_done"], 16 * c)
                    pool.tensor_tensor(outb[:, :, :], X[:, c * NJ:(c + 1) * NJ, :], bias_row[:, None, :].to_broadcast([P, NJ, D]),
                                       ALU.add).then_inc(s["fft_b"], 1)

        @block.vector
        def _(vec):
            chain = [0]
            L = [0]

            def link(ins):
                ins.then_inc(s["vec_chain"], 1)
                chain[0] += 1
                vec.wait_ge(s["vec_chain"], chain[0])

            def sig(ins, name, count):
                ins.then_inc(s[name], 1)
                vec.wait_ge(s[name], count)

            def ln_stats(c):
                Xc = X[:, c * NJ:(c + 1) * NJ, :]
                for j in range(NJ):
                    ins = vec.bn_stats(ln_st[:, j, :], Xc[:, j, :])
                link(ins)
                for j in range(NJ):
                    ins = vec.bn_aggr(ln_mv[:, j, :], ln_st[:, j, :])
                ins.then_inc(s["ln_stats"], 1)

            def ln_apply(c):
                Xc = X[:, c * NJ:(c + 1) * NJ, :]
                vec.wait_ge(s["ln_stats"], L[0] + 1)
                vec.wait_ge(s["ln_rstd"], L[0] + 1)
                if L[0]:
                    vec.wait_ge(s["ln_tr"], L[0])
                for j in range(NJ):
                    vec.tensor_scalar(ln_x[:, j, :], Xc[:, j, :], ln_mv[:, j, 0:1], ln_rs[:, j:j + 1],
                                      ALU.subtract, ALU.mult).then_inc(s["ln_xn"], 1)
                L[0] += 1

            def gn(g, gamma, beta):
                link(vec.bn_aggr(gn_mv[:, :], gn_st[:, :, :].rearrange("p c k -> p (c k)")))
                vec.tensor_copy(gn_me[:, 0:1], gn_mv[:, 0:1])
                vec.scalar_tensor_tensor(gn_me[:, 1:2], gn_mv[:, 0:1], gn_mv[:, 0:1], gn_mv[:, 1:2],
                                         ALU.mult, ALU.add).then_inc(s["gn_m"], 1)
                vec.wait_ge(s["gn_mm"], g + 1)
                link(vec.tensor_copy(gn_g[:, :], pO[:, 0:2]))
                link(vec.scalar_tensor_tensor(gn_ve[:, :], gn_g[:, 0:1], gn_g[:, 0:1], gn_g[:, 1:2],
                                              ALU.mult, ALU.subtract))
                vec.tensor_scalar(gn_ve[:, :], gn_ve[:, :], -1.0, EPS, ALU.mult, ALU.add).then_inc(s["gn_v"], 1)
                vec.wait_ge(s["gn_r"], g + 1)
                link(vec.tensor_tensor(gn_sb[:, 0:1], gn_rs[:, :], col(gamma), ALU.mult))
                link(vec.scalar_tensor_tensor(gn_sb[:, 1:2], gn_g[:, 0:1], gn_sb[:, 0:1], col(beta),
                                              ALU.mult, ALU.subtract))
                vec.tensor_scalar(gn_sb[:, 1:2], gn_sb[:, 1:2], -1.0, None, ALU.mult).then_inc(s["gn_ready"], 1)

            def ln0_stats(c):
                vec.wait_ge(ld_x[c], 16)
                for j in range(c * NJ, (c + 1) * NJ):
                    ins = vec.bn_stats(ln0_st[:, j, :], X[:, j, :])
                link(ins)
                for j in range(c * NJ, (c + 1) * NJ):
                    ins = vec.bn_aggr(ln0_mv[:, j, :], ln0_st[:, j, :])
                ins.then_inc(s["ln_stats"], 1)

            def modulation(l):
                vec.wait_ge(s["mod_mm"], 2 * l + 2)
                vec.tensor_copy(mods[:, 4 * l:4 * l + 4], [pT, pB][l][:, 0:4])
                link(vec.tensor_copy(gates[:, 2 * l:2 * l + 2, :], [pO, pY0][l][:, 0:256].rearrange("p (g d) -> p g d", g=2)))
                mc = mods[:, 4 * l:4 * l + 4].rearrange("p (a b) -> p a b", b=2)[:, :, 1]
                vec.tensor_scalar(mc, mc, 1.0, None, ALU.add).then_inc(s["set_dve"], 1)

            def clamp_gates():
                link(vec.tensor_scalar(gate_t[:, :, :], gates[:, :, :], 0.0, 2.0, ALU.is_ge, ALU.mult))
                link(vec.scalar_tensor_tensor(gates[:, :, :], gates[:, :, :], -1.0, gates[:, :, :], ALU.mult, ALU.max))
                link(vec.tensor_scalar(gates[:, :, :], gates[:, :, :], 0.25, None, ALU.max))
                link(vec.scalar_tensor_tensor(gates[:, :, :], gate_t[:, :, :], -1.0, gates[:, :, :], ALU.add, ALU.mult))
                vec.tensor_tensor(diag_ga[:, :], ident[:, :], gates[:, 0, :], ALU.mult)
                vec.tensor_tensor(bias_row[:, :], bias_row[:, :], gates[:, 3, :], ALU.mult).then_inc(s["set_dve"], 1)

            ln0_stats(0)
            vec.wait_ge(s["silu_c_ready"], 1)
            vec.tensor_copy(silu_cb[:, 0, :], silu_c[:, 0:1].to_broadcast([P, P])).then_inc(s["set_cb"], 1)
            vec.tensor_copy(silu_cb[:, 1, :], silu_c[:, 1:2].to_broadcast([P, P])).then_inc(s["set_cb"], 1)
            for c in range(1, NC):
                ln0_stats(c)
            modulation(0)
            for c in range(NC):
                vec.wait_ge(s["ln_rstd"], c + 1)
                vec.wait_ge(s["ln_stats"], c + 1)
                for j in range(c * NJ, (c + 1) * NJ):
                    vec.tensor_scalar(ln0_x[:, j, :], X[:, j, :], ln0_mv[:, j, 0:1], ln0_rs[:, j:j + 1],
                                      ALU.subtract, ALU.mult).then_inc(s["ln_xn"], 1)
            L[0] = NC
            modulation(1)
            for c in range(NC):
                vec.wait_ge(s["ln_evac"], c + 1)
                ins = vec.bn_stats(gn_st[:, c, :], hT[:, c, :])
            link(ins)
            gn(0, "norm_g", "norm_b")

            def qk_parts(c):
                for k in range(2):
                    vec.wait_ge(s["att_hi"], 2 * c + k + 1)
                    vec.wait_ge(s["att_sq"], 2 * c + k + 1)
                    vec.tensor_tensor(qk_lo[:, 2 * (c % 2) + k, :], pY[k][:, :], qk_hi[:, 2 * (c % 2) + k, :].bitcast(F32),
                                      ALU.subtract).then_inc(s["att_lo"], 1)

            def norms(c):
                vec.wait_ge(s["att_nr"], c + 1)
                link(vec.tensor_scalar(nrm[:, :], nrm[:, :], 1e-12, None, ALU.max))
                vec.reciprocal(rnm[:, :], nrm[:, :]).then_inc(s["att_r"], 1)

            def values(c):
                vec.wait_ge(s["att_qkv"], 3 * c + 3)
                vec.wait_ge(s["att_rbs"], 2 * c + 2)
                sig(vec.tensor_tensor(vp[:, :], pB[:, :], rb[:, 2 * (c % 2) + 1, :], ALU.mult), "att_vp", c + 1)

            def finish(c):
                vec.wait_ge(s["att_ow"], NR * (c + 1))
                link(vec.scalar_tensor_tensor(att_t[:, :], pO[:, :], float(1.0 / np.sqrt(DH)), rb[:, 2 * (c % 2), :],
                                              ALU.mult, ALU.mult))
                sig(vec.scalar_tensor_tensor(hT[:, c, :], att_t[:, :], col("ob"), hT[:, c, :], ALU.add, ALU.add),
                    "att_x2", c + 1)
                link(vec.bn_stats(gn_st[:, c, :], hT[:, c, :]))

            vec.memset(wts[:, :, :], 0.0)
            vec.tensor_copy(pick[:, :, :].rearrange("p i (h v) -> p i h v", v=DH),
                            ident[:, :].rearrange("p (h i) -> p i h", i=DH)[:, :, :, None].to_broadcast([P, DH, HEADS, DH])
                            ).then_inc(s["att_pick"], 1)
            qk_parts(0)
            clamp_gates()
            norms(0)
            values(0)
            for c in range(NC):
                for r in range(NR):
                    R = NR * c + r
                    vec.wait_ge(s["att_kb"], R + 1)
                    sig(vec.tensor_tensor(U[:, :, :], pH01[:, :, :], vp[:, None, :].to_broadcast([P, 2, TC]), ALU.mult),
                        "att_u", R + 1)
                    if c:
                        vec.wait_ge(s["att_zo"], R - NR + 1)
                    for o in range(2):
                        i = 2 * r + o
                        ins = vec.tensor_tensor_scan(S[:, i, :], col("gamma").to_broadcast([P, TC]), U[:, o, :],
                                                     S[:, i, TC - 1:TC] if c else 0.0, ALU.mult, ALU.add)
                    sig(ins, "att_sc", R + 1)
                    if r == 1 and c:
                        finish(c - 1)
                    if c + 1 < NC and r < NR - 1:
                        [qk_parts, norms, lambda c: None][r](c + 1)
                if c + 1 < NC:
                    values(c + 1)
            vec.wait_ge(s["fr_mm"], 2)
            vec.tensor_copy(g_freq[:, 0, :], pH0[:, 0:P]).then_inc(s["fr_sb"], 1)
            vec.tensor_copy(g_freq[:, 1, :], pH1[:, 0:P]).then_inc(s["fr_sb"], 1)
            finish(NC - 1)
            gn(1, "ffn_g", "ffn_b")
            vec.wait_ge(s["fft_mm"], 1)
            vec.scalar_tensor_tensor(w_fft[:, :], pH0[:, 0:P], 1.0 / D, gates[:, 3, :], ALU.mult, ALU.mult).then_inc(s["fft_w"], 1)
            vec.wait_ge(s["exp_A"], 1)
            vec.tensor_scalar(a_neg[:, :, :], a_neg[:, :, :], -1.0, None, ALU.mult).then_inc(s["neg_A"], 1)

            def ffn_x1(c):
                vec.wait_ge(s["ffn_tok"], c + 1)
                Xc = X[:, c * NJ:(c + 1) * NJ, :]
                sig(vec.tensor_tensor(Xc, Xc, j4([pB, pC][c % 2][:, :]), ALU.add), "ffn_x1", c + 1)

            for c in range(NC):
                vec.wait_ge(s["ffn_o"], c + 1)
                if c >= 2:
                    vec.wait_ge(s["ffn_tok"], c - 1)
                vec.scalar_tensor_tensor(x3T[:, c % 2, :], pY[c % 2][:, :], col("b2"), hT[:, c, :], ALU.add,
                                         ALU.add).then_inc(s["ffn_x3"], 1)
                if c:
                    ffn_x1(c - 1)
                if c == 1:
                    ln_stats(0)
                if c == 2:
                    ln_apply(0)
            ffn_x1(NC - 1)

            def route(c):
                vec.wait_ge(s["h2_hi"], c + 1)
                vec.wait_ge(s["ln_evac"], L[0])
                vec.tensor_tensor(h2l[:, c % 2, :], h2T[:, :], h2h[:, c % 2, :].bitcast(F32), ALU.subtract).then_inc(s["h2_lo"], 1)
                vec.wait_ge(s["moe_rt"], c + 1)
                logits = pT[:, 0:NJ * E].rearrange("p (j e) -> p j e", j=NJ)
                mx, sm, rs = (s4[:, k, :] for k in range(3))

                def over(v):
                    return v[:, :, None].to_broadcast([P, NJ, E])
                link(vec.tensor_reduce(mx, logits, AX.X, ALU.max))
                vec.tensor_tensor(lg[:, :, :], logits, over(mx), ALU.subtract).then_inc(s["moe_lg"], 1)
                vec.wait_ge(s["moe_ex"], c + 1)
                link(vec.tensor_reduce(sm, ex[:, :, :], AX.X, ALU.add))
                link(vec.reciprocal(rs, sm))
                link(vec.tensor_tensor(pr[:, :, :], ex[:, :, :], over(rs), ALU.mult))
                full = [P, NJ, E, E]
                G, M = cmp_[:, 0, :, :, :], cmp_[:, 1, :, :, :]
                link(vec.tensor_tensor(G, pr[:, :, None, :].to_broadcast(full), pr[:, :, :, None].to_broadcast(full), ALU.is_gt))
                link(vec.tensor_tensor(M, G, later[:, None, :, 0:E].to_broadcast(full), ALU.mult))
                link(vec.tensor_tensor(G, M, M.rearrange("p t i j -> p t j i"), ALU.subtract))
                link(vec.tensor_reduce(rank[:, :, :], G, AX.X, ALU.add))
                link(vec.tensor_tensor(rank[:, :, :], rank[:, :, :], later[:, None, :, E].to_broadcast([P, NJ, E]), ALU.is_lt))
                sig(vec.tensor_tensor(wts[:, c % 2, 0:NJ * E].rearrange("p (t e) -> p t e", e=E), rank[:, :, :], pr[:, :, :],
                                      ALU.mult), "moe_w", c + 1)

            def weigh(c):
                vec.wait_ge(s["moe_bias"], c + 1)
                Xc = X[:, c * NJ:(c + 1) * NJ, :]
                sig(vec.tensor_tensor(Xc, Xc, j4(pT[:, :]), ALU.add), "moe_xb", c + 1)

            def moe_acc(g):
                c, e = divmod(g, E)
                vec.wait_ge(s["moe_g2"], NK * (g + 1))
                for j in range(NJ):
                    Xj = X[:, c * NJ + j, :]
                    ins = vec.scalar_tensor_tensor(Xj, pO[:, j * P:(j + 1) * P], wts[:, c % 2, j * E + e:j * E + e + 1], Xj,
                                                   ALU.mult, ALU.add)
                sig(ins, "moe_acc", g + 1)

            def conv(c, d):
                vec.wait_ge(s["mam_xr"], 2 * c + d + 1)
                for k in range(TAPS):
                    w = col(f"conv_w{d}{k}")
                    if k == 0:
                        link(vec.tensor_scalar(cv[:, d, :], xr[:, d, 0:TC], w, col(f"conv_b{d}"), ALU.mult, ALU.add))
                    else:
                        ins = vec.scalar_tensor_tensor(cv[:, d, :], xr[:, d, k:k + TC], w, cv[:, d, :], ALU.mult, ALU.add)
                        if k < TAPS - 1:
                            link(ins)
                sig(ins, "mam_cv", 2 * c + d + 1)
                if c + 1 < NC:
                    vec.tensor_copy(xr[:, d, 0:TAPS - 1], xr[:, d, TC:TC + TAPS - 1]).then_inc(s["mam_hist"], 1)

            def step(c):
                d_ = half_of(dt, c)
                vec.wait_ge(s["mam_ex"], c + 1)
                link(vec.tensor_scalar(wx[:, :, :], exd[:, :, :], 1.0, None, ALU.add))
                link(vec.scalar_tensor_tensor(wx[:, :, :], wx[:, :, :], -1.0, exd[:, :, :], ALU.add, ALU.subtract))
                vec.wait_ge(s["mam_ln"], c + 1)
                link(vec.scalar_tensor_tensor(d_, d_, 0.0, lnd[:, :, :], ALU.max, ALU.add))
                sig(vec.tensor_tensor(d_, d_, wx[:, :, :], ALU.subtract), "mam_dt", c + 1)
                vec.wait_ge(s["mam_xc"], 2 * c + 2)
                sig(vec.tensor_tensor(half_of(u, c), d_, xc[:, :, :], ALU.mult), "mam_u", c + 1)

            def half(p, o):
                c, k = divmod(p, NP)
                m = 2 * p + o
                n = 2 * k + o
                if p >= 0 and o == 0:
                    vec.wait_ge(s["mam_bB"], m + 2)
                    sig(vec.tensor_tensor(UB[:, :, :], half_of(u, c), pB[:, None, :].to_broadcast([P, ND, TC]), ALU.mult),
                        "mam_ub", p + 1)
                if o == 0 and 0 <= p + AHEAD - 2 < NC * E:
                    moe_acc(p + AHEAD - 2)
                if p < 0:
                    return
                vec.wait_ge(s["mam_dA"], 2 * ND * (p + 1))
                if o:
                    vec.wait_ge(s["mam_uo"], p + 1)
                    if p:
                        vec.wait_ge(s["mam_zo"], p)
                for d in range(ND):
                    r = 2 * o + d
                    in_ = UBo[:, 2 * (p % 2) + d, :] if o else UB[:, d, :]
                    ins = vec.tensor_tensor_scan(Hs[:, r, :], dA[:, 4 * (p % 2) + r, :], in_,
                                                 HL[:, d, n:n + 1] if c else 0.0, ALU.mult, ALU.add)
                sig(ins, "mam_sc", m + 1)
                if c + 1 < NC:
                    vec.tensor_copy(HL[:, :, n:n + 1], Hs[:, 2 * o:2 * o + 2, TC - 1:TC])
                if o == 0:
                    vec.wait_ge(s["mam_bC"], m + 1)
                    if p >= 2:
                        vec.wait_ge(s["mam_y" if alone(p - 2) else "mam_zs"], p - 1)
                    z = Zev[:, 2 * (p % 2):2 * (p % 2) + 2, :]
                    sig(vec.tensor_tensor(z, Hs[:, 0:2, :], pC[:, None, :].to_broadcast([P, ND, TC]), ALU.mult),
                        "mam_z", p + 1)
                elif p == NC * NP - 1:
                    vec.wait_ge(s["mam_bC"], m + 1)
                    vec.wait_ge(s["mam_y"], p - 1)
                    vec.tensor_tensor(ZS[:, 2 * (p % 2):2 * (p % 2) + 2, :], Hs[:, 2:4, :], pC[:, None, :].to_broadcast([P, ND, TC]),
                                      ALU.mult).then_inc(s["mam_zo"], 1)

            def gate(c):
                vec.wait_ge(s["mam_y"], NS // 2 * (c + 1))
                for d in range(ND):
                    vec.tensor_tensor(y2[:, d, :], pY[d][:, :], half_of(gz, c)[:, d, :], ALU.mult).then_inc(s["mam_y2"], 1)

            def project(c):
                vec.wait_ge(s["mam_o"], c + 1)
                Xc = X[:, c * NJ:(c + 1) * NJ, :]
                sig(vec.tensor_tensor(Xc, Xc, j4(pT[:, :]), ALU.add), "mam_x", c + 1)

            def fft(c):
                vec.wait_ge(s["fft_b"], c + 1)
                vec.wait_ge(s["fft_o"], c + 1)
                sig(vec.tensor_tensor(outb[:, :, :], j4(pT[:, :]), outb[:, :, :], ALU.add), "fft_x", c + 1)

            for d in range(ND):
                vec.memset(xr[:, d, 0:TAPS - 1], 0.0).then_inc(s["mam_hist"], 1)
            for stage, c, *k in later_stages():
                if stage == "ln_stats":
                    ln_stats(c)
                elif stage == "ln_apply":
                    ln_apply(c)
                elif stage == "half":
                    half(c, *k)
                elif stage == "conv":
                    conv(c, *k)
                elif stage in ("route", "weigh", "step", "gate", "project", "fft"):
                    {"route": route, "weigh": weigh, "step": step, "gate": gate, "project": project,
                     "fft": fft}[stage](c)

        @block.scalar
        def _(act):
            chain = [0]
            L = [0]

            def link(ins):
                ins.then_inc(s["act_chain"], 1)
                chain[0] += 1
                act.wait_ge(s["act_chain"], chain[0])

            act.dma_start(w_mod[:, 0, :], a["w_mod0"]).then_inc(s["ld_small"], 16)
            act.dma_start(group_avg[:, :], a["group_avg"]).then_inc(s["ld_small"], 16)
            act.dma_start(bias_row[:, :], a["fft_bias"].to_broadcast([P, P])).then_inc(s["ld_small"], 16)
            act.dma_start(w_mod[:, 1, :], a["w_mod1"]).then_inc(s["ld_small"], 16)
            act.wait_ge(s["ld_small"], 16 * NSM)
            nc.scalar.activation(silu_c[:, :], cols[:, COL["c0"]:COL["c0"] + 2], ACT.Silu).then_inc(s["silu_c_ready"], 1)

            def ln(dest, m, high=None):
                act.wait_ge(s["ln_tr"], L[0] + 1)
                if high is not None:
                    nc.scalar.activation(high, pT[:, :], ACT.Identity, bias=mods[:, m:m + 1],
                                         scale=mods[:, m + 1:m + 2]).then_inc(s["h2_hi"], 1)
                nc.scalar.activation(dest, pT[:, :], ACT.Identity, bias=mods[:, m:m + 1],
                                     scale=mods[:, m + 1:m + 2]).then_inc(s["ln_evac"], 1)
                L[0] += 1

            act.wait_ge(s["set_dve"], 1)
            for c in range(NC):
                act.wait_ge(s["ln_tr"], c + 1)
                nc.scalar.activation(hT[:, c, :], pCT[:, c % 2, :], ACT.Identity, bias=mods[:, 0:1],
                                     scale=mods[:, 1:2]).then_inc(s["ln_evac"], 1)
            L[0] = NC

            def xn_of(k, c):
                act.wait_ge(s["gn_ready"], k + 1)
                if c >= 2:
                    act.wait_ge(s["att_qkv" if k == 0 else "ffn_h"], (3 if k == 0 else 2) * (c - 1))
                nc.scalar.activation(xn[:, c % 2, :], hT[:, c, :], ACT.Identity, bias=gn_sb[:, 1:2],
                                     scale=gn_sb[:, 0:1]).then_inc(s["xn_ready"], 1)

            def qk_parts(c):
                for k in range(2):
                    act.wait_ge(s["att_qkv"], 3 * c + k + 1)
                    if c >= 2:
                        act.wait_ge(s["att_qb"], NR * (c - 1))
                    nc.scalar.copy(qk_hi[:, 2 * (c % 2) + k, :], pY[k][:, :]).then_inc(s["att_hi"], 1)
                    nc.scalar.activation(q2[:, k, :], pY[k][:, :], ACT.Square).then_inc(s["att_sq"], 1)

            def norms(c):
                act.wait_ge(s["att_ss"], c + 1)
                nc.scalar.activation(nrm[:, :], pY1[:, 0:2 * NJ], ACT.Sqrt).then_inc(s["att_nr"], 1)

            def spread(c):
                for k in range(2):
                    act.wait_ge(s["att_rb"], 2 * c + k + 1)
                    if c >= 2:
                        act.wait_ge(s["att_x2"], c - 1)
                    nc.scalar.copy(rb[:, 2 * (c % 2) + k, :], pY[k][:, :]).then_inc(s["att_rbs"], 1)

            xn_of(0, 0)
            qk_parts(0)
            xn_of(0, 1)
            norms(0)
            spread(0)
            for c in range(NC):
                for r in range(NR):
                    R = NR * c + r
                    act.wait_ge(s["att_qb"], R + 1)
                    if R >= 2:
                        act.wait_ge(s["att_zo"], R - 1)
                    nc.scalar.copy(Qsb[:, 2 * (R % 2):2 * (R % 2) + 2, :], pCT[:, :, :]).then_inc(s["att_qs"], 1)
                    if c + 1 < NC and r < NR - 1:
                        [qk_parts, norms, spread][r](c + 1)
                if c + 2 < NC:
                    xn_of(0, c + 2)
                if c == 0:
                    act.wait_ge(s["ld_moe"], 16 * NMO)
                part = slice(E // NC * c, E // NC * (c + 1))
                nc.scalar.copy(w_e1h[:, part, :], w_e1[:, part, :]).then_inc(s["w_hi"], 1)

            act.wait_ge(s["ld_mam"], 16 * NMA)
            nc.scalar.activation(a_neg[:, :, :], a_neg[:, :, :], ACT.Exp).then_inc(s["exp_A"], 1)
            act.wait_ge(s["set_dve"], 3)
            xn_of(1, 0)
            for c in range(NC):
                if c + 1 < NC:
                    xn_of(1, c + 1)
                for m in range(2):
                    act.wait_ge(s["ffn_h"], 2 * c + m + 1)
                    if c >= 2:
                        act.wait_ge(s["ffn_o"], c - 1)
                    nc.scalar.activation(h1[:, 2 * (c % 2) + m, :], pH[m][:, :], ACT.Silu,
                                         bias=col(f"b1_{m}")).then_inc(s["ffn_silu"], 1)
                if c == 3:
                    ln(h2T[:, :], 2, h2h[:, 0, :])

            def route(c):
                act.wait_ge(s["moe_lg"], c + 1)
                nc.scalar.activation(ex[:, :, :], lg[:, :, :], ACT.Exp).then_inc(s["moe_ex"], 1)

            def turn(c):
                act.wait_ge(s["moe_wt"], c + 1)
                nc.scalar.copy(wT[:, :], pT[:, P:2 * P]).then_inc(s["moe_wts"], 1)

            def x_part(c):
                for d in range(ND):
                    act.wait_ge(s["mam_hist"], 2 * c + d + 1)
                    act.wait_ge(s["mam_xz"], 4 * c + d + 1)
                    nc.scalar.copy(xr[:, d, TAPS - 1:TC + TAPS - 1], pH[d][:, :]).then_inc(s["mam_xr"], 1)

            def rows(c):
                act.wait_ge(s["mam_bc"], c + 1)
                if c:
                    act.wait_ge(s["mam_st"], c)
                nc.scalar.copy(BCf[:, :], pT[0:96, :]).then_inc(s["mam_bcs"], 1)
                act.wait_ge(s["mam_bcs"], c + 1)
                nc.scalar.copy(ST[:, c % 2, :], BCf[:, :]).then_inc(s["mam_st0"], 1)

            def dt_part(c):
                v_ = half_of(dt, c)
                for d in range(ND):
                    act.wait_ge(s["mam_dtp"], 2 * c + d + 1)
                    nc.scalar.activation(v_[:, d, :], pH[d][:, :], ACT.Identity,
                                         bias=col(f"b_dt{d}")).then_inc(s["mam_v"], 1)

            def z_part(c):
                for d in range(ND):
                    act.wait_ge(s["mam_xz"], 4 * c + 3 + d)
                    nc.scalar.activation(half_of(gz, c)[:, d, :], pH[d][:, :], ACT.Silu).then_inc(s["mam_gz"], 1)
                for d in range(ND):
                    act.wait_ge(s["mam_cv"], 2 * c + d + 1)
                    nc.scalar.activation(xc[:, d, :], cv[:, d, :], ACT.Silu).then_inc(s["mam_xc"], 1)
                act.wait_ge(s["mam_v"], 2 * c + 2)
                act.wait_ge(s["mam_st"], c + 1)
                nc.scalar.activation(exd[:, :, :], half_of(dt, c), ACT.Abs).then_inc(s["mam_ab"], 1)

            def soft(c):
                act.wait_ge(s["mam_ab"], c + 1)
                nc.scalar.activation(exd[:, :, :], exd[:, :, :], ACT.Exp, scale=-1.0).then_inc(s["mam_ex"], 1)
                act.wait_ge(s["mam_ex"], c + 1)
                nc.scalar.activation(lnd[:, :, :], exd[:, :, :], ACT.Ln, bias=1.0).then_inc(s["mam_ln"], 1)

            def hidden(g, ks):
                for k in ks:
                    n = NK * g + k
                    e = g % E
                    act.wait_ge(s["moe_h"], n + 1)
                    if n >= NG:
                        act.wait_ge(s["moe_g2"], n - NG + 1)
                    nc.scalar.activation(gel[:, n % NG, :], pH[n % 2][:, :], ACT.Gelu_apprx_tanh,
                                         bias=b_e1[:, NK * e + k:NK * e + k + 1]).then_inc(s["moe_g"], 1)

            def decays(p):
                c, k = divmod(p, NP)
                if k == 0:
                    act.wait_ge(s["mam_dt"], c + 1)
                if p >= 2:
                    act.wait_ge(s["mam_sc"], 2 * (p - 1))
                for r in range(4):
                    n = 2 * k + r // 2
                    nc.scalar.activation(dA[:, 4 * (p % 2) + r, :], half_of(dt, c)[:, r % 2, :], ACT.Exp,
                                         scale=a_neg[:, r % 2, n:n + 1]).then_inc(s["mam_dA"], 1)

            def odd_row(p):
                act.wait_ge(s["mam_bC"], 2 * p + 2)
                if p >= 2:
                    act.wait_ge(s["mam_zo"], p - 1)
                nc.scalar.copy(Csb[:, p % 2, :], pC[:, :]).then_inc(s["mam_Cs"], 1)

            def odd_input_row(p):
                act.wait_ge(s["mam_bB"], 2 * p + 1)
                if p >= 2:
                    act.wait_ge(s["mam_uo"], p - 1)
                nc.scalar.copy(Bsb[:, p % 2, :], pB[:, :]).then_inc(s["mam_Bs"], 1)

            def half(p, o):
                nxt = p + 1 if 0 <= p + 1 < NC * NP else None
                if o == 0 and nxt is not None:
                    odd_input_row(nxt)
                if p + AHEAD < NC * E:
                    hidden(p + AHEAD, (2 * o, 2 * o + 1))
                if o == 0:
                    if 0 <= p < NC * NP - 1 and alone(p):
                        odd_row(p)
                    if nxt is not None:
                        if nxt % NP:
                            decays(nxt)
                    if 0 <= p and not alone(p):
                        odd_row(p)
                elif nxt is not None and nxt % NP == 0:
                    decays(nxt)

            for stage, c, *k in later_stages():
                if stage == "ln_apply":
                    ln([h2T, h3T, h4T][k[0]][:, :], 2 + 2 * k[0], None if k[0] else h2h[:, c % 2, :])
                elif stage == "half":
                    half(c, *k)
                elif stage in ("route", "turn", "x_part", "rows", "dt_part", "z_part", "soft"):
                    {"route": route, "turn": turn, "x_part": x_part, "rows": rows, "dt_part": dt_part,
                     "z_part": z_part, "soft": soft}[stage](c)

        @block.tensor
        def _(pe):
            mm = nc.tensor.matmul
            L = [0]
            L3 = [0]
            held = {}

            def use(bank, free, count):
                if bank in held:
                    pe.wait_ge(s[held[bank][0]], held[bank][1])
                held[bank] = (free, count)

            def ln():
                use("pT", "ln_evac", L[0] + 1)
                pe.wait_ge(s["ln_xn"], NJ * (L[0] + 1))
                for j in range(NJ):
                    ins = nc.tensor.transpose(pT[:, j * P:(j + 1) * P], ln_x[:, j, :], ident[:, :])
                ins.then_inc(s["ln_tr"], 1)
                L[0] += 1

            def gn(g):
                pe.wait_ge(s["gn_m"], g + 1)
                mm(pO[:, 0:2], group_avg[:, :], gn_me[:, :], start=True, stop=True).then_inc(s["gn_mm"], 1)

            pe.wait_ge(s["ld_small"], 16 * NSM)
            pe.wait_ge(s["set_cb"], 2)
            for l in range(2):
                def wm(k):
                    return w_mod[:, l, k * P:(k + 1) * P]
                for i, k in enumerate((0, 1, 3, 4)):
                    mm([pT, pB][l][:, i:i + 1], wm(k), silu_c[:, l:l + 1], start=True, stop=True)
                for i, k in enumerate((2, 5)):
                    ins = mm([pO, pY0][l][:, i * P:(i + 1) * P], silu_cb[:, l, :], wm(k), start=True, stop=True)
                    ins.then_inc(s["mod_mm"], 1)
            for c in range(NC):
                if c == 1:
                    pe.wait_ge(s["set_dve"], 1)
                if c >= 2:
                    pe.wait_ge(s["ln_evac"], c - 1)
                pe.wait_ge(s["ln_xn"], NJ * (c + 1))
                for j in range(NJ):
                    ins = nc.tensor.transpose(pCT[:, c % 2, j * P:(j + 1) * P], ln0_x[:, c * NJ + j, :], ident[:, :])
                ins.then_inc(s["ln_tr"], 1)
            L[0] = NC
            pe.wait_ge(s["set_dve"], 2)
            gn(0)
            pe.wait_ge(s["ld_attn"], 16 * NAT)
            pe.wait_ge(s["set_pool"], 1)
            pe.wait_ge(s["att_pick"], 1)

            def qkv(c):
                pe.wait_ge(s["xn_ready"], c + 1)
                if c:
                    pe.wait_ge(s["att_rbs"], 2 * c)
                for k in range(2):
                    mm(pY[k][:, :], w_qkv[:, k, :], xn[:, c % 2, :], start=True, stop=True).then_inc(s["att_qkv"], 1)

            def v_part(c):
                if c:
                    pe.wait_ge(s["att_vp"], c)
                mm(pB[:, :], w_qkv[:, 2, :], xn[:, c % 2, :], start=True, stop=True).then_inc(s["att_qkv"], 1)

            def norms(c):
                v_part(c)
                pe.wait_ge(s["att_sq"], 2 * c + 2)
                pe.wait_ge(s["att_lo"], 2 * c + 2)
                for k in range(2):
                    for j in range(NJ):
                        ins = mm(pY1[:, k * NJ + j:k * NJ + j + 1], q2[:, k, j * P:(j + 1) * P], ones[:, 0:1],
                                 start=True, stop=True)
                ins.then_inc(s["att_ss"], 1)

            def spread(c):
                pe.wait_ge(s["att_r"], c + 1)
                for k in range(2):
                    for j in range(NJ):
                        r = rnm[:, k * NJ + j:k * NJ + j + 1].to_broadcast([P, P])
                        ins = mm(pY[k][:, j * P:(j + 1) * P], r, ident[:, :], start=True, stop=True)
                    ins.then_inc(s["att_rb"], 1)

            def replicate(bank, c, k, i):
                mm(bank, pick[:, i, :], qk_hi[:, 2 * (c % 2) + k, :], start=True, stop=False)
                return mm(bank, pick[:, i, :], qk_lo[:, 2 * (c % 2) + k, :], start=False, stop=True)

            def out_part(R):
                c, r = divmod(R, NR)
                if r == 0 and c:
                    pe.wait_ge(s["att_x2"], c)
                pe.wait_ge(s["att_zs"], R + 1)
                mm(pO[:, :], w_o[:, :], ZAs[:, R % 2, :], start=(r == 0), stop=(r == NR - 1)).then_inc(s["att_ow"], 1)

            def k_pair(R):
                c, r = divmod(R, NR)
                if r == 0:
                    pe.wait_ge(s["att_lo"], 2 * c + 2)
                if R:
                    pe.wait_ge(s["att_u"], R)
                replicate(pH0, c, 1, 2 * r)
                replicate(pH1, c, 1, 2 * r + 1).then_inc(s["att_kb"], 1)

            for stage in (qkv, norms, spread):
                stage(0)
            k_pair(0)
            for c in range(NC):
                for r in range(NR):
                    R = NR * c + r
                    if R:
                        pe.wait_ge(s["att_qs"], R)
                    replicate(pC, c, 0, 2 * r)
                    replicate(pT, c, 0, 2 * r + 1).then_inc(s["att_qb"], 1)
                    if c + 1 < NC and r < NR - 1:
                        [qkv, norms, spread][r](c + 1)
                    if R + 1 < NR * NC:
                        k_pair(R + 1)
                    if R >= 2:
                        out_part(R - 2)
            pe.wait_ge(s["ld_mam"], 16 * NMA)
            pe.wait_ge(s["att_u"], NR * NC)
            for k in range(2):
                mm(pH[k][:, 0:P], w_freq[:, k, :], dft[:, 0, :], start=True, stop=False)
                mm(pH[k][:, 0:P], w_freq[:, 1 - k, :], dft[:, 1 + k, :], start=False, stop=True).then_inc(s["fr_mm"], 1)
            out_part(NR * NC - 2)
            pe.wait_ge(s["fr_sb"], 2)
            mm(pH0[:, 0:P], g_freq[:, 0, :], dft[:, 0, :], start=True, stop=False)
            mm(pH0[:, 0:P], g_freq[:, 1, :], dft[:, 2, :], start=False, stop=True).then_inc(s["fft_mm"], 1)
            out_part(NR * NC - 1)
            gn(1)
            pe.wait_ge(s["ld_ffn"], 16 * NFF)

            def ffn_tok(c):
                pe.wait_ge(s["ffn_x3"], c + 1)
                if c >= 2:
                    pe.wait_ge(s["ffn_x1"], c - 1)
                for j in range(NJ):
                    ins = mm([pB, pC][c % 2][:, j * P:(j + 1) * P], x3T[:, c % 2, j * P:(j + 1) * P], diag_ga[:, :],
                             start=True, stop=True)
                ins.then_inc(s["ffn_tok"], 1)

            for c in range(NC):
                pe.wait_ge(s["xn_ready"], NC + c + 1)
                for m in range(2):
                    if c:
                        pe.wait_ge(s["ffn_silu"], 2 * c + m - 1)
                    elif m == 0:
                        pe.wait_ge(s["fft_w"], 1)
                    mm(pH[m][:, :], w_f1[:, m, :], xn[:, c % 2, :], start=True, stop=True).then_inc(s["ffn_h"], 1)
                if c:
                    ffn_tok(c - 1)
                for m in range(2):
                    pe.wait_ge(s["ffn_silu"], 2 * c + m + 1)
                    if m == 0 and c >= 2:
                        pe.wait_ge(s["ffn_x3"], c - 1)
                    ins = mm(pY[c % 2][:, :], w_f2[:, m, :], h1[:, 2 * (c % 2) + m, :], start=(m == 0), stop=(m == 1))
                ins.then_inc(s["ffn_o"], 1)
            ln()
            ffn_tok(NC - 1)

            def route(c):
                pe.wait_ge(s["ln_evac"], L[0])
                if c == 0:
                    pe.wait_ge(s["ld_moe"], 16 * NMO)
                h = h2T[:, :]
                use("pT", "moe_w", c + 1)
                for j in range(NJ):
                    ins = mm(pT[:, j * E:(j + 1) * E], h[:, j * P:(j + 1) * P], w_router[:, :], start=True, stop=True)
                ins.then_inc(s["moe_rt"], 1)

            def turn(c):
                use("pT", "moe_wts", c + 1)
                nc.tensor.transpose(pT[:, P:2 * P], wts[:, c % 2, :], ident[:, :]).then_inc(s["moe_wt"], 1)

            def weigh(c):
                use("pT", "moe_xb", c + 1)
                for j in range(NJ):
                    ins = mm(pT[:, j * P:(j + 1) * P], wT[:, :], b_e2[:, j, :], start=True, stop=True)
                ins.then_inc(s["moe_bias"], 1)

            def up(g, k):
                n = NK * g + k
                use(n % 2, "moe_g", n + 1)
                c, part = g // E % 2, slice(k * P, (k + 1) * P)
                if k == 0 and g % E == 0:
                    pe.wait_ge(s["h2_lo"], g // E + 1)
                if k == 0 and g < E and g % (E // NC) == 0:
                    pe.wait_ge(s["set_pool"], 5 + 2 * (g // (E // NC)))
                mm(pH[n % 2][:, :], w_e1h[:, g % E, part], h2h[:, c, :], start=True, stop=False)
                mm(pH[n % 2][:, :], w_e1h[:, g % E, part], h2l[:, c, :], start=False, stop=False)
                mm(pH[n % 2][:, :], w_e1l[:, g % E, part], h2h[:, c, :], start=False, stop=True).then_inc(s["moe_h"], 1)

            def down(g, k):
                n = NK * g + k
                if k == 0 and g:
                    pe.wait_ge(s["moe_acc"], g)
                pe.wait_ge(s["moe_g"], n + 1)
                for j in range(NJ):
                    ins = mm(pO[:, j * P:(j + 1) * P], gel[:, n % NG, j * P:(j + 1) * P], w_e2[:, NK * (g % E) + k, :],
                             start=(k == 0 and j == 0), stop=(k == NK - 1 and j == NJ - 1), skip_group_check=True)
                ins.then_inc(s["moe_g2"], 1)

            def half(p, o):
                g = p + AHEAD
                if o == 0 and 0 <= p + 1 < NC * NP:
                    row_b(p + 1, 1)
                if g < NC * E:
                    up(g, 2 * o)
                    up(g, 2 * o + 1)
                if o == 1 and 0 <= p + 1 < NC * NP:
                    row_b(p + 1, 0)
                    row_c(2 * p + 2)
                if 0 < g <= NC * E:
                    down(g - 1, 2 * o)
                when = 0 if not alone(p) or not alone(p - 1) else 1
                if (o, when) == (0, 1):
                    total(p - 1, slice(0, 1))
                if (o, when) == (0, 0) and p > 0:
                    total(p - 1)
                if o == 0 and p >= 0:
                    row_c(2 * p + 1)
                if 0 < g <= NC * E:
                    down(g - 1, 2 * o + 1)
                if (o, when) == (0, 1):
                    total(p - 1, slice(1, 2))

            def x_part(c):
                pe.wait_ge(s["ln_evac"], L3[0])
                for d in range(ND):
                    use(d, "mam_xr", 2 * c + d + 1)
                    mm(pH[d][:, :], w_in[:, d, :], h3T[:, :], start=True, stop=True).then_inc(s["mam_xz"], 1)

            def rows(c):
                use("pT", "mam_bcs", c + 1)
                mm(pT[0:96, :], w_bc[:, :], h3T[:, :], start=True, stop=True).then_inc(s["mam_bc"], 1)

            def dt_part(c):
                for d in range(ND):
                    use(d, "mam_v", 2 * c + d + 1)
                    mm(pH[d][:, :], w_dt[:, d, :], h3T[:, :], start=True, stop=True).then_inc(s["mam_dtp"], 1)

            def z_part(c):
                for d in range(ND):
                    use(d, "mam_gz", 2 * c + d + 1)
                    mm(pH[d][:, :], w_in[:, ND + d, :], h3T[:, :], start=True, stop=True).then_inc(s["mam_xz"], 1)

            def row_b(p, o):
                c, k = divmod(p, NP)
                if o:
                    if k == 0:
                        pe.wait_ge(s["mam_st"], c + 1)
                    if p:
                        pe.wait_ge(s["mam_ub"], p)
                else:
                    pe.wait_ge(s["mam_Bs"], p + 1)
                mm(pB[:, :], sel[:, 2 * k + o:2 * k + o + 1].to_broadcast([96, P]), ST[:, c % 2, :], start=True, stop=True).then_inc(s["mam_bB"], 1)

            def row_c(m):
                c, n = divmod(m, NS)
                if n % 2:
                    pe.wait_ge(s["mam_z"], (m + 1) // 2)
                elif m:
                    pe.wait_ge(s["mam_Cs"], m // 2)
                mm(pC[:, :], sel[:, NS + n:NS + n + 1].to_broadcast([96, P]), ST[:, c % 2, :], start=True, stop=True).then_inc(s["mam_bC"], 1)

            def total(p, part=slice(0, 2)):
                c, k = divmod(p, NP)
                if k == 0 and c:
                    pe.wait_ge(s["mam_y2"], 2 * c)
                if alone(p):
                    for name, Z in (("mam_z", Zev), ("mam_zo", ZS))[part]:
                        pe.wait_ge(s[name], p + 1)
                        for d in range(ND):
                            ins = mm(pY[d][:, :], ident[:, :], Z[:, 2 * (p % 2) + d, :], start=(k == 0 and Z is Zev),
                                     stop=(k == NP - 1 and Z is ZS))
                    if Z is ZS:
                        ins.then_inc(s["mam_y"], 1)
                    return
                pe.wait_ge(s["mam_zs"], p + 1)
                for d in range(ND):
                    ins = mm(pY[d][:, :], ident[:, :], ZS[:, 2 * (p % 2) + d, :], start=(k == 0), stop=(k == NP - 1))
                ins.then_inc(s["mam_y"], 1)

            def project(c):
                pe.wait_ge(s["mam_y2"], 2 * c + 2)
                if c == 0:
                    pe.wait_ge(s["set_pool"], 4 + 2 * NC)
                use("pT", "mam_x", c + 1)
                for j in range(NJ):
                    for d in range(ND):
                        ins = mm(pT[:, j * P:(j + 1) * P], y2[:, d, j * P:(j + 1) * P], w_out[:, d, :],
                                 start=(d == 0), stop=(d == 1))
                ins.then_inc(s["mam_o"], 1)

            def fft(c):
                use("pT", "fft_x", c + 1)
                for j in range(NJ):
                    ins = mm(pT[:, j * P:(j + 1) * P], h4T[:, j * P:(j + 1) * P], w_fft[:, :], start=True, stop=True)
                ins.then_inc(s["fft_o"], 1)

            for stage, c, *k in later_stages():
                if stage == "ln_apply":
                    ln()
                    if k[0] == 1:
                        L3[0] = L[0]
                elif stage == "half":
                    half(c, *k)
                elif stage in ("route", "turn", "weigh", "x_part", "rows", "dt_part", "z_part", "total", "project", "fft"):
                    {"route": route, "turn": turn, "weigh": weigh, "x_part": x_part, "rows": rows, "dt_part": dt_part,
                     "z_part": z_part, "total": total, "project": project, "fft": fft}[stage](c)


def constants():
    n = np.arange(D)
    turn = 2 * np.pi * (np.outer(n, n) % D) / D
    dft = np.stack([np.cos(turn), np.sin(turn), -np.sin(turn)], 1).astype(np.float32)
    group = (n[:, None] // DH == n[None, :] // DH).astype(np.float32) / DH
    later = np.concatenate([np.arange(E)[None, :] > np.arange(E)[:, None], 2 - np.arange(E)[:, None]], 1)
    later = np.ascontiguousarray(np.broadcast_to(later.astype(np.float32), (P, E, E + 1)))
    m = np.arange(96) % 32
    part_row = (m[:, None] == np.arange(2 * NS)[None, :]).astype(np.float32)
    gam = np.float32(1.0) - np.exp(np.linspace(np.log(1 / 32), np.log(1 / 512), HEADS).astype(np.float32))
    return {"dft": dft, "group_avg": group, "later": later, "part_row": part_row,
            "ident": np.eye(P, dtype=np.float32), "gamma": np.repeat(gam.astype(np.float32), DH)}


def kernel(**inputs):
    import concourse.bacc as bacc
    from concourse.bass_utils import run_bass_kernel_spmd

    v = {k: np.asarray(x) for k, x in inputs.items()}
    k = constants()

    def tiles(w, n):
        return w.reshape(w.shape[0], n, -1)

    def rows(w, n):
        return w.reshape(n, P, -1).transpose(1, 0, 2)

    qT, kT, vT = (v[f"L0_attn_{n}w"].T for n in "qkv")
    cols = {
        "norm_g": v["L0_attn_norm_g"], "norm_b": v["L0_attn_norm_b"], "ob": v["L0_attn_ob"],
        "ffn_g": v["L0_attn_ffn_norm_g"], "ffn_b": v["L0_attn_ffn_norm_b"],
        "b1_0": v["L0_attn_b1"][:P], "b1_1": v["L0_attn_b1"][P:], "b2": v["L0_attn_b2"],
        "conv_b0": v["L1_attn_conv_b"][:P], "conv_b1": v["L1_attn_conv_b"][P:],
        "b_dt0": v["L1_attn_b_dt"][:P], "b_dt1": v["L1_attn_b_dt"][P:],
        "c0": v["L0_c"][0], "c1": v["L1_c"][0], "gamma": k["gamma"],
    }
    for d in range(ND):
        for t in range(TAPS):
            cols[f"conv_w{d}{t}"] = v["L1_attn_conv_w"][d * P:(d + 1) * P, 0, t]
    w_dt = np.zeros((P, DI), np.float32)
    w_dt[:RANK] = v["L1_attn_W_dt"].T
    b_e2 = np.zeros((P, NJ, P), np.float32)
    for j in range(NJ):
        b_e2[j * E:(j + 1) * E, j] = v["L0_ffn_b2"]
    bc = np.concatenate([v["L1_attn_W_B"], v["L1_attn_W_C"]], 0).T
    arrays = {
        "x": v["L0_attn_x"][0], "cols": np.stack([cols[n] for n in COLS], 1), "ident": k["ident"],
        "group_avg": k["group_avg"], "dft": k["dft"], "later": k["later"], "part_row": k["part_row"],
        "w_qkv": np.stack([qT, kT, vT], 1), "w_o": v["L0_attn_ow"].T,
        "w_f1": tiles(v["L0_attn_w1"].T, 2), "w_f2": rows(v["L0_attn_w2"].T, 2),
        "w_router": v["L0_ffn_w_router"], "w_e1": v["L0_ffn_w1"].transpose(1, 0, 2),
        "w_e2": v["L0_ffn_w2"].reshape(E * NK, P, D).transpose(1, 0, 2),
        "b_e1": v["L0_ffn_b1"].reshape(E * NK, P).T, "b_e2": b_e2,
        "w_mod0": v["L0_wmod"], "w_mod1": v["L1_wmod"],
        "w_in": tiles(v["L1_attn_W_in"].T, 4), "w_dt": tiles(w_dt, ND),
        "w_bc": np.concatenate([bc, bc, bc], 1), "w_out": rows(v["L1_attn_W_out"].T, ND),
        "a_log": rows(v["L1_attn_A_log"], ND),
        "w_freq": np.stack([v["L1_ffn_w_freq_real"], v["L1_ffn_w_freq_imag"]], 1),
        "fft_bias": v["L1_ffn_bias"][None],
    }
    arrays = {n: np.ascontiguousarray(x) for n, x in arrays.items()}
    nc = bacc.Bacc("TRN2", target_bir_lowering=False, num_devices=1)
    aps = {n: nc.dram_tensor(f"in_{n}", x.shape, mybir.dt.from_np(x.dtype), kind="ExternalInput").ap()
           for n, x in arrays.items()}
    out = nc.dram_tensor("out_0", (T, D), F32, kind="ExternalOutput").ap()
    build(nc, aps, out)
    r = run_bass_kernel_spmd(nc, [{f"in_{n}": x for n, x in arrays.items()}], core_ids=[0])
    return r.results[0]["out_0"].reshape(1, T, D)
```
